# Optimizing a Trainium2 kernel written in Bass

```python
import numpy as np
import jax
import jax.numpy as jnp

def _softmax(x, axis=-1):
    return jax.nn.softmax(x, axis=axis)

def _gelu(x):
    return jax.nn.gelu(x, approximate=True)

def _silu(x):
    return jax.nn.silu(x)

def _sigmoid(x):
    return jax.nn.sigmoid(x)

def _layernorm(x, axis=-1, eps=1e-05):
    m = jnp.mean(x, axis=axis, keepdims=True)
    v = jnp.var(x, axis=axis, keepdims=True)
    return (x - m) / jnp.sqrt(v + eps)

def _scatter_add(tgt, idx, src, axis=0):
    return tgt.at[idx].add(src)

def _segment_sum(src, seg, n):
    return jax.ops.segment_sum(src, seg, n)
kernel_name = 'mk_sandwich_d2_jaxref_r4_b63053'

def setup_inputs(seed: int=0):
    np.random.seed(seed)
    _w = jnp.asarray

    def _L0_attn_setup():
        import jax, jax.numpy as jnp
        import numpy as np
        N_FILTERS = 256
        N_HEADS = 16
        key = jax.random.key(seed)
        k1, k2, k3 = jax.random.split(key, 3)
        x = jax.random.normal(k1, (8, 256, N_FILTERS), dtype=jnp.float32)
        w_qkv = jax.random.normal(k2, (N_FILTERS, N_FILTERS * 3), dtype=jnp.float32) * (0.02 / N_FILTERS) ** 0.5
        w_out = jax.random.normal(k3, (N_FILTERS, N_FILTERS), dtype=jnp.float32) * (0.02 / N_FILTERS) ** 0.5
        return {'x': x, 'w_qkv': w_qkv, 'w_out': w_out}
    _L0_attn_in = _L0_attn_setup()

    def _L0_ffn_setup():
        import jax, jax.numpy as jnp
        import numpy as np
        LOOPS = 2
        NUM_GROUPS = 4
        EXPERTS_PER_GROUP = 2
        NUM_EXPERTS = NUM_GROUPS * EXPERTS_PER_GROUP
        GROUPS_TOP_K = 2
        TOP_K = 1
        RMS_EPS = 1e-06
        EPS = 1e-09

        def _rmsnorm(x, w):
            return x * jax.lax.rsqrt(jnp.mean(x * x, axis=-1, keepdims=True) + RMS_EPS) * w

        def _combine_weights(x_flat, w_macro, w_micro):
            T = x_flat.shape[0]
            macro = jax.nn.softmax(x_flat @ w_macro.T, axis=-1)
            mvals, midx = jax.lax.top_k(macro, GROUPS_TOP_K)
            mvals = mvals / (jnp.sum(mvals, axis=-1, keepdims=True) + EPS)
            micro = jax.nn.softmax(jnp.einsum('td,ged->tge', x_flat, w_micro), axis=-1)
            uvals, uidx = jax.lax.top_k(micro, TOP_K)
            uvals = uvals / (jnp.sum(uvals, axis=-1, keepdims=True) + EPS)
            tok = jnp.arange(T)
            combine = jnp.zeros((T, NUM_EXPERTS), x_flat.dtype)
            for s in range(GROUPS_TOP_K):
                g = midx[:, s]
                wg = mvals[:, s:s + 1]
                li = uidx[tok, g]
                lv = uvals[tok, g]
                eidx = g[:, None] * EXPERTS_PER_GROUP + li
                combine = combine.at[tok[:, None], eidx].add(lv * wg)
            return combine
        key = jax.random.key(seed)
        ks = jax.random.split(key, 6)
        B, S, D, F = (2, 256, 256, 512)
        return {'z': jax.random.normal(ks[0], (B, S, D), jnp.float32), 'norm_w': jnp.ones((D,), jnp.float32), 'w_macro': jax.random.normal(ks[1], (NUM_GROUPS, D), jnp.float32) * D ** (-0.5), 'w_micro': jax.random.normal(ks[2], (NUM_GROUPS, EXPERTS_PER_GROUP, D), jnp.float32) * D ** (-0.5), 'w1': jax.random.normal(ks[3], (NUM_EXPERTS, F, D), jnp.float32) * D ** (-0.5), 'w2': jax.random.normal(ks[4], (NUM_EXPERTS, D, F), jnp.float32) * F ** (-0.5)}
    _L0_ffn_in = _L0_ffn_setup()

    def _L1_attn_setup():
        import jax, jax.numpy as jnp
        import numpy as np
        import math
        D_MODEL = 256
        N_HEADS = 16
        HEAD_DIM = D_MODEL // N_HEADS

        def get_slopes(n_heads: int) -> jnp.ndarray:

            def pow2_slopes(n):
                start = 2.0 ** (-8.0 / n)
                return np.array([start * start ** i for i in range(n)], dtype=np.float32)
            if math.log2(n_heads).is_integer():
                return jnp.asarray(pow2_slopes(n_heads))
            closest = 2 ** math.floor(math.log2(n_heads))
            base = pow2_slopes(closest)
            extra = pow2_slopes(2 * closest)[::2][:n_heads - closest]
            return jnp.asarray(np.concatenate([base, extra]))
        key = jax.random.key(seed)
        ks = jax.random.split(key, 9)
        s = 1.0 / math.sqrt(D_MODEL)
        x = jax.random.normal(ks[0], (2, 512, D_MODEL), dtype=jnp.float32)
        q_w = jax.random.uniform(ks[1], (D_MODEL, D_MODEL), jnp.float32, -s, s)
        q_b = jax.random.uniform(ks[2], (D_MODEL,), jnp.float32, -s, s)
        k_w = jax.random.uniform(ks[3], (D_MODEL, D_MODEL), jnp.float32, -s, s)
        k_b = jax.random.uniform(ks[4], (D_MODEL,), jnp.float32, -s, s)
        v_w = jax.random.uniform(ks[5], (D_MODEL, D_MODEL), jnp.float32, -s, s)
        v_b = jax.random.uniform(ks[6], (D_MODEL,), jnp.float32, -s, s)
        o_w = jax.random.uniform(ks[7], (D_MODEL, D_MODEL), jnp.float32, -s, s)
        o_b = jax.random.uniform(ks[8], (D_MODEL,), jnp.float32, -s, s)
        return {'x': x, 'q_w': q_w, 'q_b': q_b, 'k_w': k_w, 'k_b': k_b, 'v_w': v_w, 'v_b': v_b, 'o_w': o_w, 'o_b': o_b}
    _L1_attn_in = _L1_attn_setup()

    def _L1_ffn_setup():
        import jax, jax.numpy as jnp
        import numpy as np
        LN_EPS = 1e-05

        def layer_norm(x, g, b):
            mu = jnp.mean(x, axis=-1, keepdims=True)
            var = jnp.var(x, axis=-1, keepdims=True)
            return (x - mu) / jnp.sqrt(var + LN_EPS) * g + b

        def balanced_assignment(scores):
            T, E = scores.shape
            C = T // E
            taken = jnp.zeros((T,), dtype=bool)
            parts = []
            for e in range(E):
                s = jnp.where(taken, -jnp.inf, scores[:, e])
                _, idx = jax.lax.top_k(s, C)
                parts.append(idx)
                taken = taken.at[idx].set(True)
            return jnp.concatenate(parts)
        key = jax.random.key(seed)
        ks = jax.random.split(key, 4)
        B, S, D, F, E = (4, 512, 256, 1024, 8)
        return {'x': jax.random.normal(ks[0], (B, S, D), dtype=jnp.float32), 'centroids': jax.random.normal(ks[1], (E, D), dtype=jnp.float32) * 0.1, 'ln_g': jnp.ones((D,), dtype=jnp.float32), 'ln_b': jnp.zeros((D,), dtype=jnp.float32), 'w1': jax.random.normal(ks[2], (E, D, F), dtype=jnp.float32) * 0.02, 'b1': jnp.zeros((E, F), dtype=jnp.float32), 'w2': jax.random.normal(ks[3], (E, F, D), dtype=jnp.float32) * 0.02, 'b2': jnp.zeros((E, D), dtype=jnp.float32)}
    _L1_ffn_in = _L1_ffn_setup()
    _d = {'L0_attn_x': _L0_attn_in['x'], 'L0_attn_w_qkv': _L0_attn_in['w_qkv'], 'L0_attn_w_out': _L0_attn_in['w_out'], 'L0_ffn_norm_w': _L0_ffn_in['norm_w'], 'L0_ffn_w_macro': _L0_ffn_in['w_macro'], 'L0_ffn_w_micro': _L0_ffn_in['w_micro'], 'L0_ffn_w1': _L0_ffn_in['w1'], 'L0_ffn_w2': _L0_ffn_in['w2'], 'L1_attn_q_w': _L1_attn_in['q_w'], 'L1_attn_q_b': _L1_attn_in['q_b'], 'L1_attn_k_w': _L1_attn_in['k_w'], 'L1_attn_k_b': _L1_attn_in['k_b'], 'L1_attn_v_w': _L1_attn_in['v_w'], 'L1_attn_v_b': _L1_attn_in['v_b'], 'L1_attn_o_w': _L1_attn_in['o_w'], 'L1_attn_o_b': _L1_attn_in['o_b'], 'L1_ffn_centroids': _L1_ffn_in['centroids'], 'L1_ffn_ln_g': _L1_ffn_in['ln_g'], 'L1_ffn_ln_b': _L1_ffn_in['ln_b'], 'L1_ffn_w1': _L1_ffn_in['w1'], 'L1_ffn_b1': _L1_ffn_in['b1'], 'L1_ffn_w2': _L1_ffn_in['w2'], 'L1_ffn_b2': _L1_ffn_in['b2']}
    _x0 = _d['L0_attn_x']
    _d['L0_attn_x'] = jax.random.normal(jax.random.fold_in(jax.random.key(seed), 1), (4, 1024, 256), dtype=_x0.dtype)
    del _x0
    return _d

def reference(L0_attn_x, L0_attn_w_qkv, L0_attn_w_out, L0_ffn_norm_w, L0_ffn_w_macro, L0_ffn_w_micro, L0_ffn_w1, L0_ffn_w2, L1_attn_q_w, L1_attn_q_b, L1_attn_k_w, L1_attn_k_b, L1_attn_v_w, L1_attn_v_b, L1_attn_o_w, L1_attn_o_b, L1_ffn_centroids, L1_ffn_ln_g, L1_ffn_ln_b, L1_ffn_w1, L1_ffn_b1, L1_ffn_w2, L1_ffn_b2):

    def _L0_attn_ref(x, w_qkv, w_out):
        import jax, jax.numpy as jnp
        import numpy as np
        N_FILTERS = 256
        N_HEADS = 16
        b, n, c = x.shape
        h = N_HEADS
        d = c // h
        qkv = jnp.einsum('bnc,ce->bne', x, w_qkv)
        q, k, v = jnp.split(qkv, 3, axis=-1)
        to_heads = lambda t: t.reshape(b, n, h, d).transpose(0, 2, 1, 3)
        q, k, v = (to_heads(q), to_heads(k), to_heads(v))
        scale = jnp.sqrt(jnp.asarray(c, jnp.float32))
        attn = jnp.einsum('bhnd,bhmd->bhnm', q, k) / scale
        attn = jax.nn.softmax(attn, axis=-1)
        out = jnp.einsum('bhnm,bhmd->bhnd', attn, v)
        out = out.transpose(0, 2, 1, 3).reshape(b, n, c)
        return jnp.einsum('bnc,co->bno', out, w_out)

    def _L0_ffn_ref(z, norm_w, w_macro, w_micro, w1, w2):
        import jax, jax.numpy as jnp
        import numpy as np
        LOOPS = 2
        NUM_GROUPS = 4
        EXPERTS_PER_GROUP = 2
        NUM_EXPERTS = NUM_GROUPS * EXPERTS_PER_GROUP
        GROUPS_TOP_K = 2
        TOP_K = 1
        RMS_EPS = 1e-06
        EPS = 1e-09

        def _rmsnorm(x, w):
            return x * jax.lax.rsqrt(jnp.mean(x * x, axis=-1, keepdims=True) + RMS_EPS) * w

        def _combine_weights(x_flat, w_macro, w_micro):
            T = x_flat.shape[0]
            macro = jax.nn.softmax(x_flat @ w_macro.T, axis=-1)
            mvals, midx = jax.lax.top_k(macro, GROUPS_TOP_K)
            mvals = mvals / (jnp.sum(mvals, axis=-1, keepdims=True) + EPS)
            micro = jax.nn.softmax(jnp.einsum('td,ged->tge', x_flat, w_micro), axis=-1)
            uvals, uidx = jax.lax.top_k(micro, TOP_K)
            uvals = uvals / (jnp.sum(uvals, axis=-1, keepdims=True) + EPS)
            tok = jnp.arange(T)
            combine = jnp.zeros((T, NUM_EXPERTS), x_flat.dtype)
            for s in range(GROUPS_TOP_K):
                g = midx[:, s]
                wg = mvals[:, s:s + 1]
                li = uidx[tok, g]
                lv = uvals[tok, g]
                eidx = g[:, None] * EXPERTS_PER_GROUP + li
                combine = combine.at[tok[:, None], eidx].add(lv * wg)
            return combine
        B, S, D = z.shape
        T = B * S
        for _ in range(LOOPS):
            zn = _rmsnorm(z, norm_w)
            x = zn.reshape(T, D)
            combine = _combine_weights(x, w_macro, w_micro)
            h = jax.nn.silu(jnp.einsum('td,efd->tef', x, w1))
            y = jnp.einsum('tef,edf->ted', h, w2)
            mixed = jnp.einsum('ted,te->td', y, combine)
            z = z + mixed.reshape(B, S, D)
        return z

    def _L1_attn_ref(x, q_w, q_b, k_w, k_b, v_w, v_b, o_w, o_b):
        import jax, jax.numpy as jnp
        import numpy as np
        import math
        D_MODEL = 256
        N_HEADS = 16
        HEAD_DIM = D_MODEL // N_HEADS

        def get_slopes(n_heads: int) -> jnp.ndarray:

            def pow2_slopes(n):
                start = 2.0 ** (-8.0 / n)
                return np.array([start * start ** i for i in range(n)], dtype=np.float32)
            if math.log2(n_heads).is_integer():
                return jnp.asarray(pow2_slopes(n_heads))
            closest = 2 ** math.floor(math.log2(n_heads))
            base = pow2_slopes(closest)
            extra = pow2_slopes(2 * closest)[::2][:n_heads - closest]
            return jnp.asarray(np.concatenate([base, extra]))
        B, S, D = x.shape
        H, hd = (N_HEADS, HEAD_DIM)
        Q = (x @ q_w.T + q_b).reshape(B, S, H, hd).transpose(0, 2, 1, 3)
        K = (x @ k_w.T + k_b).reshape(B, S, H, hd).transpose(0, 2, 1, 3)
        V = (x @ v_w.T + v_b).reshape(B, S, H, hd).transpose(0, 2, 1, 3)
        scores = jnp.einsum('bhqd,bhkd->bhqk', Q, K) / math.sqrt(hd)
        pos = jnp.arange(S)
        rel = (pos[None, :] - pos[:, None]).astype(scores.dtype)
        slopes = get_slopes(H)
        scores = scores + slopes[None, :, None, None] * rel[None, None, :, :]
        causal = pos[None, :] <= pos[:, None]
        scores = jnp.where(causal[None, None], scores, -jnp.inf)
        attn = jax.nn.softmax(scores, axis=-1)
        out = jnp.einsum('bhqk,bhkd->bhqd', attn, V)
        out = out.transpose(0, 2, 1, 3).reshape(B, S, D)
        return out @ o_w.T + o_b

    def _L1_ffn_ref(x, centroids, ln_g, ln_b, w1, b1, w2, b2):
        import jax, jax.numpy as jnp
        import numpy as np
        LN_EPS = 1e-05

        def layer_norm(x, g, b):
            mu = jnp.mean(x, axis=-1, keepdims=True)
            var = jnp.var(x, axis=-1, keepdims=True)
            return (x - mu) / jnp.sqrt(var + LN_EPS) * g + b

        def balanced_assignment(scores):
            T, E = scores.shape
            C = T // E
            taken = jnp.zeros((T,), dtype=bool)
            parts = []
            for e in range(E):
                s = jnp.where(taken, -jnp.inf, scores[:, e])
                _, idx = jax.lax.top_k(s, C)
                parts.append(idx)
                taken = taken.at[idx].set(True)
            return jnp.concatenate(parts)
        D = x.shape[-1]
        feat = x.reshape(-1, D)
        T = feat.shape[0]
        E = centroids.shape[0]
        C = T // E
        norm = layer_norm(feat, ln_g, ln_b)
        scores = jax.lax.stop_gradient(norm @ centroids.T)
        sort_by_expert = balanced_assignment(scores)
        routed = feat[sort_by_expert].reshape(E, C, D)
        h = layer_norm(routed, ln_g, ln_b)
        h = jax.nn.gelu(jnp.einsum('ecd,edf->ecf', h, w1) + b1[:, None, :])
        h = jnp.einsum('ecf,efd->ecd', h, w2) + b2[:, None, :]
        out = routed + h
        inv = jnp.zeros((T,), dtype=jnp.int32).at[sort_by_expert].set(jnp.arange(T, dtype=jnp.int32))
        return out.reshape(T, D)[inv].reshape(x.shape)
    x = L0_attn_x
    x = x + _layernorm(_L0_attn_ref(_layernorm(x, axis=-1), L0_attn_w_qkv, L0_attn_w_out), axis=-1)
    x = x + _layernorm(_L0_ffn_ref(_layernorm(x, axis=-1), L0_ffn_norm_w, L0_ffn_w_macro, L0_ffn_w_micro, L0_ffn_w1, L0_ffn_w2), axis=-1)
    x = x + _layernorm(_L1_attn_ref(_layernorm(x, axis=-1), L1_attn_q_w, L1_attn_q_b, L1_attn_k_w, L1_attn_k_b, L1_attn_v_w, L1_attn_v_b, L1_attn_o_w, L1_attn_o_b), axis=-1)
    x = x + _layernorm(_L1_ffn_ref(_layernorm(x, axis=-1), L1_ffn_centroids, L1_ffn_ln_g, L1_ffn_ln_b, L1_ffn_w1, L1_ffn_b1, L1_ffn_w2, L1_ffn_b2), axis=-1)
    return x

_drawn_inputs = setup_inputs


def setup_inputs(seed=0):
    import zlib

    import numpy as np

    out = dict(_drawn_inputs(seed))
    spreads = {'L0_ffn_norm_w': (1.0, 0.2),
     'L1_ffn_ln_g': (1.0, 0.536),
     'L1_ffn_ln_b': (0.0, 0.8),
     'L1_ffn_b1': (0.0, 0.699),
     'L1_ffn_b2': (0.0, 0.1)}
    factors = {'L1_attn_q_b': 7.028, 'L1_attn_k_b': 8.0}
    for name, (base, spread) in spreads.items():
        noise = np.random.default_rng([zlib.crc32(name.encode()), seed]).standard_normal(out[name].shape)
        drawn = base * np.exp(spread * noise) if base else spread * noise
        out[name] = jnp.asarray(drawn.astype(out[name].dtype))
    for name, factor in factors.items():
        out[name] = (out[name] * factor).astype(out[name].dtype)
    return out
```

```python
from contextlib import ExitStack
import numpy as np
import concourse.bass as bass
from concourse import mybir
F32=mybir.dt.float32; F32R=mybir.dt.float32r; BF=mybir.dt.bfloat16; I32=mybir.dt.int32; U32=mybir.dt.uint32
ALU=mybir.AluOpType; ACT=mybir.ActivationFunctionType; AX=mybir.AxisListType
BATCH,SEQ,DIM,HEADS,HD=4,1024,256,16,16
TILES=SEQ//128
GROUPS=4
AUG=5
WIDE=64

class Mem:
    def __init__(self,nc,tag):
        self.nc,self.tag,self.ctx,self.sems=nc,tag,ExitStack(),[]
    def __enter__(self): return self
    def __exit__(self,*a):
        self.ctx.close()
        if self.sems:
            self.nc.clear_and_free_semaphores(self.sems)
            self.nc.all_engine_barrier()
    def sb(self,n,s,d=F32): return self.ctx.enter_context(self.nc.sbuf_tensor(f"{self.tag}_{n}",s,d))
    def ps(self,n,s,d=F32): return self.ctx.enter_context(self.nc.psum_tensor(f"{self.tag}_{n}",s,d))
    def sem(self,n):
        s=self.nc.alloc_semaphore(name=f"{self.tag}_{n}")
        self.sems.append(s)
        return s

def attention(nc, tag, qkv, ao, causal, exp_scale, ident_d, aug_d=None, masks_d=None):
    with Mem(nc,tag) as m:
        sb,ps,sem=m.sb,m.ps,m.sem
        ident=sb("ident",[128,128])
        raw=sb("raw",[128,3,TILES,64])
        qn=sb("qn",[128,TILES,2,WIDE]); kn=sb("kn",[128,TILES,2,WIDE])
        hiR=sb("hiR",[128,2,TILES,2,HD],F32R)
        vn=sb("vn",[128,2,TILES,2,32])
        qT=sb("qT",[128,2,SEQ],F32R)
        kT=sb("kT",[128,2,2,SEQ],F32R)
        pr=sb("pr",[128,4,2,512])
        ot=sb("ot",[128,512])
        mparts=sb("mparts",[128,2,TILES,2]); m16=sb("m16",[128,2*TILES]); mT=sb("mT",[2*TILES,128],F32R)
        osum=sb("osum",[128,4,2,HD+1]); rcp=sb("rcp",[128,4,2,1]); aon=sb("aon",[128,TILES,4,HD])
        if causal:
            augt=sb("augt",[128,2,2*GROUPS,TILES*2*AUG])
            maskf=sb("maskf",[128,128+128+256])
            maskr=sb("maskr",[128,128+128+256],F32R)
        S1=ps("S1",[128,2,512]); S2=ps("S2",[128,2,2,512]); OP=ps("OP",[128,512]); TP=ps("TP",[128,512])
        consts=sem("consts"); raw_loaded=sem("raw_loaded"); raw_free=sem("raw_free")
        nat_ready=sem("nat_ready"); nat_free=sem("nat_free"); v_ready=[sem("v_ready0"),sem("v_ready1")]; v_free=[sem("v_free0"),sem("v_free1")]
        pool_done=sem("pool_done"); dve_done=sem("dve_done"); zeros_done=sem("zeros_done")
        t_dve=sem("t_dve"); t_act=sem("t_act"); t_free=sem("t_free")
        s1_full=sem("s1_full"); s1_free=sem("s1_free"); m_ready=sem("m_ready"); mT_ready=sem("mT_ready"); m_placed=sem("m_placed")
        s2_full=sem("s2_full"); s2_free=sem("s2_free")
        o_full=sem("o_full"); ot_ready=sem("ot_ready"); ao_ready=sem("ao_ready"); ao_stored=sem("ao_stored")

        steps=[(c,kt) for c in range(2) for kt in range(4*(c+1) if causal else TILES)]
        def first_col(c,kt):
            return 0 if (not causal or kt<2) else max(0,kt*128-c*512)
        maxes=[(qt,h,half) for qt in range(TILES) for h in range(2) for half in range(2) if not causal or half*4<=qt]
        NS=len(steps)
        step_of={}
        share=[[] for _ in range(NS)]
        for x,mx in enumerate(maxes): share[x*NS//len(maxes)].append(mx)
        groups=[[(2*g),(2*g+1)] for g in range(NS//2)]
        last_group_c0=(4 if causal else 8)//2-1
        FIN=2*last_group_c0+4
        blk=(TILES//2)

        with nc.Block() as block:
            @block.sync
            def _(sp):
                sp.dma_start(ident[:],ident_d).then_inc(consts,16)
                if causal:
                    sp.dma_start(augt[:],aug_d).then_inc(consts,16)
                    sp.dma_start(maskf[:],masks_d).then_inc(consts,16)
                def load(bg):
                    sp.wait_ge(raw_free,1).then_inc(raw_free,-1)
                    for m in range(3):
                        sp.dma_start(raw[:,m],qkv[bg][0,m].rearrange("(t p) c -> p t c",p=128)).then_inc(raw_loaded,16)
                def place():
                    sp.wait_ge(mT_ready,1).then_inc(mT_ready,-1)
                    for h in range(2):
                        sp.dma_start(qT[64*h:64*h+1,place.s,:].bitcast(F32).rearrange("o (t q) -> o t q",t=TILES),
                                     mT[TILES*h:TILES*h+TILES,:].bitcast(F32)).then_inc(m_placed,16)
                load(bass.ds(0,1))
                place.s=0; place()
                def store(bg):
                    sp.wait_ge(ao_ready,1).then_inc(ao_ready,-1)
                    sp.dma_start(ao[bass.ds(bg,1)][0].rearrange("(t p) c -> p t c",p=128),aon[:].rearrange("p t h d -> p t (h d)")).then_inc(ao_stored,16)
                def loop_body(bg,first,last):
                    if not last: load(bass.ds(bg+1,1))
                    if not first: store(bg-1)
                    place.s=1; place()
                    if not last:
                        place.s=0; place()
                loop_body(0,True,False)
                with sp.Fori(1,BATCH*GROUPS-1) as bg:
                    loop_body(bg,False,False)
                loop_body(BATCH*GROUPS-1,False,True)
                store(BATCH*GROUPS-1)
                sp.wait_ge(ao_stored,16)

            @block.gpsimd
            def _(pool):
                nc.gpsimd.memset(qn[:],0.0).then_inc(pool_done,1)
                nc.gpsimd.memset(kn[:],0.0).then_inc(pool_done,1)
                nc.gpsimd.memset(vn[:],0.0).then_inc(pool_done,1)
                pool.wait_ge(pool_done,3).then_inc(pool_done,-3)
                nc.gpsimd.memset(kn[:,:,:,0:1],-1.0).then_inc(pool_done,1)
                nc.gpsimd.memset(vn[:,:,:,:,HD:HD+1],1.0).then_inc(pool_done,1)
                pool.wait_ge(pool_done,2).then_inc(pool_done,-2)
                pool.sem_inc(raw_free,1)
                if causal: pool.wait_ge(consts,48)
                def natural(pair,first=False):
                    s=pair[1]
                    pool.wait_ge(nat_free,1).then_inc(nat_free,-1)
                    for m in range(2):
                        r=raw[:,m,:,32*s:32*s+32].rearrange("p t (h d) -> p t h d",h=2)
                        nc.gpsimd.tensor_copy(hiR[:,m],r).then_inc(pool_done,1)
                    if causal:
                        for m,n in ((0,qn),(1,kn)):
                            src=augt[:,m,pair[0],:]
                            nc.gpsimd.tensor_copy(n[:,:,:,0:AUG],src.rearrange("p (t h a) -> p t h a",t=TILES,h=2)).then_inc(pool_done,1)
                    pool.wait_ge(pool_done,4 if causal else 2).then_inc(pool_done,-(4 if causal else 2))
                    A,B,C=AUG,AUG+HD,AUG+2*HD
                    for m,n,his,lo in ((0,qn,(A,B),C),(1,kn,(A,C),B)):
                        r=raw[:,m,:,32*s:32*s+32].rearrange("p t (h d) -> p t h d",h=2)
                        hi=hiR[:,m].bitcast(F32)
                        for at in his:
                            nc.gpsimd.tensor_copy(n[:,:,:,at:at+HD],hi).then_inc(pool_done,1)
                        nc.gpsimd.tensor_tensor(n[:,:,:,lo:lo+HD],r,hi,ALU.subtract).then_inc(pool_done,1)
                    pool.wait_ge(pool_done,6).then_inc(pool_done,-6)
                    pool.sem_inc(nat_ready,1)
                def values(s):
                    pool.wait_ge(v_free[s],1).then_inc(v_free[s],-1)
                    nc.gpsimd.tensor_copy(vn[:,s,:,:,0:HD],raw[:,2,:,32*s:32*s+32].rearrange("p t (h d) -> p t h d",h=2)).then_inc(v_ready[s],1)
                def pidx(g,s):
                    return bass.ds(g*2+s,1)
                def body(bgn,last):
                    values(1)
                    pool.drain().then_inc(raw_free,1)
                    if not last:
                        pool.wait_ge(raw_loaded,48).then_inc(raw_loaded,-48)
                        natural((gsel(bgn,0),0)); values(0); natural((gsel(bgn,1),1))
                def gsel(g,s): return g*2+s
                pool.wait_ge(raw_loaded,48).then_inc(raw_loaded,-48)
                natural((0,0)); values(0); natural((1,1))
                nb=BATCH*GROUPS
                if causal:
                    body(1,False); body(2,False); body(3,False)
                    with pool.Fori(1,BATCH):
                        for g in range(GROUPS): body(g,False)
                    values(1)
                else:
                    with pool.Fori(1,nb):
                        body(0,False)
                    values(1)

            def fills(f):
                return (kn,qn)[f//2], (f%2)*4

            @block.tensor
            def _(pe):
                pe.sem_inc(nat_free,1); pe.sem_inc(v_free[0],1); pe.sem_inc(v_free[1],1)
                pe.wait_ge(consts,48 if causal else 16)
                if causal: pe.wait_ge(zeros_done,1).then_inc(zeros_done,-1)
                def fill(f):
                    src,t0=fills(f)
                    if f==0: pe.wait_ge(nat_ready,1).then_inc(nat_ready,-1)
                    pe.wait_ge(s1_free if f<2 else t_free,1).then_inc(s1_free if f<2 else t_free,-1)
                    bank=S1[:,f,:] if f<2 else TP[:]
                    for t in range(4):
                        last=pe.transpose(bank[:,128*t:128*t+128],src[:,t0+t].rearrange("p h w -> p (h w)"),ident[:])
                    last.then_inc(s1_full if f<2 else t_act,1)
                def pass1(s,mx,first):
                    qt,h,half=mx
                    if first:
                        pe.wait_ge(t_free,1)
                        pe.sem_inc(nat_free,1)
                    pe.wait_ge(s1_free,1).then_inc(s1_free,-1)
                    b=pass1.n%2; pass1.n+=1
                    n=512 if not causal else min(512,(qt+1)*128-half*512)
                    diag=causal and qt//4==half
                    mm=pe.matmul(S1[:,b,0:n],qT[:,s,qt*128:qt*128+128],kT[:,s,h,half*512:half*512+n],start=True,stop=not diag)
                    if diag:
                        mm=pe.matmul(S1[:,b,n-128:n],maskr[:,0:128],maskr[:,128:256],start=False,stop=True)
                    mm.then_inc(s1_full,1)
                pass1.n=0
                def qk(s,n):
                    c,kt=steps[n]
                    if n==0: pe.wait_ge(m_placed,32).then_inc(m_placed,-32)
                    pe.wait_ge(s2_free,1).then_inc(s2_free,-1)
                    f=first_col(c,kt)
                    for h in range(2):
                        diag=causal and kt*128>=c*512
                        mm=pe.matmul(S2[:,n%2,h,f:512],kT[:,s,h,kt*128:kt*128+128],qT[:,s,c*512+f:c*512+512],start=True,stop=not diag)
                        if diag:
                            e=kt*128-c*512+128
                            w=e-f
                            mm=pe.matmul(S2[:,n%2,h,f:e],maskr[:,0:128],maskr[:,512-w:512],start=False,stop=True)
                    mm.then_inc(s2_full,1)
                def pv(s,g):
                    if g==NS//2-1:
                        pe.wait_ge(s2_free,2).then_inc(s2_free,-2); pe.sem_inc(s2_free,2)
                    if g==0: pe.wait_ge(v_ready[s],1).then_inc(v_ready[s],-1)
                    c,_=steps[2*g]
                    for h in range(2):
                        for x in range(2):
                            n=2*g+x; c,kt=steps[n]; f=first_col(c,kt); j=2*h+x
                            st=kt<2; en=g in (last_group_c0,NS//2-1)
                            mm=pe.matmul(OP[32*j:32*j+32,f:512],vn[:,s,kt,h,:],pr[:,n%4,h,f:512],start=st,stop=en,skip_group_check=True)
                    if g in (last_group_c0,NS//2-1): mm.then_inc(o_full,1)
                def finish(free_v=None):
                    pe.wait_ge(ot_ready,1).then_inc(ot_ready,-1)
                    if free_v is not None: pe.sem_inc(v_free[free_v],1)
                    pe.wait_ge(t_free,1).then_inc(t_free,-1)
                    for t in range(4):
                        mm=pe.transpose(TP[:,128*t:128*t+128],ot[:,128*t:128*t+128],ident[:])
                    mm.then_inc(t_dve,1)
                def mtrans():
                    pe.wait_ge(m_ready,1).then_inc(m_ready,-1); pe.wait_ge(t_free,1).then_inc(t_free,-1)
                    pe.transpose(TP[0:2*TILES,0:128],m16[:],ident[:]).then_inc(t_dve,1)
                def slot(p2,p1,prev):
                    first=True
                    if p1 is not None:
                        for f in range(4): fill(f)
                    for n in range(NS):
                        if prev and n==1: finish(1-p2)
                        if p2 is not None: qk(p2,n)
                        if p1 is not None:
                            for mx in share[n]:
                                pass1(p1,mx,first); first=False
                        if p2 is not None:
                            if n==FIN+1: finish()
                            if n%2==1 and n>=3: pv(p2,(n-3)//2)
                    if p2 is not None:
                        pv(p2,NS//2-1)
                    if p1 is not None: mtrans()
                slot(None,0,False)
                slot(0,1,False); slot(1,0,True)
                with pe.Fori(1,BATCH*GROUPS-1):
                    slot(0,1,True); slot(1,0,True)
                slot(0,1,True); slot(1,None,True)
                finish()

            @block.scalar
            def _(act):
                nc.scalar.preload_act_table(ACT.Exp)
                act.sem_inc(s2_free,2)
                def evac_q(s,f):
                    act.wait_ge(t_act,1).then_inc(t_act,-1)
                    nc.scalar.activation(qT[:,s,(f-2)*512:(f-2)*512+512],TP[:],ACT.Copy).then_inc(t_free,1)
                def exp(n):
                    c,kt=steps[n]; f=first_col(c,kt)
                    act.wait_ge(s2_full,1).then_inc(s2_full,-1)
                    nc.scalar.activation(pr[:,n%4,:,f:512],S2[:,n%2,:,f:512],ACT.Exp,scale=exp_scale).then_inc(s2_free,1)
                def slot(p2,p1):
                    if p1 is not None:
                        evac_q(p1,2); evac_q(p1,3)
                    for n in range(NS):
                        if p2 is not None: exp(n)
                slot(None,0)
                slot(0,1); slot(1,0)
                with act.Fori(1,BATCH*GROUPS-1):
                    slot(0,1); slot(1,0)
                slot(0,1); slot(1,None)

            @block.vector
            def _(dve):
                nc.vector.memset(kT[64:128,:,0,:].bitcast(F32),0.0).then_inc(dve_done,1)
                nc.vector.memset(kT[0:64,:,1,:].bitcast(F32),0.0).then_inc(dve_done,1)
                nc.vector.memset(mparts[:],-3.0e38).then_inc(dve_done,1)
                dve.wait_ge(dve_done,3).then_inc(dve_done,-3)
                if causal:
                    dve.wait_ge(consts,48)
                    nc.vector.tensor_copy(maskr[:],maskf[:]).then_inc(zeros_done,1)
                dve.sem_inc(t_free,1); dve.sem_inc(s1_free,2)
                def evac_k(s,f):
                    dve.wait_ge(s1_full,1).then_inc(s1_full,-1)
                    for h in range(2):
                        x=nc.vector.tensor_copy(kT[64*h:64*h+64,s,h,f*512:f*512+512],S1[64*h:64*h+64,f,:])
                    x.then_inc(s1_free,1)
                def rowmax(mx):
                    qt,h,half=mx
                    b=rowmax.n%2; rowmax.n+=1
                    n=512 if not causal else min(512,(qt+1)*128-half*512)
                    dve.wait_ge(s1_full,1).then_inc(s1_full,-1)
                    nc.vector.tensor_reduce(mparts[:,h,qt,half:half+1],S1[:,b,0:n],AX.X,ALU.max).then_inc(s1_free,1)
                rowmax.n=0
                def evac_o():
                    dve.wait_ge(o_full,1).then_inc(o_full,-1)
                    nc.vector.tensor_copy(ot[:],OP[:]).then_inc(ot_ready,1)
                def finish(s,c):
                    dve.wait_ge(t_dve,1).then_inc(t_dve,-1)
                    o4=TP[:].rearrange("p (t h x d) -> p t h x d",t=4,h=2,x=2)
                    nc.vector.tensor_reduce(osum[:],o4[:,:,:,:,0:HD+1].rearrange("p t h x d -> p t h d x"),AX.X,ALU.add).then_inc(dve_done,1)
                    dve.wait_ge(dve_done,1).then_inc(dve_done,-1)
                    dve.sem_inc(t_free,1)
                    nc.vector.reciprocal(rcp[:],osum[:,:,:,HD:HD+1]).then_inc(dve_done,1)
                    dve.wait_ge(dve_done,1).then_inc(dve_done,-1)
                    x=nc.vector.tensor_tensor(aon[:,4*c:4*c+4,2*s:2*s+2,:],osum[:,:,:,0:HD],rcp[:].broadcast_to([128,4,2,HD]),ALU.mult)
                    x.then_inc(ao_ready if (s==1 and c==1) else dve_done,1)
                    if not (s==1 and c==1): dve.wait_ge(dve_done,1).then_inc(dve_done,-1)
                def mfinal():
                    dve.drain().then_inc(dve_done,1)
                    dve.wait_ge(dve_done,1).then_inc(dve_done,-1)
                    nc.vector.tensor_reduce(m16[:].rearrange("p (h t) -> p h t",h=2),mparts[:],AX.X,ALU.max).then_inc(m_ready,1)
                    dve.wait_ge(t_dve,1).then_inc(t_dve,-1)
                    nc.vector.tensor_copy(mT[:],TP[0:2*TILES,0:128]).then_inc(dve_done,1)
                    dve.wait_ge(dve_done,1).then_inc(dve_done,-1)
                    dve.sem_inc(mT_ready,1); dve.sem_inc(t_free,1)
                def slot(p2,p1,prev,first_slot=False):
                    if p1 is not None:
                        evac_k(p1,0); evac_k(p1,1)
                    if prev: evac_o()
                    for n in range(NS):
                        if prev and n==1:
                            finish(1-p2,1)
                        if p1 is not None:
                            for mx in share[n]: rowmax(mx)
                        if p2 is not None:
                            if n==FIN: evac_o()
                            if n==FIN+1:
                                if p2==0 and not first_slot: dve.wait_ge(ao_stored,16).then_inc(ao_stored,-16)
                                finish(p2,0)
                    if p1 is not None: mfinal()
                slot(None,0,False)
                slot(0,1,False,True); slot(1,0,True)
                with dve.Fori(1,BATCH*GROUPS-1):
                    slot(0,1,True); slot(1,0,True)
                slot(0,1,True); slot(1,None,True)
                evac_o(); finish(1,1)

TOK=BATCH*SEQ
NT=TOK//128
KC=DIM//128
EXPERTS=8
F0=512
SLOTS0=NT*2+EXPERTS
F1=1024
CAP=TOK//EXPERTS
RMS_EPS=1e-6; LN_EPS=1e-5; EPS=1e-9

def staged(stages,count):
    for n in range(count+len(stages)-1):
        for k in reversed(range(len(stages))):
            if 0<=n-k<count: stages[k](n-k)

def rows_of(ap,b,u):
    return ap[bass.ds(b*SEQ+u*128,128),:]

def ln_qkv(nc,tag,src,w_d,qkv,ident_d,bias_d=None,z=None,x_out=None):
    W=3*DIM
    with Mem(nc,tag) as m:
        ident=m.sb("ident",[128,128]); w=m.sb("w",[128,KC,W]); half=m.sb("half",[128,1])
        bias=m.sb("bias",[128,W]) if bias_d is not None else None
        R=4
        xt=m.sb("xt",[128,R,DIM]); st=m.sb("st",[128,R,12]); xn=m.sb("xn",[128,2,DIM]); xT=m.sb("xT",[128,2,DIM]); y=m.sb("y",[128,2,W])
        st2=m.sb("st2",[128,R,12]); x2=m.sb("x2",[128,R,DIM]); tmp=m.sb("tmp",[128,R,DIM])
        T=m.ps("T",[128,2,512]); Y=m.ps("Y",[128,2,1024])
        consts=m.sem("consts"); half_done=m.sem("half_done")
        x_loaded=[m.sem(f"x_loaded{i}") for i in range(R)]; x_free=m.sem("x_free")
        dve_done=m.sem("dve_done"); var_ready=m.sem("var_ready"); rstd_ready=m.sem("rstd_ready"); var2_ready=m.sem("var2_ready"); rstd2_ready=m.sem("rstd2_ready")
        xn_ready=m.sem("xn_ready"); xn_free=m.sem("xn_free"); t_full=m.sem("t_full"); xT_ready=m.sem("xT_ready")
        y_full=m.sem("y_full"); y_copied=m.sem("y_copied"); y_free=m.sem("y_free"); y_store=m.sem("y_store")
        stored=[m.sem(f"stored{i}") for i in range(2)]
        xs_ready=m.sem("xs_ready"); xs_stored=[m.sem(f"xs_stored{i}") for i in range(R)]
        xs=x2 if z is not None else xt
        with nc.Block() as block:
            @block.sync
            def _(sp):
                sp.dma_start(ident[:],ident_d).then_inc(consts,16)
                sp.dma_start(w[:],w_d.rearrange("(k p) n -> p k n",p=128)).then_inc(consts,16)
                if bias is not None: sp.dma_start(bias[:],bias_d.partition_broadcast(128)).then_inc(consts,16)
                with sp.Fori(0,BATCH) as b:
                    for u in range(TILES):
                        sp.wait_ge(x_free,1).then_inc(x_free,-1)
                        sp.dma_start(xt[:,u%R],rows_of(src,b,u)).then_inc(x_loaded[u%R],16)
                        if z is not None and u>=2:
                            sp.wait_ge(xs_ready,1).then_inc(xs_ready,-1)
                            sp.dma_start(rows_of(x_out,b,u-2),x2[:,(u-2)%R]).then_inc(xs_stored[(u-2)%R],16)
                    if z is not None:
                        for u in (TILES-2,TILES-1):
                            sp.wait_ge(xs_ready,1).then_inc(xs_ready,-1)
                            sp.dma_start(rows_of(x_out,b,u),x2[:,u%R]).then_inc(xs_stored[u%R],16)
            @block.gpsimd
            def _(pool):
                nc.gpsimd.memset(half[:],-0.5).then_inc(half_done,1)
                pool.wait_ge(half_done,1)
                with pool.Fori(0,BATCH):
                    def r1(u):
                        pool.wait_ge(var_ready,1).then_inc(var_ready,-1)
                        nc.gpsimd.tensor_tensor(st[:,u%R,9:10],st[:,u%R,8:9],half[:],ALU.pow).then_inc(rstd_ready,1)
                    def r2(u):
                        pool.wait_ge(var2_ready,1).then_inc(var2_ready,-1)
                        nc.gpsimd.tensor_tensor(st2[:,u%R,9:10],st2[:,u%R,8:9],half[:],ALU.pow).then_inc(rstd2_ready,1)
                    staged([r2,r1] if z is not None else [r1],TILES)
            @block.vector
            def _(dve):
                def done(i):
                    i.then_inc(dve_done,1); dve.wait_ge(dve_done,1).then_inc(dve_done,-1)
                def stats(x,s,out):
                    done(nc.vector.bn_stats(s[:,0:6],x))
                    done(nc.vector.bn_aggr(s[:,6:8],s[:,0:6]))
                    nc.vector.tensor_scalar(s[:,8:9],s[:,7:8],LN_EPS,None,ALU.add).then_inc(out,1)
                if bias is not None: dve.wait_ge(consts,48)
                with dve.Fori(0,BATCH) as b:
                    def z_stats(u):
                        stats(z[:,bass.ds(b*TILES+u,1),:].rearrange("p o d -> p (o d)"),st2[:,u%R],var2_ready)
                    def x_new(u):
                        dve.wait_ge(rstd2_ready,1).then_inc(rstd2_ready,-1)
                        done(nc.vector.tensor_scalar(tmp[:,u%R],z[:,bass.ds(b*TILES+u,1),:].rearrange("p o d -> p (o d)"),st2[:,u%R,6:7],st2[:,u%R,9:10],ALU.subtract,ALU.mult))
                        dve.wait_ge(x_loaded[u%R],16).then_inc(x_loaded[u%R],-16)
                        dve.wait_ge(xs_stored[u%R],16).then_inc(xs_stored[u%R],-16)
                        done(nc.vector.tensor_tensor(x2[:,u%R],tmp[:,u%R],xt[:,u%R],ALU.add))
                        dve.sem_inc(xs_ready,1); dve.sem_inc(x_free,1)
                        stats(x2[:,u%R],st[:,u%R],var_ready)
                    def x_stats(u):
                        dve.wait_ge(x_loaded[u%R],16).then_inc(x_loaded[u%R],-16)
                        stats(xt[:,u%R],st[:,u%R],var_ready)
                    def normal(u):
                        dve.wait_ge(rstd_ready,1).then_inc(rstd_ready,-1); dve.wait_ge(xn_free,1).then_inc(xn_free,-1)
                        done(nc.vector.tensor_scalar(xn[:,u%2],xs[:,u%R],st[:,u%R,6:7],st[:,u%R,9:10],ALU.subtract,ALU.mult))
                        dve.sem_inc(xn_ready,1)
                        if z is None: dve.sem_inc(x_free,1)
                    def y_out(u):
                        if bias is None: return
                        dve.wait_ge(y_full,1).then_inc(y_full,-1); dve.wait_ge(stored[u%2],16).then_inc(stored[u%2],-16)
                        nc.vector.tensor_tensor(y[:,u%2],Y[:,u%2,0:W],bias[:],ALU.add).then_inc(y_copied,1)
                    staged(([z_stats,x_new] if z is not None else [x_stats])+[normal,lambda u:None,y_out],TILES)
                if bias is not None:
                    for i in range(2): dve.wait_ge(stored[i],16)
                if z is not None:
                    for i in range(R): dve.wait_ge(xs_stored[i],16)
            @block.tensor
            def _(pe):
                pe.sem_inc(xn_free,2); pe.sem_inc(x_free,R); pe.sem_inc(y_free,2)
                pe.wait_ge(consts,48 if bias is not None else 32)
                with pe.Fori(0,BATCH):
                    def turn(u):
                        pe.wait_ge(xn_ready,1).then_inc(xn_ready,-1)
                        for k in range(KC):
                            mm=pe.transpose(T[:,u%2,128*k:128*k+128],xn[:,u%2,128*k:128*k+128],ident[:])
                        mm.then_inc(t_full,1)
                    def product(u):
                        pe.wait_ge(xT_ready,1).then_inc(xT_ready,-1)
                        pe.sem_inc(xn_free,1)
                        pe.wait_ge(y_free,1).then_inc(y_free,-1)
                        for n0,n1 in ((0,512),(512,W)):
                            for k in range(KC):
                                mm=pe.matmul(Y[:,u%2,n0:n1],xT[:,u%2,128*k:128*k+128],w[:,k,n0:n1],start=k==0,stop=k==KC-1)
                        mm.then_inc(y_full,1)
                    staged([turn,product],TILES)
            @block.scalar
            def _(act):
                nc.scalar.preload_act_table(ACT.Exp)
                for i in range(2): act.sem_inc(stored[i],16)
                if z is not None:
                    for i in range(R): act.sem_inc(xs_stored[i],16)
                with act.Fori(0,BATCH) as b:
                    def turned(u):
                        act.wait_ge(t_full,1).then_inc(t_full,-1)
                        nc.scalar.activation(xT[:,u%2],T[:,u%2,0:DIM],ACT.Copy).then_inc(xT_ready,1)
                    def y_out(u):
                        if bias is None:
                            act.wait_ge(y_full,1).then_inc(y_full,-1); act.wait_ge(stored[u%2],16).then_inc(stored[u%2],-16)
                            nc.scalar.activation(y[:,u%2],Y[:,u%2,0:W],ACT.Copy).then_inc(y_copied,1)
                        act.wait_ge(y_copied,1).then_inc(y_copied,-1)
                        act.sem_inc(y_free,1)
                        act.dma_start(qkv[bass.ds(b*GROUPS,GROUPS)][:,:,u*128:u*128+128,:].rearrange("g m p c -> p (g m) c"),
                                      y[:,u%2].rearrange("p (a c) -> p a c",c=64)).then_inc(stored[u%2],16)
                    staged([turned,y_out],TILES)
                if bias is None:
                    for i in range(2): act.wait_ge(stored[i],16)

def attn_post(nc,tag,ao,w_d,x_in,ident_d,x_out=None,z=None,bias_d=None,g_d=None,b_d=None,cent_d=None,f=None,norm=None,scores=None):
    last=bias_d is not None
    with Mem(nc,tag) as m:
        ident=m.sb("ident",[128,128]); w=m.sb("w",[128,KC,DIM]); half=m.sb("half",[128,1])
        R=4
        at=m.sb("at",[128,R,DIM]); xt=m.sb("xt",[128,R,DIM]); aT=m.sb("aT",[128,2,DIM])
        s1=m.sb("s1",[128,R,12]); s2=m.sb("s2",[128,R,12]); s3=m.sb("s3",[128,R,12])
        yb=m.sb("yb",[128,R,DIM]); t=m.sb("t",[128,R,DIM]); xo=m.sb("xo",[128,R,DIM])
        T=m.ps("T",[128,2,512]); YR=2 if last else 4; Y=m.ps("Y",[128,YR,512])
        if last:
            bias=m.sb("bias",[128,DIM]); gm=m.sb("gm",[128,DIM]); bm=m.sb("bm",[128,DIM]); cent=m.sb("cent",[128,KC,EXPERTS])
            fn=m.sb("fn",[128,R,DIM]); nrm=m.sb("nrm",[128,R,DIM]); n_free=m.sem("n_free"); n_keep=m.sem("n_keep"); n_turned_=m.sem("n_turned"); nT=m.sb("nT",[128,2,DIM]); T2=m.ps("T2",[128,2,512]); SC=m.ps("SC",[128,2,512])
            t2_full=m.sem("t2_full"); nT_ready=m.sem("nT_ready"); sc_full=m.sem("sc_full"); sc_free=m.sem("sc_free"); n_ready=m.sem("n_ready"); rstd3=m.sem("rstd3"); var3=m.sem("var3")
        consts=m.sem("consts"); half_done=m.sem("half_done")
        a_loaded=[m.sem(f"a_loaded{i}") for i in range(R)]; x_loaded=[m.sem(f"x_loaded{i}") for i in range(R)]; a_free=m.sem("a_free"); x_free=m.sem("x_free")
        dve_done=m.sem("dve_done"); var1=m.sem("var1"); rstd1=m.sem("rstd1"); var2=m.sem("var2"); rstd2=m.sem("rstd2")
        t_full=m.sem("t_full"); aT_ready=m.sem("aT_ready"); y_full=m.sem("y_full"); y_free=m.sem("y_free")
        xo_ready=m.sem("xo_ready"); xo_stored=[m.sem(f"xo_stored{i}") for i in range(R)]
        NCONST=16*(2 if not last else 6)
        with nc.Block() as block:
            @block.sync
            def _(sp):
                sp.dma_start(ident[:],ident_d).then_inc(consts,16)
                sp.dma_start(w[:],w_d.rearrange("(k p) n -> p k n",p=128)).then_inc(consts,16)
                if last:
                    for dst,s in ((bias,bias_d),(gm,g_d),(bm,b_d)):
                        sp.dma_start(dst[:],s.partition_broadcast(128)).then_inc(consts,16)
                    sp.dma_start(cent[:],cent_d.rearrange("(k p) n -> p k n",p=128)).then_inc(consts,16)
                with sp.Fori(0,BATCH) as b:
                    for u in range(TILES):
                        sp.wait_ge(a_free,1).then_inc(a_free,-1)
                        sp.dma_start(at[:,u%R].rearrange("p (g c) -> p g c",g=GROUPS),ao[bass.ds(b*GROUPS,GROUPS)][:,u*128:u*128+128,:].rearrange("g p c -> p g c")).then_inc(a_loaded[u%R],16)
                        sp.wait_ge(x_free,1).then_inc(x_free,-1)
                        sp.dma_start(xt[:,u%R],rows_of(x_in,b,u)).then_inc(x_loaded[u%R],16)
            @block.gpsimd
            def _(pool):
                nc.gpsimd.memset(half[:],-0.5).then_inc(half_done,1)
                pool.wait_ge(half_done,1)
                with pool.Fori(0,BATCH):
                    def root(var,s,out):
                        def r(u):
                            pool.wait_ge(var,1).then_inc(var,-1)
                            nc.gpsimd.tensor_tensor(s[:,u%R,9:10],s[:,u%R,8:9],half[:],ALU.pow).then_inc(out,1)
                        return r
                    staged([root(var1,s1,rstd1),root(var2,s2,rstd2)]+([root(var3,s3,rstd3)] if last else []),TILES)
            @block.vector
            def _(dve):
                def done(i):
                    i.then_inc(dve_done,1); dve.wait_ge(dve_done,1).then_inc(dve_done,-1)
                def stats(x,s,out):
                    done(nc.vector.bn_stats(s[:,0:6],x))
                    done(nc.vector.bn_aggr(s[:,6:8],s[:,0:6]))
                    nc.vector.tensor_scalar(s[:,8:9],s[:,7:8],LN_EPS,None,ALU.add).then_inc(out,1)
                if last: dve.wait_ge(consts,NCONST)
                with dve.Fori(0,BATCH) as b:
                    def y_stats(u):
                        dve.wait_ge(y_full,1).then_inc(y_full,-1)
                        if last:
                            done(nc.vector.tensor_tensor(yb[:,u%R],Y[:,u%YR,0:DIM],bias[:],ALU.add))
                            dve.sem_inc(y_free,1)
                        stats(yb[:,u%R] if last else Y[:,u%YR,0:DIM],s1[:,u%R],var1)
                    def row(x,u):
                        return x[:,bass.ds(b*TILES+u,1),:].rearrange("p o d -> p (o d)")
                    def residual(u):
                        dve.wait_ge(rstd1,1).then_inc(rstd1,-1)
                        done(nc.vector.tensor_scalar(t[:,u%R],yb[:,u%R] if last else Y[:,u%YR,0:DIM],s1[:,u%R,6:7],s1[:,u%R,9:10],ALU.subtract,ALU.mult))
                        if not last: dve.sem_inc(y_free,1)
                        dve.wait_ge(x_loaded[u%R],16).then_inc(x_loaded[u%R],-16)
                        if not last: dve.wait_ge(xo_stored[u%R],16).then_inc(xo_stored[u%R],-16)
                        x=row(z,u) if last else xo[:,u%R]
                        done(nc.vector.tensor_tensor(x,t[:,u%R],xt[:,u%R],ALU.add))
                        dve.sem_inc(x_free,1)
                        if not last: dve.sem_inc(xo_ready,1)
                        stats(x,s2[:,u%R],var2)
                    def normal(u):
                        dve.wait_ge(rstd2,1).then_inc(rstd2,-1)
                        done(nc.vector.tensor_scalar(row(f if last else z,u),row(z,u) if last else xo[:,u%R],s2[:,u%R,6:7],s2[:,u%R,9:10],ALU.subtract,ALU.mult))
                        if last: stats(row(f,u),s3[:,u%R],var3)
                    def affine(u):
                        dve.wait_ge(rstd3,1).then_inc(rstd3,-1)
                        done(nc.vector.tensor_scalar(fn[:,u%R],row(f,u),s3[:,u%R,6:7],s3[:,u%R,9:10],ALU.subtract,ALU.mult))
                        done(nc.vector.tensor_tensor(fn[:,u%R],fn[:,u%R],gm[:],ALU.mult))
                        dve.wait_ge(n_free,1).then_inc(n_free,-1); dve.wait_ge(n_turned_,1).then_inc(n_turned_,-1)
                        done(nc.vector.tensor_tensor(nrm[:,u%R],fn[:,u%R],bm[:],ALU.add))
                        dve.sem_inc(n_ready,1); dve.sem_inc(n_keep,1)
                    def score_out(u):
                        dve.wait_ge(sc_full,1).then_inc(sc_full,-1)
                        nc.vector.tensor_copy(scores[:,:,bass.ds(b*TILES+u,1)].rearrange("p e o -> p (e o)"),SC[:,u%2,0:EXPERTS]).then_inc(sc_free,1)
                    staged([y_stats,residual,normal]+([affine,lambda u:None,score_out] if last else []),TILES)
                if not last:
                    for i in range(R): dve.wait_ge(xo_stored[i],16)
            @block.tensor
            def _(pe):
                pe.sem_inc(a_free,R); pe.sem_inc(x_free,R); pe.sem_inc(y_free,YR)
                if last: pe.sem_inc(sc_free,2); pe.sem_inc(n_free,R); pe.sem_inc(n_turned_,R)
                pe.wait_ge(consts,NCONST)
                with pe.Fori(0,BATCH):
                    def turn(u):
                        pe.wait_ge(a_loaded[u%R],16).then_inc(a_loaded[u%R],-16)
                        for k in range(KC):
                            mm=pe.transpose(T[:,u%2,128*k:128*k+128],at[:,u%R,128*k:128*k+128],ident[:])
                        mm.then_inc(t_full,1)
                    def product(u):
                        pe.wait_ge(aT_ready,1).then_inc(aT_ready,-1)
                        pe.sem_inc(a_free,1)
                        pe.wait_ge(y_free,1).then_inc(y_free,-1)
                        for k in range(KC):
                            mm=pe.matmul(Y[:,u%YR,0:DIM],aT[:,u%2,128*k:128*k+128],w[:,k,:],start=k==0,stop=k==KC-1)
                        mm.then_inc(y_full,1)
                    def n_turn(u):
                        pe.wait_ge(n_ready,1).then_inc(n_ready,-1)
                        for k in range(KC):
                            mm=pe.transpose(T2[:,u%2,128*k:128*k+128],nrm[:,u%R,128*k:128*k+128],ident[:])
                        mm.then_inc(t2_full,1)
                    def score(u):
                        pe.wait_ge(nT_ready,1).then_inc(nT_ready,-1); pe.sem_inc(n_turned_,1); pe.wait_ge(sc_free,1).then_inc(sc_free,-1)
                        for k in range(KC):
                            mm=pe.matmul(SC[:,u%2,0:EXPERTS],nT[:,u%2,128*k:128*k+128],cent[:,k,:],start=k==0,stop=k==KC-1)
                        mm.then_inc(sc_full,1)
                    no=lambda u:None
                    staged([turn,product]+([no,no,no,n_turn,score] if last else []),TILES)
            @block.scalar
            def _(act):
                nc.scalar.preload_act_table(ACT.Exp)
                if not last:
                    for i in range(R): act.sem_inc(xo_stored[i],16)
                with act.Fori(0,BATCH) as b:
                    def turned(u):
                        act.wait_ge(t_full,1).then_inc(t_full,-1)
                        nc.scalar.activation(aT[:,u%2],T[:,u%2,0:DIM],ACT.Copy).then_inc(aT_ready,1)
                    def store(u):
                        act.wait_ge(xo_ready,1).then_inc(xo_ready,-1)
                        act.dma_start(rows_of(x_out,b,u),xo[:,u%R]).then_inc(xo_stored[u%R],16)
                    def n_turned(u):
                        act.wait_ge(t2_full,1).then_inc(t2_full,-1)
                        nc.scalar.activation(nT[:,u%2],T2[:,u%2,0:DIM],ACT.Copy).then_inc(nT_ready,1)
                    def keep(u):
                        act.wait_ge(n_keep,1).then_inc(n_keep,-1)
                        nc.scalar.activation(norm[:,bass.ds(b*TILES+u,1),:].rearrange("p o d -> p (o d)"),nrm[:,u%R],ACT.Copy).then_inc(n_free,1)
                    no=lambda u:None
                    staged([turned,no,no]+([no,no,keep,n_turned] if last else [store]),TILES)

GR,PER=4,2
LG=GR+GR*PER

def rms_logits(nc,tag,z,zn,lg,norm_d,wg_d,ident_d):
    with Mem(nc,tag) as m:
        ident=m.sb("ident",[128,128]); wg=m.sb("wg",[128,KC,LG]); nw=m.sb("nw",[128,DIM]); half=m.sb("half",[128,NT])
        sq=m.sb("sq",[128,2,DIM]); ss=m.sb("ss",[128,NT]); ms=m.sb("ms",[128,NT]); rstd=m.sb("rstd",[128,NT])
        zs=m.sb("zs",[128,2,DIM]); zT=m.sb("zT",[128,2,DIM])
        T=m.ps("T",[128,2,512]); L=m.ps("L",[128,2,512])
        consts=m.sem("consts"); half_done=m.sem("half_done"); squares=m.sem("squares"); ms_ready=m.sem("ms_ready"); rstd_ready=m.sem("rstd_ready")
        zs_ready=m.sem("zs_ready"); zs_copy=m.sem("zs_copy"); zs_free=m.sem("zs_free"); zs_turned=m.sem("zs_turned"); t_full=m.sem("t_full"); zT_ready=m.sem("zT_ready"); l_full=m.sem("l_full"); l_free=m.sem("l_free")
        act_done=m.sem("act_done")
        with nc.Block() as block:
            @block.sync
            def _(sp):
                sp.dma_start(ident[:],ident_d).then_inc(consts,16)
                sp.dma_start(wg[:],wg_d.rearrange("(k p) n -> p k n",p=128)).then_inc(consts,16)
                sp.dma_start(nw[:],norm_d.partition_broadcast(128)).then_inc(consts,16)
            @block.gpsimd
            def _(pool):
                nc.gpsimd.memset(half[:],-0.5).then_inc(half_done,1)
                pool.wait_ge(half_done,1)
                pool.wait_ge(ms_ready,1).then_inc(ms_ready,-1)
                nc.gpsimd.tensor_tensor(rstd[:],ms[:],half[:],ALU.pow).then_inc(rstd_ready,1)
            @block.scalar
            def _(act):
                nc.scalar.preload_act_table(ACT.Exp)
                act.sem_inc(act_done,2)
                with act.Fori(0,BATCH) as b:
                    for u in range(TILES):
                        act.wait_ge(act_done,1).then_inc(act_done,-1)
                        t=bass.ds(b*TILES+u,1)
                        nc.scalar.activation(sq[:,u%2],z[:,t,:].rearrange("p o d -> p (o d)"),ACT.Square,accum_out=ss[:,t]).then_inc(act_done,1)
                act.wait_ge(act_done,2).then_inc(act_done,-2)
                act.sem_inc(squares,1)
                with act.Fori(0,BATCH) as b:
                    def turned(u):
                        act.wait_ge(t_full,1).then_inc(t_full,-1)
                        nc.scalar.activation(zT[:,u%2],T[:,u%2,0:DIM],ACT.Copy).then_inc(zT_ready,1)
                    def keep(u):
                        act.wait_ge(zs_copy,1).then_inc(zs_copy,-1)
                        nc.scalar.activation(zn[:,bass.ds(b*TILES+u,1),:].rearrange("p o d -> p (o d)"),zs[:,u%2],ACT.Copy).then_inc(zs_free,1)
                    staged([keep,turned],TILES)
            @block.vector
            def _(dve):
                dve.wait_ge(consts,48)
                dve.wait_ge(squares,1).then_inc(squares,-1)
                nc.vector.tensor_scalar(ms[:],ss[:],1.0/DIM,RMS_EPS,ALU.mult,ALU.add).then_inc(ms_ready,1)
                dve.wait_ge(rstd_ready,1).then_inc(rstd_ready,-1)
                with dve.Fori(0,BATCH) as b:
                    def scaled(u):
                        dve.wait_ge(zs_free,1).then_inc(zs_free,-1); dve.wait_ge(zs_turned,1).then_inc(zs_turned,-1)
                        t=bass.ds(b*TILES+u,1)
                        nc.vector.scalar_tensor_tensor(out=zs[:,u%2],in0=z[:,t,:].rearrange("p o d -> p (o d)"),scalar=rstd[:,t],in1=nw[:],op0=ALU.mult,op1=ALU.mult).then_inc(zs_ready,1)
                    staged([scaled],TILES)
                    dve.wait_ge(l_full,1).then_inc(l_full,-1)
                    nc.vector.tensor_copy(lg[:,:,bass.ds(b*TILES,TILES)],L[:,0,0:TILES*LG].rearrange("p (t l) -> p l t",l=LG)).then_inc(l_free,1)
            @block.tensor
            def _(pe):
                pe.sem_inc(zs_free,2); pe.sem_inc(zs_turned,2); pe.sem_inc(l_free,1)
                pe.wait_ge(consts,48)
                with pe.Fori(0,BATCH):
                    pe.wait_ge(l_free,1).then_inc(l_free,-1)
                    def turn(u):
                        pe.wait_ge(zs_ready,1).then_inc(zs_ready,-1); pe.sem_inc(zs_copy,1)
                        for k in range(KC):
                            mm=pe.transpose(T[:,u%2,128*k:128*k+128],zs[:,u%2,128*k:128*k+128],ident[:])
                        mm.then_inc(t_full,1)
                    def product(u):
                        pe.wait_ge(zT_ready,1).then_inc(zT_ready,-1)
                        pe.sem_inc(zs_turned,1)
                        for k in range(KC):
                            mm=pe.matmul(L[:,0,LG*u:LG*u+LG],zT[:,u%2,128*k:128*k+128],wg[:,k,:],start=k==0,stop=k==KC-1)
                        if u==TILES-1: mm.then_inc(l_full,1)
                    staged([turn,product],TILES)

def route(nc,tag,lg,tri_d,key_d,jv_d,slot,weight,eid,prepare=None):
    with Mem(nc,tag) as m:
        tri=m.sb("tri",[128,2,128],BF); trif=m.sb("trif",[128,2,128]); key=m.sb("key",[128,GR,NT]); jv=m.sb("jv",[128,EXPERTS,SLOTS0])
        e=m.sb("e",[128,GR,NT]); p=m.sb("p",[128,GR,NT]); q=m.sb("q",[128,GR,NT]); oh=m.sb("oh",[128,2,GR,NT])
        a=m.sb("a",[128,NT]); v=m.sb("v",[128,4,NT])
        d=m.sb("d",[128,GR,PER,NT]); pu=m.sb("pu",[128,GR,PER,NT]); c=m.sb("c",[128,GR,PER,NT]); mg=m.sb("mg",[128,GR,NT]); sg=m.sb("sg",[128,GR,NT])
        E=m.sb("E",[128,2,GR,PER,NT]); M=m.sb("M",[128,EXPERTS*NT]); Mb=m.sb("Mb",[128,EXPERTS*NT],BF)
        S=m.sb("S",[128,EXPERTS*NT]); ex=m.sb("ex",[128,EXPERTS*NT]); tot=m.sb("tot",[128,EXPERTS*NT]); zero=m.sb("zero",[128,EXPERTS*NT])
        cnt=m.sb("cnt",[128,4,EXPERTS]); cnti=m.sb("cnti",[128,EXPERTS],I32); sl=m.sb("sl",[128,EXPERTS,NT]); prod=m.sb("prod",[128,2,EXPERTS,NT])
        slf=m.sb("slf",[128,2,NT]); ge=m.sb("ge",[128,EXPERTS,SLOTS0]); ef=m.sb("ef",[128,SLOTS0])
        R=m.ps("R",[128,2,512])
        consts=m.sem("consts"); dve_done=m.sem("dve_done"); x_ready=m.sem("x_ready"); e_ready=m.sem("e_ready"); m_ready=m.sem("m_ready"); r_full=m.sem("r_full")
        prepared=m.sem("prepared")
        lm=lg[:,0:GR,:]; lu=lg[:,GR:LG,:].rearrange("p (g i) t -> p g i t",i=PER)
        def over(x,n): return x.rearrange("p (o t) -> p o t",o=1).broadcast_to([128,n,NT])
        with nc.Block() as block:
            @block.sync
            def _(sp):
                sp.dma_start(trif[:],tri_d).then_inc(consts,16)
                sp.dma_start(key[:],key_d).then_inc(consts,16)
                sp.dma_start(jv[:],jv_d).then_inc(consts,16)
                if prepare:
                    w1,w1_d,w2,w2_d,zeros_d,xs_d=prepare
                    sp.dma_start(w1[:],w1_d.rearrange("(k p) n -> p k n",p=128)).then_inc(prepared,16)
                    sp.dma_start(w2[:],w2_d.rearrange("(k p) n -> p k n",p=128)).then_inc(prepared,16)
                    chunk=zeros_d.shape[0]*zeros_d.shape[1]//DIM
                    for i in range(SLOTS0*128//chunk):
                        sp.dma_start(xs_d[i*chunk:(i+1)*chunk].rearrange("(p b) c -> p (b c)",p=128),zeros_d).then_inc(prepared,16)
                    sp.wait_ge(prepared,16*(2+SLOTS0*128//chunk))
            @block.scalar
            def _(act):
                nc.scalar.preload_act_table(ACT.Exp)
                act.wait_ge(x_ready,1).then_inc(x_ready,-1)
                nc.scalar.activation(e[:],p[:],ACT.Exp).then_inc(e_ready,1)
                nc.scalar.activation(pu[:],d[:],ACT.Exp).then_inc(e_ready,1)
            @block.tensor
            def _(pe):
                pe.wait_ge(m_ready,1).then_inc(m_ready,-1)
                pe.matmul(R[:,0,0:256],tri[:,0,:],Mb[:],start=True,stop=True)
                pe.matmul(R[:,1,0:256],tri[:,1,:],Mb[:],start=True,stop=True).then_inc(r_full,1)
            @block.vector
            def _(dve):
                V=nc.vector
                def done(i):
                    i.then_inc(dve_done,1); dve.wait_ge(dve_done,1).then_inc(dve_done,-1)
                def tt(o,x,y,op): done(V.tensor_tensor(o,x,y,op))
                def ts(o,x,s1,s2,o1,o2=ALU.bypass): done(V.tensor_scalar(o,x,s1,s2,o1,o2))
                def red(o,x,op): done(V.tensor_reduce(o,x,AX.X,op))
                dve.wait_ge(consts,48)
                done(V.memset(zero[:],0.0))
                done(V.tensor_copy(tri[:],trif[:]))
                red(a[:],lm.rearrange("p g t -> p t g"),ALU.max)
                tt(p[:],lm,over(a[:],GR),ALU.subtract)
                tt(mg[:],lu[:,:,0,:],lu[:,:,1,:],ALU.max)
                for i in range(PER): tt(d[:,:,i,:],lu[:,:,i,:],mg[:],ALU.subtract)
                dve.sem_inc(x_ready,1)
                dve.wait_ge(e_ready,2).then_inc(e_ready,-2)
                red(a[:],e[:].rearrange("p g t -> p t g"),ALU.add)
                done(V.reciprocal(a[:],a[:]))
                tt(p[:],e[:],over(a[:],GR),ALU.mult)
                for s in range(2):
                    src=p if s==0 else q
                    red(v[:,s],src[:].rearrange("p g t -> p t g"),ALU.max)
                    tt(e[:],src[:],over(v[:,s],GR),ALU.is_equal)
                    tt(e[:],e[:],key[:],ALU.mult)
                    red(a[:],e[:].rearrange("p g t -> p t g"),ALU.max)
                    tt(oh[:,s],e[:],over(a[:],GR),ALU.is_equal)
                    if s==0: done(V.scalar_tensor_tensor(out=q[:],in0=oh[:,0],scalar=-2.0,in1=p[:],op0=ALU.mult,op1=ALU.add))
                tt(a[:],v[:,0],v[:,1],ALU.add)
                ts(a[:],a[:],EPS,None,ALU.add)
                done(V.reciprocal(a[:],a[:]))
                tt(sg[:],pu[:,:,0,:],pu[:,:,1,:],ALU.add)
                done(V.reciprocal(sg[:],sg[:]))
                for i in range(PER): tt(pu[:,:,i,:],pu[:,:,i,:],sg[:],ALU.mult)
                tt(mg[:],pu[:,:,0,:],pu[:,:,1,:],ALU.max)
                tt(c[:,:,1,:],pu[:,:,1,:],pu[:,:,0,:],ALU.is_gt)
                ts(c[:,:,0,:],c[:,:,1,:],-1.0,1.0,ALU.mult,ALU.add)
                ts(sg[:],mg[:],EPS,None,ALU.add)
                done(V.reciprocal(sg[:],sg[:]))
                tt(mg[:],mg[:],sg[:],ALU.mult)
                for s in range(2):
                    tt(e[:],oh[:,s],mg[:],ALU.mult)
                    red(v[:,2],e[:].rearrange("p g t -> p t g"),ALU.add)
                    tt(v[:,3],v[:,s],a[:],ALU.mult)
                    tt(weight[:,s],v[:,2],v[:,3],ALU.mult)
                    for i in range(PER): tt(E[:,s,:,i,:],oh[:,s],c[:,:,i,:],ALU.mult)
                Ef=[E[:,s].rearrange("p g i t -> p (g i t)") for s in range(2)]
                tt(M[:],Ef[0],Ef[1],ALU.add)
                done(V.tensor_copy(Mb[:],M[:]))
                dve.sem_inc(m_ready,1)
                dve.wait_ge(r_full,1).then_inc(r_full,-1)
                done(V.tensor_copy(tot[:],R[:,1,0:256]))
                done(V.tensor_tensor_scan(out=S[:],data0=tot[:],data1=zero[:],initial=0.0,op0=ALU.add,op1=ALU.add))
                tt(ex[:],S[:],tot[:],ALU.subtract)
                S3=S[:].rearrange("p (e t) -> p e t",t=NT); ex3=ex[:].rearrange("p (e t) -> p e t",t=NT)
                first=ex3[:,:,0]; end=S3[:,:,NT-1]
                tt(cnt[:,0],end,first,ALU.subtract)
                ts(cnt[:,0],cnt[:,0],127.0,None,ALU.add)
                done(V.tensor_copy(cnti[:],cnt[:,0]))
                ts(cnti[:],cnti[:],7,7,ALU.arith_shift_right,ALU.logical_shift_left)
                done(V.tensor_copy(cnt[:,0],cnti[:]))
                done(V.tensor_tensor_scan(out=cnt[:,1],data0=cnt[:,0],data1=zero[:,0:EXPERTS],initial=0.0,op0=ALU.add,op1=ALU.add))
                tt(cnt[:,2],cnt[:,1],cnt[:,0],ALU.subtract)
                tt(cnt[:,3],cnt[:,2],first,ALU.subtract)
                tt(sl[:],ex3,cnt[:,3].rearrange("p (e o) -> p e o",o=1).broadcast_to([128,EXPERTS,NT]),ALU.add)
                tt(sl[:],sl[:],R[:,0,0:256].rearrange("p (e t) -> p e t",t=NT),ALU.add)
                for s in range(2):
                    tt(prod[:,s],Ef[s].rearrange("p (e t) -> p e t",t=NT),sl[:],ALU.mult)
                    red(slf[:,s],prod[:,s].rearrange("p e t -> p t e"),ALU.add)
                    done(V.tensor_copy(slot[:,s],slf[:,s]))
                tt(ge[:],jv[:],cnt[:,1].rearrange("p (e o) -> p e o",o=1).broadcast_to([128,EXPERTS,SLOTS0]),ALU.is_ge)
                red(ef[:],ge[:].rearrange("p e j -> p j e"),ALU.add)
                ts(ef[:],ef[:],float(EXPERTS-1),None,ALU.min)
                done(V.tensor_copy(eid[:],ef[:]))

def experts(nc,tag,zn,slot,eid,w1,w2,xs_d,ys_d,ident_d):
    with Mem(nc,tag) as m:
        ident=m.sb("ident",[128,128]); R=4
        xs=m.sb("xs",[128,R,DIM]); xT=m.sb("xT",[128,2,DIM]); h=m.sb("h",[128,2,F0]); hT=m.sb("hT",[128,2,F0]); y=m.sb("y",[128,2,DIM])
        TX=m.ps("TX",[128,2,512]); TH=m.ps("TH",[128,2,512]); H=m.ps("H",[128,2,512]); Y=m.ps("Y",[128,2,512])
        consts=m.sem("consts"); scattered=m.sem("scattered"); sorted_=m.sem("sorted")
        x_loaded=[m.sem(f"x_loaded{i}") for i in range(R)]; x_free=m.sem("x_free"); tx_full=m.sem("tx_full"); xT_ready=m.sem("xT_ready")
        h_full=m.sem("h_full"); h_ready=m.sem("h_ready"); th_full=m.sem("th_full"); hT_ready=m.sem("hT_ready"); y_full=m.sem("y_full"); y_free=m.sem("y_free"); y_ready=m.sem("y_ready")
        y_stored=[m.sem(f"y_stored{i}") for i in range(2)]; dve_done=m.sem("dve_done")
        U=4
        with nc.Block() as block:
            @block.gpsimd
            def _(pool):
                for t in range(NT):
                    for s in range(2):
                        nc.gpsimd.indirect_dma_start(out=xs_d,out_offset=bass.IndirectOffsetOnAxis(ap=slot[:,s,t:t+1],axis=0),in_=zn[:,t,:],in_offset=None).then_inc(scattered,16)
                pool.wait_ge(scattered,16*2*NT)
                pool.sem_inc(sorted_,1)
            @block.sync
            def _(sp):
                sp.dma_start(ident[:],ident_d).then_inc(consts,16)
                sp.wait_ge(sorted_,1).then_inc(sorted_,-1)
                with sp.Fori(0,SLOTS0//U) as j:
                    def load(u):
                        sp.wait_ge(x_free,1).then_inc(x_free,-1)
                        sp.dma_start(xs[:,u%R],xs_d[bass.ds((j*U+u)*128,128),:]).then_inc(x_loaded[u%R],16)
                    for u in range(U): load(u)
                    
            @block.tensor
            def _(pe):
                pe.sem_inc(x_free,R); pe.sem_inc(y_free,2)
                pe.wait_ge(consts,16)
                def turn_x(u):
                    pe.wait_ge(x_loaded[u%R],16).then_inc(x_loaded[u%R],-16)
                    for k in range(KC):
                        mm=pe.transpose(TX[:,u%2,128*k:128*k+128],xs[:,u%R,128*k:128*k+128],ident[:])
                    mm.then_inc(tx_full,1)
                def first(u,e):
                    pe.wait_ge(xT_ready,1).then_inc(xT_ready,-1)
                    pe.sem_inc(x_free,1)
                    for k in range(KC):
                        mm=pe.matmul(H[:,u%2,:],xT[:,u%2,128*k:128*k+128],w1[:,k,bass.ds(e*F0,F0)],start=k==0,stop=k==KC-1)
                    mm.then_inc(h_full,1)
                def turn_h(u):
                    pe.wait_ge(h_ready,1).then_inc(h_ready,-1)
                    for k in range(F0//128):
                        mm=pe.transpose(TH[:,u%2,128*k:128*k+128],h[:,u%2,128*k:128*k+128],ident[:])
                    mm.then_inc(th_full,1)
                def second(u,e):
                    pe.wait_ge(hT_ready,1).then_inc(hT_ready,-1); pe.wait_ge(y_free,1).then_inc(y_free,-1)
                    for k in range(F0//128):
                        mm=pe.matmul(Y[:,u%2,0:DIM],hT[:,u%2,128*k:128*k+128],w2[:,k,bass.ds(e*DIM,DIM)],start=k==0,stop=k==F0//128-1)
                    mm.then_inc(y_full,1)
                with pe.Fori(0,SLOTS0//U) as j:
                    es=[pe.value_load(eid[0:1,bass.ds(j*U+u,1)],min_val=0,max_val=EXPERTS-1) for u in range(U)]
                    turn_x(0); first(0,es[0]); turn_x(1)
                    for u in range(U):
                        turn_h(u)
                        if u+2<U: turn_x(u+2)
                        if u+1<U: first(u+1,es[u+1])
                        second(u,es[u])
            @block.scalar
            def _(act):
                nc.scalar.preload_act_table(ACT.Silu)
                def x_turned(u):
                    act.wait_ge(tx_full,1).then_inc(tx_full,-1)
                    nc.scalar.activation(xT[:,u%2],TX[:,u%2,0:DIM],ACT.Copy).then_inc(xT_ready,1)
                def silu(u):
                    act.wait_ge(h_full,1).then_inc(h_full,-1)
                    nc.scalar.activation(h[:,u%2],H[:,u%2,:],ACT.Silu).then_inc(h_ready,1)
                with act.Fori(0,SLOTS0//U) as j:
                    def store(u):
                        act.wait_ge(y_ready,1).then_inc(y_ready,-1)
                        act.dma_start(ys_d[bass.ds((j*U+u)*128,128),:],y[:,u%2]).then_inc(y_stored[u%2],16)
                    x_turned(0); x_turned(1); silu(0)
                    for u in range(U):
                        if u+2<U: x_turned(u+2)
                        if u+1<U: silu(u+1)
                        if u>=1: store(u-1)
                    store(U-1)
            @block.vector
            def _(dve):
                for i in range(2): dve.sem_inc(y_stored[i],16)
                with dve.Fori(0,SLOTS0//U) as j:
                    for u in range(U):
                        dve.wait_ge(th_full,1).then_inc(th_full,-1)
                        nc.vector.tensor_copy(hT[:,u%2],TH[:,u%2,:]).then_inc(hT_ready,1)
                        dve.wait_ge(y_full,1).then_inc(y_full,-1); dve.wait_ge(y_stored[u%2],16).then_inc(y_stored[u%2],-16)
                        nc.vector.tensor_copy(y[:,u%2],Y[:,u%2,0:DIM]).then_inc(dve_done,1)
                        dve.wait_ge(dve_done,1).then_inc(dve_done,-1)
                        dve.sem_inc(y_free,1)
                        dve.sem_inc(y_ready,1)
                for i in range(2): dve.wait_ge(y_stored[i],16)

def combine(nc,tag,z,slot,weight,ys_d):
    with Mem(nc,tag) as m:
        R=8
        y=m.sb("y",[128,R,DIM])
        y_loaded=[m.sem(f"y_loaded{i}") for i in range(R)]; y_free=m.sem("y_free"); dve_done=m.sem("dve_done")
        with nc.Block() as block:
            @block.gpsimd
            def _(pool):
                for n in range(2*NT):
                    pool.wait_ge(y_free,1).then_inc(y_free,-1)
                    t,s=n//2,n%2
                    nc.gpsimd.indirect_dma_start(out=y[:,n%R,:],out_offset=None,in_=ys_d,in_offset=bass.IndirectOffsetOnAxis(ap=slot[:,s,t:t+1],axis=0)).then_inc(y_loaded[n%R],16)
            @block.vector
            def _(dve):
                dve.sem_inc(y_free,R)
                for n in range(2*NT):
                    t,s=n//2,n%2
                    dve.wait_ge(y_loaded[n%R],16*(n//R+1))
                    nc.vector.scalar_tensor_tensor(out=z[:,t,:],in0=y[:,n%R],scalar=weight[:,s,t:t+1],in1=z[:,t,:],op0=ALU.mult,op1=ALU.add).then_inc(dve_done,1)
                    dve.wait_ge(dve_done,1).then_inc(dve_done,-1)
                    dve.sem_inc(y_free,1)

BITS=4; LEVELS=32//BITS; CANDS=2**BITS-1

def assign(nc,tag,scores,tri_d,cand_d,pos):
    with Mem(nc,tag) as m:
        tri=m.sb("tri",[128,2,128],BF); trif=m.sb("trif",[128,2,128]); jt=m.sb("jt",[128,LEVELS,CANDS],I32)
        keep=m.sb("keep",[128,NT]); out_=m.sb("out",[128,NT]); s=m.sb("s",[128,NT]); P=m.sb("P",[128,1],I32)
        cand=m.sb("cand",[128,CANDS],I32); msk=m.sb("msk",[128,CANDS],I32); ge=m.sb("ge",[128,CANDS,NT]); part=m.sb("part",[128,CANDS],BF)
        ok=m.sb("ok",[128,CANDS]); jf=m.sb("jf",[128,1]); ji=m.sb("ji",[128,1],I32)
        thr=m.sb("thr",[128,1],I32); flags=m.sb("flags",[128,2,NT],BF); gt=m.sb("gt",[128,2,NT]); tot=m.sb("tot",[128,2,NT]); zero=m.sb("zero",[128,NT]); S=m.sb("S",[128,2,NT])
        rank=m.sb("rank",[128,2,NT]); need=m.sb("need",[128,1]); sel=m.sb("sel",[128,NT]); w=m.sb("w",[128,NT]); base=m.sb("base",[128,1]); posf=m.sb("posf",[128,NT])
        CN=m.ps("CN",[128,512]); R=m.ps("R",[128,2,512])
        consts=m.sem("consts"); dve_done=m.sem("dve_done"); part_ready=m.sem("part_ready"); count_full=m.sem("count_full"); flags_ready=m.sem("flags_ready"); rank_full=m.sem("rank_full")
        with nc.Block() as block:
            @block.sync
            def _(sp):
                sp.dma_start(trif[:],tri_d).then_inc(consts,16)
                sp.dma_start(jt[:],cand_d).then_inc(consts,16)
            @block.tensor
            def _(pe):
                def ranks():
                    pe.wait_ge(flags_ready,1).then_inc(flags_ready,-1)
                    for i in range(2):
                        mm=pe.matmul(R[:,i,0:2*NT],tri[:,i,:],flags[:].rearrange("p f t -> p (f t)"),start=True,stop=True)
                    mm.then_inc(rank_full,1)
                with pe.Fori(0,EXPERTS-1):
                    for l in range(LEVELS):
                        pe.wait_ge(part_ready,1).then_inc(part_ready,-1)
                        pe.matmul(CN[:,0:CANDS],tri[:,1,:],part[:],start=True,stop=True).then_inc(count_full,1)
                    ranks()
                ranks()
            @block.vector
            def _(dve):
                V=nc.vector
                def done(i):
                    i.then_inc(dve_done,1); dve.wait_ge(dve_done,1).then_inc(dve_done,-1)
                def tt(o,x,y,op): done(V.tensor_tensor(o,x,y,op))
                def ts(o,x,s1,s2,o1,o2=ALU.bypass): done(V.tensor_scalar(o,x,s1,s2,o1,o2))
                def red(o,x,op): done(V.tensor_reduce(o,x,AX.X,op))
                dve.wait_ge(consts,32)
                done(V.tensor_copy(tri[:],trif[:]))
                done(V.memset(zero[:],0.0)); done(V.memset(keep[:],1.0)); done(V.memset(base[:],0.0)); done(V.memset(posf[:],0.0))
                def ranks():
                    dve.sem_inc(flags_ready,1)
                    dve.wait_ge(rank_full,1).then_inc(rank_full,-1)
                    done(V.tensor_copy(tot[:].rearrange("p f t -> p (f t)"),R[:,1,0:2*NT]))
                    for i in range(2):
                        done(V.tensor_tensor_scan(out=S[:,i],data0=tot[:,i],data1=zero[:],initial=0.0,op0=ALU.add,op1=ALU.add))
                    tt(rank[:],S[:],tot[:],ALU.subtract)
                    tt(rank[:],rank[:],R[:,0,0:2*NT].rearrange("p (f t) -> p f t",t=NT),ALU.add)
                with dve.Fori(0,EXPERTS-1) as e:
                    sc=scores[:,bass.ds(e,1),:].rearrange("p o t -> p (o t)")
                    ts(out_[:],keep[:],1.0,3.0e38,ALU.subtract,ALU.mult)
                    tt(s[:],sc,keep[:],ALU.mult)
                    tt(s[:],s[:],out_[:],ALU.add)
                    done(V.memset(P[:],-2**31))
                    for l in range(LEVELS):
                        tt(cand[:],jt[:,l,:],P[:].broadcast_to([128,CANDS]),ALU.bitwise_xor)
                        ts(msk[:],cand[:],31,0x7fffffff,ALU.arith_shift_right,ALU.bitwise_and)
                        tt(cand[:],cand[:],msk[:],ALU.bitwise_xor)
                        tt(ge[:],s[:].rearrange("p (o t) -> p o t",o=1).broadcast_to([128,CANDS,NT]),cand[:].bitcast(F32).rearrange("p (c o) -> p c o",o=1).broadcast_to([128,CANDS,NT]),ALU.is_ge)
                        with nc.allow_low_precision("counts up to 32 are exact"):
                            red(part[:],ge[:],ALU.add)
                        dve.sem_inc(part_ready,1)
                        dve.wait_ge(count_full,1).then_inc(count_full,-1)
                        ts(ok[:],CN[:,0:CANDS],float(CAP),None,ALU.is_ge)
                        red(jf[:],ok[:],ALU.add)
                        done(V.tensor_copy(ji[:],jf[:]))
                        ts(ji[:],ji[:],32-BITS*(l+1),None,ALU.logical_shift_left)
                        tt(P[:],ji[:],P[:],ALU.bitwise_xor)
                    ts(thr[:],P[:],31,0x7fffffff,ALU.arith_shift_right,ALU.bitwise_and)
                    tt(thr[:],thr[:],P[:],ALU.bitwise_xor)
                    ts(gt[:,0],s[:],thr[:].bitcast(F32),None,ALU.is_gt)
                    ts(gt[:,1],s[:],thr[:].bitcast(F32),None,ALU.is_equal)
                    done(V.tensor_copy(flags[:],gt[:]))
                    ranks()
                    ts(need[:],S[:,0,NT-1:NT],-1.0,float(CAP),ALU.mult,ALU.add)
                    ts(w[:],rank[:,1],need[:],None,ALU.is_lt)
                    tt(w[:],w[:],gt[:,1],ALU.mult)
                    tt(sel[:],w[:],gt[:,0],ALU.add)
                    ts(w[:],rank[:,1],need[:],base[:],ALU.min,ALU.add)
                    tt(w[:],w[:],rank[:,0],ALU.add)
                    tt(w[:],w[:],sel[:],ALU.mult)
                    tt(posf[:],posf[:],w[:],ALU.add)
                    tt(keep[:],keep[:],sel[:],ALU.subtract)
                    ts(base[:],base[:],float(CAP),None,ALU.add)
                done(V.memset(flags[:],0.0))
                done(V.tensor_copy(flags[:,0],keep[:]))
                ranks()
                ts(w[:],rank[:,0],base[:],None,ALU.add)
                tt(w[:],w[:],keep[:],ALU.mult)
                tt(posf[:],posf[:],w[:],ALU.add)
                done(V.tensor_copy(pos[:],posf[:]))

def experts1(nc,tag,norm,pos,w1_d,w2_d,b1_d,b2_d,xs_d,ys_d,ident_d):
    T4=CAP//128; FC=F1//128
    with Mem(nc,tag) as m:
        ident=m.sb("ident",[128,128]); b1=m.sb("b1",[128,EXPERTS,FC]); b2=m.sb("b2",[128,EXPERTS*DIM])
        w1=m.sb("w1",[128,2,KC,F1]); w2=m.sb("w2",[128,2,FC,DIM]); xs=m.sb("xs",[128,2,T4,DIM]); xT=m.sb("xT",[128,KC,CAP]); hT=m.sb("hT",[128,FC,CAP]); y=m.sb("y",[128,2,DIM])
        TX=m.ps("TX",[128,2,512]); H=m.ps("H",[128,2,512]); Y=m.ps("Y",[128,4,512])
        consts=m.sem("consts"); scattered=m.sem("scattered"); sorted_=m.sem("sorted")
        w_loaded=[m.sem(f"w_loaded{i}") for i in range(2)]; x_loaded=[m.sem(f"x_loaded{i}") for i in range(2)]; w_free=m.sem("w_free")
        tx_full=m.sem("tx_full"); xT_ready=m.sem("xT_ready"); h_full=m.sem("h_full"); hT_ready=m.sem("hT_ready")
        y_full=m.sem("y_full"); y_ready=m.sem("y_ready"); y_stored=[m.sem(f"y_stored{i}") for i in range(2)]
        with nc.Block() as block:
            @block.gpsimd
            def _(pool):
                for t in range(NT):
                    nc.gpsimd.indirect_dma_start(out=xs_d,out_offset=bass.IndirectOffsetOnAxis(ap=pos[:,t:t+1],axis=0),in_=norm[:,t,:],in_offset=None).then_inc(scattered,16)
                pool.wait_ge(scattered,16*NT)
                pool.sem_inc(sorted_,1)
            @block.sync
            def _(sp):
                sp.dma_start(ident[:],ident_d).then_inc(consts,16)
                sp.dma_start(b1[:],b1_d).then_inc(consts,16)
                sp.dma_start(b2[:],b2_d.partition_broadcast(128)).then_inc(consts,16)
                sp.wait_ge(sorted_,1).then_inc(sorted_,-1)
                with sp.Fori(0,EXPERTS//2) as j:
                    for i in range(2):
                        sp.wait_ge(w_free,1).then_inc(w_free,-1)
                        e=bass.ds(j*2+i,1)
                        sp.dma_start(xs[:,i],xs_d[bass.ds((j*2+i)*CAP,CAP),:].rearrange("(t p) d -> p t d",p=128)).then_inc(x_loaded[i],16)
                        sp.dma_start(w1[:,i],w1_d[e][0].rearrange("(k p) f -> p k f",p=128)).then_inc(w_loaded[i],16)
                        sp.dma_start(w2[:,i],w2_d[e][0].rearrange("(k p) d -> p k d",p=128)).then_inc(w_loaded[i],16)
            @block.tensor
            def _(pe):
                pe.sem_inc(w_free,2)
                pe.wait_ge(consts,48)
                with pe.Fori(0,EXPERTS//2):
                    for i in range(2):
                        pe.wait_ge(x_loaded[i],16).then_inc(x_loaded[i],-16)
                        for k in range(KC):
                            for t in range(T4):
                                mm=pe.transpose(TX[:,k,128*t:128*t+128],xs[:,i,t,128*k:128*k+128],ident[:])
                            mm.then_inc(tx_full,1)
                        pe.wait_ge(w_loaded[i],32).then_inc(w_loaded[i],-32)
                        pe.wait_ge(xT_ready,2).then_inc(xT_ready,-2)
                        for c in range(FC):
                            if c>=2: pe.wait_ge(hT_ready,1).then_inc(hT_ready,-1)
                            for k in range(KC):
                                mm=pe.matmul(H[:,c%2,:],w1[:,i,k,128*c:128*c+128],xT[:,k,:],start=k==0,stop=k==KC-1)
                            mm.then_inc(h_full,1)
                        pe.wait_ge(hT_ready,2).then_inc(hT_ready,-2)
                        for t in range(T4):
                            for c in range(FC):
                                mm=pe.matmul(Y[:,t,0:DIM],hT[:,c,128*t:128*t+128],w2[:,i,c,:],start=c==0,stop=c==FC-1)
                            mm.then_inc(y_full,1)
            @block.scalar
            def _(act):
                nc.scalar.preload_act_table(ACT.Gelu_apprx_tanh)
                act.wait_ge(consts,48)
                for i in range(2): act.sem_inc(y_stored[i],16)
                with act.Fori(0,EXPERTS//2) as j:
                    for i in range(2):
                        for c in range(FC):
                            act.wait_ge(h_full,1).then_inc(h_full,-1)
                            nc.scalar.activation(hT[:,c,:],H[:,c%2,:],ACT.Gelu_apprx_tanh,bias=b1[:,bass.ds(j*2+i,1),c:c+1].rearrange("p o c -> p (o c)")).then_inc(hT_ready,1)
                        for t in range(T4):
                            act.wait_ge(y_ready,1).then_inc(y_ready,-1)
                            act.dma_start(ys_d[bass.ds((j*2+i)*CAP+t*128,128),:],y[:,t%2]).then_inc(y_stored[t%2],16)
            @block.vector
            def _(dve):
                with dve.Fori(0,EXPERTS//2) as j:
                    for i in range(2):
                        for k in range(KC):
                            dve.wait_ge(tx_full,1).then_inc(tx_full,-1)
                            nc.vector.tensor_copy(xT[:,k,:],TX[:,k,:]).then_inc(xT_ready,1)
                        for t in range(T4):
                            dve.wait_ge(y_full,1).then_inc(y_full,-1); dve.wait_ge(y_stored[t%2],16).then_inc(y_stored[t%2],-16)
                            nc.vector.tensor_tensor(y[:,t%2],Y[:,t,0:DIM],b2[:,bass.ds((j*2+i)*DIM,DIM)],ALU.add).then_inc(y_ready,1)
                        dve.sem_inc(w_free,1)
                for i in range(2): dve.wait_ge(y_stored[i],16)

def finish(nc,tag,x,f,pos,ys_d,out_d):
    with Mem(nc,tag) as m:
        R=8
        y=m.sb("y",[128,R,DIM]); o=m.sb("o",[128,R,DIM]); st=m.sb("st",[128,R,12]); fin=m.sb("fin",[128,R,DIM]); half=m.sb("half",[128,1])
        y_loaded=[m.sem(f"y_loaded{i}") for i in range(R)]; y_free=m.sem("y_free"); dve_done=m.sem("dve_done"); half_done=m.sem("half_done")
        var=m.sem("var"); rstd=m.sem("rstd"); fin_ready=m.sem("fin_ready"); stored=[m.sem(f"stored{i}") for i in range(R)]
        LAG=3
        with nc.Block() as block:
            @block.gpsimd
            def _(pool):
                nc.gpsimd.memset(half[:],-0.5).then_inc(half_done,1)
                pool.wait_ge(half_done,1)
                def gather(n):
                    if n>=R: pool.wait_ge(y_free,1).then_inc(y_free,-1)
                    nc.gpsimd.indirect_dma_start(out=y[:,n%R,:],out_offset=None,in_=ys_d,in_offset=bass.IndirectOffsetOnAxis(ap=pos[:,n:n+1],axis=0)).then_inc(y_loaded[n%R],16)
                def root(n):
                    pool.wait_ge(var,1).then_inc(var,-1)
                    nc.gpsimd.tensor_tensor(st[:,n%R,9:10],st[:,n%R,8:9],half[:],ALU.pow).then_inc(rstd,1)
                staged([gather,lambda n:None,lambda n:None,lambda n:None,root],NT)
            @block.vector
            def _(dve):
                def done(i):
                    i.then_inc(dve_done,1); dve.wait_ge(dve_done,1).then_inc(dve_done,-1)
                def add(n):
                    dve.wait_ge(y_loaded[n%R],16*(n//R+1))
                    done(nc.vector.tensor_tensor(o[:,n%R],y[:,n%R],f[:,n,:],ALU.add))
                    dve.sem_inc(y_free,1)
                    done(nc.vector.bn_stats(st[:,n%R,0:6],o[:,n%R]))
                    done(nc.vector.bn_aggr(st[:,n%R,6:8],st[:,n%R,0:6]))
                    nc.vector.tensor_scalar(st[:,n%R,8:9],st[:,n%R,7:8],LN_EPS,None,ALU.add).then_inc(var,1)
                def norm(n):
                    dve.wait_ge(rstd,1).then_inc(rstd,-1)
                    done(nc.vector.tensor_scalar(o[:,n%R],o[:,n%R],st[:,n%R,6:7],st[:,n%R,9:10],ALU.subtract,ALU.mult))
                    if n>=R: dve.wait_ge(stored[n%R],16).then_inc(stored[n%R],-16)
                    nc.vector.tensor_tensor(fin[:,n%R],o[:,n%R],x[:,n,:],ALU.add).then_inc(fin_ready,1)
                staged([add,lambda n:None,norm],NT)
                for i in range(R): dve.wait_ge(stored[i],16)
            @block.sync
            def _(sp):
                for n in range(NT):
                    sp.wait_ge(fin_ready,1).then_inc(fin_ready,-1)
                    sp.dma_start(out_d[n*128:n*128+128,:],fin[:,n%R]).then_inc(stored[n%R],16)

def two_layers(nc,out,x,w_qkv0,w_out0,norm_w,w_route,w1_0,w2_0,w_qkv1,b_qkv1,w_out1,b_out1,ln_g,ln_b,centroids,
               w1_1,w2_1,b1_1,b2_1,ident,prefix,order,starts,cands,positions,masks,zeros):
    def scratch(name,*shape): return nc.dram_tensor(name,shape,F32,kind="Internal").ap()
    qkv=scratch("qkv",BATCH*GROUPS,3,SEQ,4*HD); ao=scratch("ao",BATCH*GROUPS,SEQ,4*HD)
    x1=scratch("x1",TOK,DIM); x2=scratch("x2",TOK,DIM)
    sorted_in=scratch("sorted_in",SLOTS0*128,DIM); sorted_out=scratch("sorted_out",SLOTS0*128,DIM)
    ln_qkv(nc,"qkv0",x,w_qkv0,qkv,ident)
    attention(nc,"att0",qkv,ao,False,1.0/DIM**0.5,ident)
    with Mem(nc,"l0") as m:
        z=m.sb("z",[128,NT,DIM])
        attn_post(nc,"post0",ao,w_out0,x,ident,x_out=x1,z=z)
        with Mem(nc,"ffn0") as f:
            zn=f.sb("zn",[128,NT,DIM]); w1=f.sb("w1",[128,KC,EXPERTS*F0]); w2=f.sb("w2",[128,F0//128,EXPERTS*DIM])
            logits=f.sb("logits",[128,LG,NT]); slot=f.sb("slot",[128,2,NT],U32); weight=f.sb("weight",[128,2,NT]); tile_expert=f.sb("tile_expert",[128,SLOTS0],I32)
            for loop in range(2):
                first=loop==0
                rms_logits(nc,f"rms{loop}",z,zn,logits,norm_w,w_route,ident)
                route(nc,f"route{loop}",logits,prefix,order,starts,slot,weight,tile_expert,
                      prepare=(w1,w1_0,w2,w2_0,zeros,sorted_in) if first else None)
                experts(nc,f"experts{loop}",zn,slot,tile_expert,w1,w2,sorted_in,sorted_out,ident)
                combine(nc,f"combine{loop}",z,slot,weight,sorted_out)
        ln_qkv(nc,"qkv1",x1,w_qkv1,qkv,ident,bias_d=b_qkv1,z=z,x_out=x2)
    attention(nc,"att1",qkv,ao,True,1.0/HD**0.5,ident,positions,masks)
    with Mem(nc,"l1") as m:
        x3=m.sb("x3",[128,NT,DIM]); f=m.sb("f",[128,NT,DIM]); norm=m.sb("norm",[128,NT,DIM])
        scores=m.sb("scores",[128,EXPERTS,NT]); pos=m.sb("pos",[128,NT],U32)
        attn_post(nc,"post1",ao,w_out1,x2,ident,z=x3,bias_d=b_out1,g_d=ln_g,b_d=ln_b,cent_d=centroids,f=f,norm=norm,scores=scores)
        assign(nc,"assign",scores,prefix,cands,pos)
        experts1(nc,"ffn1",norm,pos,w1_1,w2_1,b1_1,b2_1,sorted_in,sorted_out,ident)
        finish(nc,"finish",x3,f,pos,sorted_out,out)

def twelve_bits(x):
    bits=np.asarray(x,np.float32).view(np.uint32).astype(np.uint64)
    return ((bits+0x800)&0xFFFFF000).astype(np.uint32).view(np.float32)

def position_columns():
    start=2.0**(-8.0/HEADS)
    slopes=4*np.array([start*start**i for i in range(HEADS)],dtype=np.float32)
    high=twelve_bits(slopes); low=slopes-high
    table=np.zeros((128,2,2*GROUPS,TILES,2,AUG),np.float32)
    place=(np.arange(TILES)[None,:]*128+np.arange(128)[:,None]).astype(np.float32)
    for pair in range(2*GROUPS):
        for h in range(2):
            head=pair*2+h
            for col,value in ((1,high[head]),(2,-place),(3,low[head]),(4,-place)):
                table[:,0,pair,:,h,col]=value
            for col,value in ((0,-1.0),(1,place),(2,high[head]),(3,place),(4,low[head])):
                table[:,1,pair,:,h,col]=value
    return table.reshape(128,2,2*GROUPS,TILES*2*AUG)

def causal_masks():
    row=np.arange(128)[:,None]; col=np.arange(128)[None,:]
    t=np.zeros((128,4,128),np.float32)
    t[:,0]=row==col; t[:,1]=np.where(col>row,-1e30,0); t[:,2]=-1e30; t[:,3]=np.where(col<row,-1e30,0)
    return t.reshape(128,512)

def prefix_and_ones():
    p=np.arange(128)
    t=np.ones((128,2,128),np.float32); t[:,0]=p[:,None]<p[None,:]
    return t

def group_order():
    return np.broadcast_to((2*GR-np.arange(GR,dtype=np.float32))[None,:,None],(128,GR,NT))

def slot_starts():
    return np.broadcast_to((np.arange(SLOTS0)*128).astype(np.float32),(128,EXPERTS,SLOTS0))

def candidate_bits():
    t=np.array([[j<<(32-BITS*(l+1)) for j in range(1,CANDS+1)] for l in range(LEVELS)],np.int64)
    return np.broadcast_to(t.astype(np.uint32).view(np.int32),(128,LEVELS,CANDS))

def by_group(w):
    return w.reshape(-1,3,GROUPS,4*HD).transpose(0,2,1,3).reshape(w.shape[0],3*DIM)


def kernel(**inputs):
    import concourse.bacc as _bacc
    from concourse.bass_utils import run_bass_kernel_spmd as _run
    a={n:np.asarray(v) for n,v in inputs.items()}
    att=lambda n: a["L1_attn_"+n]
    ffn=lambda n: a["L1_ffn_"+n]
    laid=dict(
        x=a["L0_attn_x"].reshape(TOK,DIM), w_qkv0=by_group(a["L0_attn_w_qkv"]), w_out0=a["L0_attn_w_out"],
        norm_w=a["L0_ffn_norm_w"], w_route=np.concatenate([a["L0_ffn_w_macro"],a["L0_ffn_w_micro"].reshape(EXPERTS,DIM)]).T,
        w1_0=a["L0_ffn_w1"].transpose(2,0,1).reshape(DIM,EXPERTS*F0), w2_0=a["L0_ffn_w2"].transpose(2,0,1).reshape(F0,EXPERTS*DIM),
        w_qkv1=by_group(np.concatenate([att("q_w").T,att("k_w").T,att("v_w").T],axis=1)),
        b_qkv1=by_group(np.concatenate([att("q_b"),att("k_b"),att("v_b")])[None])[0],
        w_out1=att("o_w").T, b_out1=att("o_b"), ln_g=ffn("ln_g"), ln_b=ffn("ln_b"), centroids=ffn("centroids").T,
        w1_1=ffn("w1"), w2_1=ffn("w2"), b1_1=ffn("b1").reshape(EXPERTS,F1//128,128).transpose(2,0,1), b2_1=ffn("b2").reshape(EXPERTS*DIM),
        ident=np.eye(128,dtype=np.float32), prefix=prefix_and_ones(), order=group_order(), starts=slot_starts(),
        cands=candidate_bits(), positions=position_columns(), masks=causal_masks(), zeros=np.zeros((128,2048),np.float32))
    nc=_bacc.Bacc("TRN2",target_bir_lowering=False,num_devices=1)
    arrays,aps={},{}
    for name,value in laid.items():
        value=np.ascontiguousarray(value)
        arrays["in_"+name]=value
        aps[name]=nc.dram_tensor("in_"+name,value.shape,mybir.dt.from_np(value.dtype),kind="ExternalInput").ap()
    out=nc.dram_tensor("out",(TOK,DIM),F32,kind="ExternalOutput").ap()
    two_layers(nc,out,**aps)
    result=_run(nc,[arrays],core_ids=[0])
    return result.results[0]["out"].reshape(BATCH,SEQ,DIM)
```

```python
from contextlib import ExitStack
import numpy as np
import concourse.bass as bass
from concourse import mybir
F32=mybir.dt.float32; F32R=mybir.dt.float32r; BF=mybir.dt.bfloat16; I32=mybir.dt.int32; U32=mybir.dt.uint32
ALU=mybir.AluOpType; ACT=mybir.ActivationFunctionType; AX=mybir.AxisListType
BATCH,SEQ,DIM,HEADS,HD=4,1024,256,16,16
TILES=SEQ//128
GROUPS=4
AUG=5
WIDE=64

class Mem:
    def __init__(self,nc,tag):
        self.nc,self.tag,self.ctx,self.sems=nc,tag,ExitStack(),[]
    def __enter__(self): return self
    def __exit__(self,*a):
        self.ctx.close()
        if self.sems:
            self.nc.clear_and_free_semaphores(self.sems)
            self.nc.all_engine_barrier()
    def sb(self,n,s,d=F32): return self.ctx.enter_context(self.nc.sbuf_tensor(f"{self.tag}_{n}",s,d))
    def ps(self,n,s,d=F32): return self.ctx.enter_context(self.nc.psum_tensor(f"{self.tag}_{n}",s,d))
    def sem(self,n):
        s=self.nc.alloc_semaphore(name=f"{self.tag}_{n}")
        self.sems.append(s)
        return s

def attention(nc, tag, qkv, ao, causal, exp_scale, ident_d, aug_d=None, masks_d=None):
    with Mem(nc,tag) as m:
        sb,ps,sem=m.sb,m.ps,m.sem
        ident=sb("ident",[128,128])
        raw=sb("raw",[128,3,TILES,64])
        qn=sb("qn",[128,TILES,2,WIDE]); kn=sb("kn",[128,TILES,2,WIDE])
        hiR=sb("hiR",[128,2,TILES,2,HD],F32R)
        vn=sb("vn",[128,2,TILES,2,32])
        qT=sb("qT",[128,2,SEQ],F32R)
        kT=sb("kT",[128,2,2,SEQ],F32R)
        pr=sb("pr",[128,4,2,512])
        ot=sb("ot",[128,512])
        mparts=sb("mparts",[128,2,TILES,2]); m16=sb("m16",[128,2*TILES]); mT=sb("mT",[2*TILES,128],F32R)
        osum=sb("osum",[128,4,2,HD+1]); rcp=sb("rcp",[128,4,2,1]); aon=sb("aon",[128,TILES,4,HD])
        if causal:
            augt=sb("augt",[128,2,2*GROUPS,TILES*2*AUG])
            maskf=sb("maskf",[128,128+128+256])
            maskr=sb("maskr",[128,128+128+256],F32R)
        S1=ps("S1",[128,3,512]); S2=ps("S2",[128,3,512]); OP=ps("OP",[128,512]); TP=ps("TP",[128,512])
        consts=sem("consts"); qk_loaded=sem("qk_loaded"); qk_free=sem("qk_free"); rv_loaded=sem("rv_loaded"); rv_free=sem("rv_free")
        nat_ready=sem("nat_ready"); nat_free=sem("nat_free"); v_ready=[sem("v_ready0"),sem("v_ready1")]; v_free=[sem("v_free0"),sem("v_free1")]
        pool_done=sem("pool_done"); dve_done=sem("dve_done"); zeros_done=sem("zeros_done")
        t_dve=sem("t_dve"); t_free=sem("t_free")
        s1_full=sem("s1_full"); t_act=sem("t_act"); half_ready=sem("half_ready"); o_step=sem("o_step"); copied=sem("copied"); s1_free=sem("s1_free"); m_ready=sem("m_ready"); mT_ready=sem("mT_ready"); m_placed=sem("m_placed")
        s2_full=sem("s2_full"); s2_free=sem("s2_free")
        o_full=sem("o_full"); ot_ready=sem("ot_ready"); ao_ready=sem("ao_ready"); ao_stored=sem("ao_stored")

        steps=[(c,kt) for c in range(2) for kt in range(4*(c+1) if causal else TILES)]
        def first_col(c,kt):
            return 0 if (not causal or kt<2) else max(0,kt*128-c*512)
        def width(qt,half):
            return 512 if not causal else min(512,(qt+1)*128-half*512)
        maxes=[(qt,heads,half) for q0,half in ((0,0),(4,0),(0,1),(4,1)) for qt in range(q0,q0+4) if width(qt,half)>0
               for heads in (((0,1),) if width(qt,half)<=256 else ((0,),(1,)))]
        EARLY=len([1 for qt,_,half in maxes if qt<4 and half==0])
        NS=len(steps)
        CYCLES=NS//2
        per=(len(maxes)-8)//(CYCLES-2)
        share=[maxes[:8]]+[maxes[8+per*c:8+per*(c+1)] for c in range(CYCLES-1)]
        BANKS=3
        assert (len(maxes)+1)%BANKS==0
        CHUNK0=(4 if causal else TILES)//2
        last_groups=(CHUNK0-1,CYCLES-1)

        with nc.Block() as block:
            @block.sync
            def _(sp):
                sp.dma_start(ident[:],ident_d).then_inc(consts,16)
                if causal:
                    sp.dma_start(augt[:],aug_d).then_inc(consts,16)
                    sp.dma_start(maskf[:],masks_d).then_inc(consts,16)
                def load(bg):
                    sp.wait_ge(qk_free,1).then_inc(qk_free,-1)
                    for m in range(2):
                        sp.dma_start(raw[:,m],qkv[bg][0,m].rearrange("(t p) c -> p t c",p=128)).then_inc(qk_loaded,16)
                    sp.wait_ge(rv_free,1).then_inc(rv_free,-1)
                    sp.dma_start(raw[:,2],qkv[bg][0,2].rearrange("(t p) c -> p t c",p=128)).then_inc(rv_loaded,16)
                def place():
                    sp.wait_ge(mT_ready,1).then_inc(mT_ready,-1)
                    for h in range(2):
                        sp.dma_start(qT[64*h:64*h+1,place.s,:].bitcast(F32).rearrange("o (t q) -> o t q",t=TILES),
                                     mT[TILES*h:TILES*h+TILES,:].bitcast(F32)).then_inc(m_placed,16)
                load(bass.ds(0,1))
                place.s=0; place()
                def store(bg):
                    sp.wait_ge(ao_ready,1).then_inc(ao_ready,-1)
                    sp.dma_start(ao[bass.ds(bg,1)][0].rearrange("(t p) c -> p t c",p=128),aon[:].rearrange("p t h d -> p t (h d)")).then_inc(ao_stored,16)
                def loop_body(bg,first,last):
                    if not last: load(bass.ds(bg+1,1))
                    if not first: store(bg-1)
                    place.s=1; place()
                    if not last:
                        place.s=0; place()
                loop_body(0,True,False)
                with sp.Fori(1,BATCH*GROUPS-1) as bg:
                    loop_body(bg,False,False)
                loop_body(BATCH*GROUPS-1,False,True)
                store(BATCH*GROUPS-1)
                sp.wait_ge(ao_stored,16)

            @block.gpsimd
            def _(pool):
                nc.gpsimd.memset(qn[:],0.0).then_inc(pool_done,1)
                nc.gpsimd.memset(kn[:],0.0).then_inc(pool_done,1)
                nc.gpsimd.memset(vn[:],0.0).then_inc(pool_done,1)
                pool.wait_ge(pool_done,3).then_inc(pool_done,-3)
                nc.gpsimd.memset(kn[:,:,:,0:1],-1.0).then_inc(pool_done,1)
                nc.gpsimd.memset(vn[:,:,:,:,HD:HD+1],1.0).then_inc(pool_done,1)
                pool.wait_ge(pool_done,2).then_inc(pool_done,-2)
                pool.sem_inc(qk_free,1); pool.sem_inc(rv_free,1)
                if causal: pool.wait_ge(consts,48)
                def natural(pair,first=False):
                    s=pair[1]
                    pool.wait_ge(nat_free,1).then_inc(nat_free,-1)
                    for m in range(2):
                        r=raw[:,m,:,32*s:32*s+32].rearrange("p t (h d) -> p t h d",h=2)
                        nc.gpsimd.tensor_copy(hiR[:,m],r).then_inc(pool_done,1)
                    if causal:
                        for m,n in ((0,qn),(1,kn)):
                            src=augt[:,m,pair[0],:]
                            nc.gpsimd.tensor_copy(n[:,:,:,0:AUG],src.rearrange("p (t h a) -> p t h a",t=TILES,h=2)).then_inc(pool_done,1)
                    pool.wait_ge(pool_done,4 if causal else 2).then_inc(pool_done,-(4 if causal else 2))
                    A,B,C=AUG,AUG+HD,AUG+2*HD
                    for m,n,his,lo in ((0,qn,(A,B),C),(1,kn,(A,C),B)):
                        r=raw[:,m,:,32*s:32*s+32].rearrange("p t (h d) -> p t h d",h=2)
                        hi=hiR[:,m].bitcast(F32)
                        for at in his:
                            nc.gpsimd.tensor_copy(n[:,:,:,at:at+HD],hi).then_inc(pool_done,1)
                        nc.gpsimd.tensor_tensor(n[:,:,:,lo:lo+HD],r,hi,ALU.subtract).then_inc(pool_done,1)
                    pool.wait_ge(pool_done,6).then_inc(pool_done,-6)
                    pool.sem_inc(nat_ready,1)
                def values(s):
                    pool.wait_ge(v_free[s],1).then_inc(v_free[s],-1)
                    nc.gpsimd.tensor_copy(vn[:,s,:,:,0:HD],raw[:,2,:,32*s:32*s+32].rearrange("p t (h d) -> p t h d",h=2)).then_inc(v_ready[s],1)
                def group(g):
                    pool.wait_ge(qk_loaded,32).then_inc(qk_loaded,-32)
                    natural((2*g,0))
                    pool.wait_ge(rv_loaded,16).then_inc(rv_loaded,-16)
                    values(0)
                    natural((2*g+1,1))
                    pool.sem_inc(qk_free,1)
                def body(g):
                    values(1)
                    pool.drain().then_inc(rv_free,1)
                    group(g)
                group(0)
                nb=BATCH*GROUPS
                if causal:
                    body(1); body(2); body(3)
                    with pool.Fori(1,BATCH):
                        for g in range(GROUPS): body(g)
                    values(1)
                else:
                    with pool.Fori(1,nb):
                        body(0)
                    values(1)

            @block.tensor
            def _(pe):
                pe.sem_inc(nat_free,1); pe.sem_inc(v_free[0],1); pe.sem_inc(v_free[1],1)
                pe.wait_ge(consts,48 if causal else 16)
                if causal: pe.wait_ge(zeros_done,1).then_inc(zeros_done,-1)
                def fill(f,half):
                    if f==0 and half==0: pe.wait_ge(nat_ready,1).then_inc(nat_ready,-1)
                    pe.wait_ge(t_free,1).then_inc(t_free,-1)
                    for t in range(4):
                        mm=pe.transpose(TP[:,128*t:128*t+128],(kn,qn)[f][:,4*half+t].rearrange("p h w -> p (h w)"),ident[:])
                    mm.then_inc(t_act,1)
                def pass1(s,mx):
                    qt,heads,half=mx
                    x=maxes.index(mx); b=x%BANKS
                    if x==0: pe.wait_ge(half_ready,2).then_inc(half_ready,-2)
                    if x==EARLY:
                        pe.wait_ge(half_ready,2).then_inc(half_ready,-2); pe.sem_inc(nat_free,1)
                    pe.wait_ge(s1_free,1).then_inc(s1_free,-1)
                    n=width(qt,half)
                    diag=causal and qt//4==half
                    for i,h in enumerate(heads):
                        mm=pe.matmul(S1[:,b,n*i:n*i+n],qT[:,s,qt*128:qt*128+128],kT[:,s,h,half*512:half*512+n],start=True,stop=not diag)
                        if diag:
                            mm=pe.matmul(S1[:,b,n*i+n-128:n*i+n],maskr[:,0:128],maskr[:,128:256],start=False,stop=True)
                    mm.then_inc(s1_full,1)
                def qk(s,n,h):
                    c,kt=steps[n]
                    b=(2*n+h)%3
                    if n==0 and h==0:
                        pe.wait_ge(m_placed,32).then_inc(m_placed,-32)
                        pe.wait_ge(s2_free,3).then_inc(s2_free,-3); pe.sem_inc(s2_free,2)
                    else: pe.wait_ge(s2_free,1).then_inc(s2_free,-1)
                    f=first_col(c,kt)
                    diag=causal and kt*128>=c*512
                    mm=pe.matmul(S2[:,b,f:512],kT[:,s,h,kt*128:kt*128+128],qT[:,s,c*512+f:c*512+512],start=True,stop=not diag)
                    if diag:
                        e=kt*128-c*512+128
                        w=e-f
                        mm=pe.matmul(S2[:,b,f:e],maskr[:,0:128],maskr[:,512-w:512],start=False,stop=True)
                    mm.then_inc(s2_full,1)
                def pv(s,g):
                    if g==CYCLES-1:
                        pe.wait_ge(s2_free,3).then_inc(s2_free,-3); pe.sem_inc(s2_free,3)
                    if g==0: pe.wait_ge(v_ready[s],1).then_inc(v_ready[s],-1)
                    for h in range(2):
                        for x in range(2):
                            n=2*g+x; c,kt=steps[n]; f=first_col(c,kt); j=2*h+x
                            mm=pe.matmul(OP[32*j:32*j+32,f:512],vn[:,s,kt,h,:],pr[:,n%4,h,f:512],start=kt<2,stop=g in last_groups,skip_group_check=True)
                    if g in last_groups: mm.then_inc(o_full,1)
                def finish(free_v=None):
                    pe.wait_ge(ot_ready,1).then_inc(ot_ready,-1)
                    if free_v is not None: pe.sem_inc(v_free[free_v],1)
                    pe.wait_ge(t_free,1).then_inc(t_free,-1)
                    for t in range(4):
                        mm=pe.transpose(TP[:,128*t:128*t+128],ot[:,128*t:128*t+128],ident[:])
                    mm.then_inc(t_dve,1)
                def mtrans():
                    pe.wait_ge(m_ready,1).then_inc(m_ready,-1); pe.wait_ge(s1_free,1).then_inc(s1_free,-1)
                    pe.transpose(S1[0:2*TILES,len(maxes)%BANKS,0:128],m16[:],ident[:]).then_inc(s1_full,1)
                def slot(p2,p1,prev,more):
                    maxima=share[0] if p1 is not None else []
                    if p1 is not None: fill(0,1)
                    for mx in maxima[:2]: pass1(p1,mx)
                    if prev is not None: pv(prev,CYCLES-1)
                    for mx in maxima[2:3]: pass1(p1,mx)
                    if p1 is not None: fill(1,1)
                    for mx in maxima[3:4]: pass1(p1,mx)
                    if prev is not None: finish(free_v=prev)
                    for c in range(CYCLES):
                        if p1 is not None: maxima=share[c] if c else share[0][4:]
                        for x in range(4):
                            if x==2 and c==CYCLES-2 and more: fill(0,0)
                            if x==0 and c==CYCLES-1 and more: fill(1,0)
                            for mx in maxima[x:x+1]: pass1(p1,mx)
                            if p2 is not None: qk(p2,2*c+x//2,x%2)
                        if p2 is not None and c==CHUNK0+1: finish()
                        if p2 is not None and c>=1: pv(p2,c-1)
                        if c==CYCLES-1 and p1 is not None: mtrans()
                fill(0,0); fill(1,0)
                slot(None,0,None,True)
                slot(0,1,None,True); slot(1,0,0,True)
                with pe.Fori(1,BATCH*GROUPS-1):
                    slot(0,1,1,True); slot(1,0,0,True)
                slot(0,1,1,False); slot(1,None,0,False)
                pv(1,CYCLES-1)
                finish()

            @block.scalar
            def _(act):
                nc.scalar.preload_act_table(ACT.Exp)
                act.sem_inc(s2_free,3)
                def evac(s,f,half):
                    act.wait_ge(t_act,1).then_inc(t_act,-1)
                    cols=slice(half*512,half*512+512)
                    if f==0:
                        for h in range(2):
                            x=nc.scalar.activation(kT[64*h:64*h+64,s,h,cols],TP[64*h:64*h+64,:],ACT.Copy)
                    else:
                        x=nc.scalar.activation(qT[:,s,cols],TP[:],ACT.Copy)
                    x.then_inc(copied,1)
                    act.wait_ge(copied,1).then_inc(copied,-1)
                    act.sem_inc(t_free,1); act.sem_inc(half_ready,1)
                def exp(n):
                    c,kt=steps[n]; f=first_col(c,kt)
                    for h in range(2):
                        act.wait_ge(s2_full,1).then_inc(s2_full,-1)
                        nc.scalar.activation(pr[:,n%4,h,f:512],S2[:,(2*n+h)%3,f:512],ACT.Exp,scale=exp_scale).then_inc(s2_free,1)
                def slot(p2,p1,more):
                    if p1 is not None:
                        evac(p1,0,1); evac(p1,1,1)
                    for n in range(NS):
                        if p2 is not None: exp(n)
                        if more and n in (NS-4,NS-3): evac(1 if p2 is None else p2,n-NS+4,0)
                evac(0,0,0); evac(0,1,0)
                slot(None,0,True)
                slot(0,1,True); slot(1,0,True)
                with act.Fori(1,BATCH*GROUPS-1):
                    slot(0,1,True); slot(1,0,True)
                slot(0,1,False); slot(1,None,False)

            @block.vector
            def _(dve):
                nc.vector.memset(kT[64:128,:,0,:].bitcast(F32),0.0).then_inc(dve_done,1)
                nc.vector.memset(kT[0:64,:,1,:].bitcast(F32),0.0).then_inc(dve_done,1)
                nc.vector.memset(mparts[:],-3.0e38).then_inc(dve_done,1)
                dve.wait_ge(dve_done,3).then_inc(dve_done,-3)
                if causal:
                    dve.wait_ge(consts,48)
                    nc.vector.tensor_copy(maskr[:],maskf[:]).then_inc(zeros_done,1)
                dve.sem_inc(t_free,1); dve.sem_inc(s1_free,3)
                def rowmax(mx):
                    qt,heads,half=mx
                    b=maxes.index(mx)%BANKS
                    n=width(qt,half)
                    dve.wait_ge(s1_full,1).then_inc(s1_full,-1)
                    nc.vector.tensor_reduce(mparts[:,heads[0]:heads[-1]+1,qt,half],S1[:,b,0:len(heads)*n].rearrange("p (h n) -> p h n",n=n),AX.X,ALU.max).then_inc(s1_free,1)
                def evac_o():
                    dve.wait_ge(o_full,1).then_inc(o_full,-1)
                    nc.vector.tensor_copy(ot[:],OP[:]).then_inc(ot_ready,1)
                def finish(s,c):
                    def add():
                        if s==0 and c==0: dve.wait_ge(ao_stored,16).then_inc(ao_stored,-16)
                        dve.wait_ge(t_dve,1).then_inc(t_dve,-1)
                        o4=TP[:].rearrange("p (t h x d) -> p t h x d",t=4,h=2,x=2)
                        nc.vector.tensor_reduce(osum[:],o4[:,:,:,:,0:HD+1].rearrange("p t h x d -> p t h d x"),AX.X,ALU.add).then_inc(o_step,1)
                    def invert():
                        dve.wait_ge(o_step,1).then_inc(o_step,-1)
                        dve.sem_inc(t_free,1)
                        nc.vector.reciprocal(rcp[:],osum[:,:,:,HD:HD+1]).then_inc(o_step,1)
                    def scale():
                        dve.wait_ge(o_step,1).then_inc(o_step,-1)
                        x=nc.vector.tensor_tensor(aon[:,4*c:4*c+4,2*s:2*s+2,:],osum[:,:,:,0:HD],rcp[:].broadcast_to([128,4,2,HD]),ALU.mult)
                        x.then_inc(ao_ready if (s==1 and c==1) else o_step,1)
                        if not (s==1 and c==1): dve.wait_ge(o_step,1).then_inc(o_step,-1)
                    return [add,invert,scale]
                def mfinal():
                    dve.drain().then_inc(dve_done,1)
                    dve.wait_ge(dve_done,1).then_inc(dve_done,-1)
                    nc.vector.tensor_reduce(m16[:].rearrange("p (h t) -> p h t",h=2),mparts[:],AX.X,ALU.max).then_inc(m_ready,1)
                def mcopy():
                    dve.wait_ge(s1_full,1).then_inc(s1_full,-1)
                    nc.vector.tensor_copy(mT[:],S1[0:2*TILES,len(maxes)%BANKS,0:128]).then_inc(dve_done,1)
                    dve.wait_ge(dve_done,1).then_inc(dve_done,-1)
                    dve.sem_inc(mT_ready,1); dve.sem_inc(s1_free,1)
                def slot(p2,p1,prev):
                    maxima=share[0] if p1 is not None else []
                    for mx in maxima[:2]: rowmax(mx)
                    if prev is not None: evac_o()
                    for mx in maxima[2:4]: rowmax(mx)
                    between=[]
                    if prev is not None: between+=finish(prev,1)
                    for c in range(CYCLES):
                        if p1 is not None: maxima=share[c] if c else share[0][4:]
                        for x in range(4):
                            if c==CHUNK0+2 and x==0 and p2 is not None: between+=finish(p2,0)
                            if between: between.pop(0)()
                            for mx in maxima[x:x+1]: rowmax(mx)
                            if x==0 and p2 is not None and c==CHUNK0+1: evac_o()
                    if p1 is not None:
                        mfinal(); mcopy()
                dve.sem_inc(ao_stored,16)
                slot(None,0,None)
                slot(0,1,None); slot(1,0,0)
                with dve.Fori(1,BATCH*GROUPS-1):
                    slot(0,1,1); slot(1,0,0)
                slot(0,1,1); slot(1,None,0)
                evac_o()
                for step in finish(1,1): step()

TOK=BATCH*SEQ
NT=TOK//128
KC=DIM//128
EXPERTS=8
F0=512
SLOTS0=NT*2+EXPERTS
F1=1024
CAP=TOK//EXPERTS
RMS_EPS=1e-6; LN_EPS=1e-5; EPS=1e-9

def staged(stages,count):
    for n in range(count+len(stages)-1):
        for k in reversed(range(len(stages))):
            if 0<=n-k<count: stages[k](n-k)

def pipelined(eng,stages,order=None):
    def beside(b,u,here):
        for k,stage in enumerate(stages):
            if stage is not None and here(u-k):
                stage(b,u-k) if u>=k else stage(b-1,u-k+TILES)
    for u in range(TILES): beside(0,u,lambda n: n>=0)
    with eng.Fori(1,BATCH) as b:
        for u in range(TILES): beside(b,u,lambda n: True)
    for u in range(len(stages)-1): beside(BATCH,u,lambda n: n<0)

def rows_of(ap,b,u):
    return ap[bass.ds(b*SEQ+u*128,128),:]

def ln_qkv(nc,tag,src,w_d,qkv,ident_d,bias_d=None,z=None,x_out=None):
    W=3*DIM
    with Mem(nc,tag) as m:
        ident=m.sb("ident",[128,128]); w=m.sb("w",[128,KC,W]); half=m.sb("half",[128,1])
        bias=m.sb("bias",[128,W]) if bias_d is not None else None
        R=4
        xt=m.sb("xt",[128,R,DIM]); st=m.sb("st",[128,R,12]); xn=m.sb("xn",[128,2,DIM]); xT=m.sb("xT",[128,2,DIM]); y=m.sb("y",[128,2,W])
        st2=m.sb("st2",[128,R,12]); x2=m.sb("x2",[128,R,DIM]); tmp=m.sb("tmp",[128,R,DIM])
        T=m.ps("T",[128,2,512]); Y=m.ps("Y",[128,2,1024])
        consts=m.sem("consts"); half_done=m.sem("half_done")
        x_loaded=[m.sem(f"x_loaded{i}") for i in range(R)]; x_free=m.sem("x_free")
        dve_done=m.sem("dve_done"); var_ready=m.sem("var_ready"); rstd_ready=m.sem("rstd_ready"); var2_ready=m.sem("var2_ready"); rstd2_ready=m.sem("rstd2_ready")
        xn_ready=m.sem("xn_ready"); xn_free=m.sem("xn_free"); t_full=m.sem("t_full"); xT_ready=m.sem("xT_ready")
        y_full=m.sem("y_full"); y_copied=m.sem("y_copied"); y_free=m.sem("y_free"); y_store=m.sem("y_store")
        stored=[m.sem(f"stored{i}") for i in range(2)]
        xs_ready=m.sem("xs_ready"); xs_stored=[m.sem(f"xs_stored{i}") for i in range(R)]
        xs=x2 if z is not None else xt
        with nc.Block() as block:
            @block.sync
            def _(sp):
                sp.dma_start(ident[:],ident_d).then_inc(consts,16)
                sp.dma_start(w[:],w_d.rearrange("(k p) n -> p k n",p=128)).then_inc(consts,16)
                if bias is not None: sp.dma_start(bias[:],bias_d.partition_broadcast(128)).then_inc(consts,16)
                def load(b,u):
                    sp.wait_ge(x_free,1).then_inc(x_free,-1)
                    sp.dma_start(xt[:,u%R],rows_of(src,b,u)).then_inc(x_loaded[u%R],16)
                def keep(b,u):
                    sp.wait_ge(xs_ready,1).then_inc(xs_ready,-1)
                    sp.dma_start(rows_of(x_out,b,u),x2[:,u%R]).then_inc(xs_stored[u%R],16)
                pipelined(sp,[load,None,None,None,keep] if z is not None else [load])
            @block.gpsimd
            def _(pool):
                nc.gpsimd.memset(half[:],-0.5).then_inc(half_done,1)
                pool.wait_ge(half_done,1)
                def r1(b,u):
                    pool.wait_ge(var_ready,1).then_inc(var_ready,-1)
                    nc.gpsimd.tensor_tensor(st[:,u%R,9:10],st[:,u%R,8:9],half[:],ALU.pow).then_inc(rstd_ready,1)
                def r2(b,u):
                    pool.wait_ge(var2_ready,1).then_inc(var2_ready,-1)
                    nc.gpsimd.tensor_tensor(st2[:,u%R,9:10],st2[:,u%R,8:9],half[:],ALU.pow).then_inc(rstd2_ready,1)
                pipelined(pool,[r2,r1] if z is not None else [r1])
            @block.vector
            def _(dve):
                def done(i):
                    i.then_inc(dve_done,1); dve.wait_ge(dve_done,1).then_inc(dve_done,-1)
                def stats(x,s,out):
                    done(nc.vector.bn_stats(s[:,0:6],x))
                    done(nc.vector.bn_aggr(s[:,6:8],s[:,0:6]))
                    nc.vector.tensor_scalar(s[:,8:9],s[:,7:8],LN_EPS,None,ALU.add).then_inc(out,1)
                if bias is not None: dve.wait_ge(consts,48)
                def z_stats(b,u):
                    stats(z[:,bass.ds(b*TILES+u,1),:].rearrange("p o d -> p (o d)"),st2[:,u%R],var2_ready)
                def x_new(b,u):
                    dve.wait_ge(rstd2_ready,1).then_inc(rstd2_ready,-1)
                    done(nc.vector.tensor_scalar(tmp[:,u%R],z[:,bass.ds(b*TILES+u,1),:].rearrange("p o d -> p (o d)"),st2[:,u%R,6:7],st2[:,u%R,9:10],ALU.subtract,ALU.mult))
                    dve.wait_ge(x_loaded[u%R],16).then_inc(x_loaded[u%R],-16)
                    dve.wait_ge(xs_stored[u%R],16).then_inc(xs_stored[u%R],-16)
                    done(nc.vector.tensor_tensor(x2[:,u%R],tmp[:,u%R],xt[:,u%R],ALU.add))
                    dve.sem_inc(xs_ready,1); dve.sem_inc(x_free,1)
                    stats(x2[:,u%R],st[:,u%R],var_ready)
                def x_stats(b,u):
                    dve.wait_ge(x_loaded[u%R],16).then_inc(x_loaded[u%R],-16)
                    stats(xt[:,u%R],st[:,u%R],var_ready)
                def normal(b,u):
                    dve.wait_ge(rstd_ready,1).then_inc(rstd_ready,-1); dve.wait_ge(xn_free,1).then_inc(xn_free,-1)
                    done(nc.vector.tensor_scalar(xn[:,u%2],xs[:,u%R],st[:,u%R,6:7],st[:,u%R,9:10],ALU.subtract,ALU.mult))
                    dve.sem_inc(xn_ready,1)
                    if z is None: dve.sem_inc(x_free,1)
                def y_out(b,u):
                    if bias is None: return
                    dve.wait_ge(y_full,1).then_inc(y_full,-1); dve.wait_ge(stored[u%2],16).then_inc(stored[u%2],-16)
                    nc.vector.tensor_tensor(y[:,u%2],Y[:,u%2,0:W],bias[:],ALU.add).then_inc(y_copied,1)
                pipelined(dve,([z_stats,x_new] if z is not None else [x_stats])+[normal,None,y_out])
                if bias is not None:
                    for i in range(2): dve.wait_ge(stored[i],16)
                if z is not None:
                    for i in range(R): dve.wait_ge(xs_stored[i],16)
            @block.tensor
            def _(pe):
                pe.sem_inc(xn_free,2); pe.sem_inc(x_free,R); pe.sem_inc(y_free,2)
                pe.wait_ge(consts,48 if bias is not None else 32)
                def turn(b,u):
                    pe.wait_ge(xn_ready,1).then_inc(xn_ready,-1)
                    for k in range(KC):
                        mm=pe.transpose(T[:,u%2,128*k:128*k+128],xn[:,u%2,128*k:128*k+128],ident[:])
                    mm.then_inc(t_full,1)
                def product(b,u):
                    pe.wait_ge(xT_ready,1).then_inc(xT_ready,-1)
                    pe.sem_inc(xn_free,1)
                    pe.wait_ge(y_free,1).then_inc(y_free,-1)
                    for n0,n1 in ((0,512),(512,W)):
                        for k in range(KC):
                            mm=pe.matmul(Y[:,u%2,n0:n1],xT[:,u%2,128*k:128*k+128],w[:,k,n0:n1],start=k==0,stop=k==KC-1)
                    mm.then_inc(y_full,1)
                pipelined(pe,[turn,product])
            @block.scalar
            def _(act):
                nc.scalar.preload_act_table(ACT.Exp)
                for i in range(2): act.sem_inc(stored[i],16)
                if z is not None:
                    for i in range(R): act.sem_inc(xs_stored[i],16)
                def turned(b,u):
                    act.wait_ge(t_full,1).then_inc(t_full,-1)
                    nc.scalar.activation(xT[:,u%2],T[:,u%2,0:DIM],ACT.Copy).then_inc(xT_ready,1)
                def y_out(b,u):
                    if bias is None:
                        act.wait_ge(y_full,1).then_inc(y_full,-1); act.wait_ge(stored[u%2],16).then_inc(stored[u%2],-16)
                        nc.scalar.activation(y[:,u%2],Y[:,u%2,0:W],ACT.Copy).then_inc(y_copied,1)
                    act.wait_ge(y_copied,1).then_inc(y_copied,-1)
                    act.sem_inc(y_free,1)
                    act.dma_start(qkv[bass.ds(b*GROUPS,GROUPS)][:,:,u*128:u*128+128,:].rearrange("g m p c -> p (g m) c"),
                                  y[:,u%2].rearrange("p (a c) -> p a c",c=64)).then_inc(stored[u%2],16)
                pipelined(act,[turned,y_out])
                if bias is None:
                    for i in range(2): act.wait_ge(stored[i],16)

def attn_post(nc,tag,ao,w_d,x_in,ident_d,x_out=None,z=None,bias_d=None,g_d=None,b_d=None,cent_d=None,f=None,norm=None,scores=None):
    last=bias_d is not None
    with Mem(nc,tag) as m:
        ident=m.sb("ident",[128,128]); w=m.sb("w",[128,KC,DIM]); half=m.sb("half",[128,1])
        R=4
        at=m.sb("at",[128,R,DIM]); xt=m.sb("xt",[128,R,DIM]); aT=m.sb("aT",[128,2,DIM])
        s1=m.sb("s1",[128,R,12]); s2=m.sb("s2",[128,R,12]); s3=m.sb("s3",[128,R,12])
        yb=m.sb("yb",[128,R,DIM]); t=m.sb("t",[128,R,DIM]); xo=m.sb("xo",[128,R,DIM])
        T=m.ps("T",[128,2,512]); YR=2 if last else 4; Y=m.ps("Y",[128,YR,512])
        if last:
            bias=m.sb("bias",[128,DIM]); gm=m.sb("gm",[128,DIM]); bm=m.sb("bm",[128,DIM]); cent=m.sb("cent",[128,KC,EXPERTS])
            fn=m.sb("fn",[128,R,DIM]); nrm=m.sb("nrm",[128,R,DIM]); n_free=m.sem("n_free"); n_keep=m.sem("n_keep"); n_turned_=m.sem("n_turned"); nT=m.sb("nT",[128,2,DIM]); T2=m.ps("T2",[128,2,512]); SC=m.ps("SC",[128,2,512])
            t2_full=m.sem("t2_full"); nT_ready=m.sem("nT_ready"); sc_full=m.sem("sc_full"); sc_free=m.sem("sc_free"); n_ready=m.sem("n_ready"); rstd3=m.sem("rstd3"); var3=m.sem("var3")
        consts=m.sem("consts"); half_done=m.sem("half_done")
        a_loaded=[m.sem(f"a_loaded{i}") for i in range(R)]; x_loaded=[m.sem(f"x_loaded{i}") for i in range(R)]; a_free=m.sem("a_free"); x_free=m.sem("x_free")
        dve_done=m.sem("dve_done"); var1=m.sem("var1"); rstd1=m.sem("rstd1"); var2=m.sem("var2"); rstd2=m.sem("rstd2")
        t_full=m.sem("t_full"); aT_ready=m.sem("aT_ready"); y_full=m.sem("y_full"); y_free=m.sem("y_free")
        xo_ready=m.sem("xo_ready"); xo_stored=[m.sem(f"xo_stored{i}") for i in range(R)]
        NCONST=16*(2 if not last else 6)
        with nc.Block() as block:
            @block.sync
            def _(sp):
                sp.dma_start(ident[:],ident_d).then_inc(consts,16)
                sp.dma_start(w[:],w_d.rearrange("(k p) n -> p k n",p=128)).then_inc(consts,16)
                if last:
                    for dst,s in ((bias,bias_d),(gm,g_d),(bm,b_d)):
                        sp.dma_start(dst[:],s.partition_broadcast(128)).then_inc(consts,16)
                    sp.dma_start(cent[:],cent_d.rearrange("(k p) n -> p k n",p=128)).then_inc(consts,16)
                def load(b,u):
                    sp.wait_ge(a_free,1).then_inc(a_free,-1)
                    sp.dma_start(at[:,u%R].rearrange("p (g c) -> p g c",g=GROUPS),ao[bass.ds(b*GROUPS,GROUPS)][:,u*128:u*128+128,:].rearrange("g p c -> p g c")).then_inc(a_loaded[u%R],16)
                    sp.wait_ge(x_free,1).then_inc(x_free,-1)
                    sp.dma_start(xt[:,u%R],rows_of(x_in,b,u)).then_inc(x_loaded[u%R],16)
                pipelined(sp,[load])
            @block.gpsimd
            def _(pool):
                nc.gpsimd.memset(half[:],-0.5).then_inc(half_done,1)
                pool.wait_ge(half_done,1)
                def root(var,s,out):
                    def r(b,u):
                        pool.wait_ge(var,1).then_inc(var,-1)
                        nc.gpsimd.tensor_tensor(s[:,u%R,9:10],s[:,u%R,8:9],half[:],ALU.pow).then_inc(out,1)
                    return r
                pipelined(pool,[root(var1,s1,rstd1),root(var2,s2,rstd2)]+([root(var3,s3,rstd3)] if last else []))
            @block.vector
            def _(dve):
                def done(i):
                    i.then_inc(dve_done,1); dve.wait_ge(dve_done,1).then_inc(dve_done,-1)
                def stats(x,s,out):
                    done(nc.vector.bn_stats(s[:,0:6],x))
                    done(nc.vector.bn_aggr(s[:,6:8],s[:,0:6]))
                    nc.vector.tensor_scalar(s[:,8:9],s[:,7:8],LN_EPS,None,ALU.add).then_inc(out,1)
                if last: dve.wait_ge(consts,NCONST)
                def y_stats(b,u):
                    dve.wait_ge(y_full,1).then_inc(y_full,-1)
                    if last:
                        done(nc.vector.tensor_tensor(yb[:,u%R],Y[:,u%YR,0:DIM],bias[:],ALU.add))
                        dve.sem_inc(y_free,1)
                    stats(yb[:,u%R] if last else Y[:,u%YR,0:DIM],s1[:,u%R],var1)
                def row(x,b,u):
                    return x[:,bass.ds(b*TILES+u,1),:].rearrange("p o d -> p (o d)")
                def residual(b,u):
                    dve.wait_ge(rstd1,1).then_inc(rstd1,-1)
                    done(nc.vector.tensor_scalar(t[:,u%R],yb[:,u%R] if last else Y[:,u%YR,0:DIM],s1[:,u%R,6:7],s1[:,u%R,9:10],ALU.subtract,ALU.mult))
                    if not last: dve.sem_inc(y_free,1)
                    dve.wait_ge(x_loaded[u%R],16).then_inc(x_loaded[u%R],-16)
                    if not last: dve.wait_ge(xo_stored[u%R],16).then_inc(xo_stored[u%R],-16)
                    x=row(z,b,u) if last else xo[:,u%R]
                    done(nc.vector.tensor_tensor(x,t[:,u%R],xt[:,u%R],ALU.add))
                    dve.sem_inc(x_free,1)
                    if not last: dve.sem_inc(xo_ready,1)
                    stats(x,s2[:,u%R],var2)
                def normal(b,u):
                    dve.wait_ge(rstd2,1).then_inc(rstd2,-1)
                    done(nc.vector.tensor_scalar(row(f if last else z,b,u),row(z,b,u) if last else xo[:,u%R],s2[:,u%R,6:7],s2[:,u%R,9:10],ALU.subtract,ALU.mult))
                    if last: stats(row(f,b,u),s3[:,u%R],var3)
                def affine(b,u):
                    dve.wait_ge(rstd3,1).then_inc(rstd3,-1)
                    done(nc.vector.tensor_scalar(fn[:,u%R],row(f,b,u),s3[:,u%R,6:7],s3[:,u%R,9:10],ALU.subtract,ALU.mult))
                    done(nc.vector.tensor_tensor(fn[:,u%R],fn[:,u%R],gm[:],ALU.mult))
                    dve.wait_ge(n_free,1).then_inc(n_free,-1); dve.wait_ge(n_turned_,1).then_inc(n_turned_,-1)
                    done(nc.vector.tensor_tensor(nrm[:,u%R],fn[:,u%R],bm[:],ALU.add))
                    dve.sem_inc(n_ready,1); dve.sem_inc(n_keep,1)
                def score_out(b,u):
                    dve.wait_ge(sc_full,1).then_inc(sc_full,-1)
                    nc.vector.tensor_copy(scores[:,:,bass.ds(b*TILES+u,1)].rearrange("p e o -> p (e o)"),SC[:,u%2,0:EXPERTS]).then_inc(sc_free,1)
                pipelined(dve,[y_stats,residual,normal]+([affine,None,score_out] if last else []))
                if not last:
                    for i in range(R): dve.wait_ge(xo_stored[i],16)
            @block.tensor
            def _(pe):
                pe.sem_inc(a_free,R); pe.sem_inc(x_free,R); pe.sem_inc(y_free,YR)
                if last: pe.sem_inc(sc_free,2); pe.sem_inc(n_free,R); pe.sem_inc(n_turned_,R)
                pe.wait_ge(consts,NCONST)
                def turn(b,u):
                    pe.wait_ge(a_loaded[u%R],16).then_inc(a_loaded[u%R],-16)
                    for k in range(KC):
                        mm=pe.transpose(T[:,u%2,128*k:128*k+128],at[:,u%R,128*k:128*k+128],ident[:])
                    mm.then_inc(t_full,1)
                def product(b,u):
                    pe.wait_ge(aT_ready,1).then_inc(aT_ready,-1)
                    pe.sem_inc(a_free,1)
                    pe.wait_ge(y_free,1).then_inc(y_free,-1)
                    for k in range(KC):
                        mm=pe.matmul(Y[:,u%YR,0:DIM],aT[:,u%2,128*k:128*k+128],w[:,k,:],start=k==0,stop=k==KC-1)
                    mm.then_inc(y_full,1)
                def n_turn(b,u):
                    pe.wait_ge(n_ready,1).then_inc(n_ready,-1)
                    for k in range(KC):
                        mm=pe.transpose(T2[:,u%2,128*k:128*k+128],nrm[:,u%R,128*k:128*k+128],ident[:])
                    mm.then_inc(t2_full,1)
                def score(b,u):
                    pe.wait_ge(nT_ready,1).then_inc(nT_ready,-1); pe.sem_inc(n_turned_,1); pe.wait_ge(sc_free,1).then_inc(sc_free,-1)
                    for k in range(KC):
                        mm=pe.matmul(SC[:,u%2,0:EXPERTS],nT[:,u%2,128*k:128*k+128],cent[:,k,:],start=k==0,stop=k==KC-1)
                    mm.then_inc(sc_full,1)
                pipelined(pe,[turn,product]+([None,None,None,n_turn,score] if last else []))
            @block.scalar
            def _(act):
                nc.scalar.preload_act_table(ACT.Exp)
                if not last:
                    for i in range(R): act.sem_inc(xo_stored[i],16)
                def turned(b,u):
                    act.wait_ge(t_full,1).then_inc(t_full,-1)
                    nc.scalar.activation(aT[:,u%2],T[:,u%2,0:DIM],ACT.Copy).then_inc(aT_ready,1)
                def store(b,u):
                    act.wait_ge(xo_ready,1).then_inc(xo_ready,-1)
                    act.dma_start(rows_of(x_out,b,u),xo[:,u%R]).then_inc(xo_stored[u%R],16)
                def n_turned(b,u):
                    act.wait_ge(t2_full,1).then_inc(t2_full,-1)
                    nc.scalar.activation(nT[:,u%2],T2[:,u%2,0:DIM],ACT.Copy).then_inc(nT_ready,1)
                def keep(b,u):
                    act.wait_ge(n_keep,1).then_inc(n_keep,-1)
                    nc.scalar.activation(norm[:,bass.ds(b*TILES+u,1),:].rearrange("p o d -> p (o d)"),nrm[:,u%R],ACT.Copy).then_inc(n_free,1)
                pipelined(act,[turned,None,None]+([None,None,keep,n_turned] if last else [store]))

GR,PER=4,2
LG=GR+GR*PER

def rms_logits(nc,tag,z,zn,lg,norm_d,wg_d,ident_d):
    with Mem(nc,tag) as m:
        ident=m.sb("ident",[128,128]); wg=m.sb("wg",[128,KC,LG]); nw=m.sb("nw",[128,DIM]); half=m.sb("half",[128,NT])
        sq=m.sb("sq",[128,2,DIM]); ss=m.sb("ss",[128,NT]); ms=m.sb("ms",[128,NT]); rstd=m.sb("rstd",[128,NT])
        ZR=4; zs=m.sb("zs",[128,ZR,DIM]); zT=m.sb("zT",[128,2,DIM])
        T=m.ps("T",[128,2,512]); L=m.ps("L",[128,2,512])
        consts=m.sem("consts"); half_done=m.sem("half_done"); squares=m.sem("squares"); ms_ready=m.sem("ms_ready"); rstd_ready=m.sem("rstd_ready")
        zs_ready=m.sem("zs_ready"); zs_copy=m.sem("zs_copy"); zs_free=m.sem("zs_free"); zs_turned=m.sem("zs_turned"); t_full=m.sem("t_full"); zT_ready=m.sem("zT_ready"); l_full=m.sem("l_full"); l_free=m.sem("l_free")
        act_done=m.sem("act_done")
        with nc.Block() as block:
            @block.sync
            def _(sp):
                sp.dma_start(ident[:],ident_d).then_inc(consts,16)
                sp.dma_start(wg[:],wg_d.rearrange("(k p) n -> p k n",p=128)).then_inc(consts,16)
                sp.dma_start(nw[:],norm_d.partition_broadcast(128)).then_inc(consts,16)
            @block.gpsimd
            def _(pool):
                nc.gpsimd.memset(half[:],-0.5).then_inc(half_done,1)
                pool.wait_ge(half_done,1)
                pool.wait_ge(ms_ready,1).then_inc(ms_ready,-1)
                nc.gpsimd.tensor_tensor(rstd[:],ms[:],half[:],ALU.pow).then_inc(rstd_ready,1)
            @block.scalar
            def _(act):
                nc.scalar.preload_act_table(ACT.Exp)
                act.sem_inc(act_done,2)
                def square(b,u):
                    act.wait_ge(act_done,1).then_inc(act_done,-1)
                    t=bass.ds(b*TILES+u,1)
                    nc.scalar.activation(sq[:,u%2],z[:,t,:].rearrange("p o d -> p (o d)"),ACT.Square,accum_out=ss[:,t]).then_inc(act_done,1)
                pipelined(act,[square])
                act.wait_ge(act_done,2).then_inc(act_done,-2)
                act.sem_inc(squares,1)
                def turned(b,u):
                    act.wait_ge(t_full,1).then_inc(t_full,-1)
                    nc.scalar.activation(zT[:,u%2],T[:,u%2,0:DIM],ACT.Copy).then_inc(zT_ready,1)
                def keep(b,u):
                    act.wait_ge(zs_copy,1).then_inc(zs_copy,-1)
                    nc.scalar.activation(zn[:,bass.ds(b*TILES+u,1),:].rearrange("p o d -> p (o d)"),zs[:,u%ZR],ACT.Copy).then_inc(zs_free,1)
                pipelined(act,[turned,keep])
            @block.vector
            def _(dve):
                dve.wait_ge(consts,48)
                dve.wait_ge(squares,1).then_inc(squares,-1)
                nc.vector.tensor_scalar(ms[:],ss[:],1.0/DIM,RMS_EPS,ALU.mult,ALU.add).then_inc(ms_ready,1)
                dve.wait_ge(rstd_ready,1).then_inc(rstd_ready,-1)
                def scaled(b,u):
                    dve.wait_ge(zs_free,1).then_inc(zs_free,-1); dve.wait_ge(zs_turned,1).then_inc(zs_turned,-1)
                    t=bass.ds(b*TILES+u,1)
                    nc.vector.scalar_tensor_tensor(out=zs[:,u%ZR],in0=z[:,t,:].rearrange("p o d -> p (o d)"),scalar=rstd[:,t],in1=nw[:],op0=ALU.mult,op1=ALU.mult).then_inc(zs_ready,1)
                def batch_out(b,u):
                    if u==TILES-1:
                        dve.wait_ge(l_full,1).then_inc(l_full,-1)
                        nc.vector.tensor_copy(lg[:,:,bass.ds(b*TILES,TILES)],L[:,0,0:TILES*LG].rearrange("p (t l) -> p l t",l=LG)).then_inc(l_free,1)
                pipelined(dve,[scaled,None,None,batch_out])
            @block.tensor
            def _(pe):
                pe.sem_inc(zs_free,ZR); pe.sem_inc(zs_turned,ZR); pe.sem_inc(l_free,1)
                pe.wait_ge(consts,48)
                def turn(b,u):
                    pe.wait_ge(zs_ready,1).then_inc(zs_ready,-1)
                    pe.sem_inc(zs_copy,1)
                    for k in range(KC):
                        mm=pe.transpose(T[:,u%2,128*k:128*k+128],zs[:,u%ZR,128*k:128*k+128],ident[:])
                    mm.then_inc(t_full,1)
                def product(b,u):
                    pe.wait_ge(zT_ready,1).then_inc(zT_ready,-1)
                    pe.sem_inc(zs_turned,1)
                    if u==0: pe.wait_ge(l_free,1).then_inc(l_free,-1)
                    for k in range(KC):
                        mm=pe.matmul(L[:,0,LG*u:LG*u+LG],zT[:,u%2,128*k:128*k+128],wg[:,k,:],start=k==0,stop=k==KC-1)
                    if u==TILES-1: mm.then_inc(l_full,1)
                pipelined(pe,[turn,product])

def route(nc,tag,lg,tri_d,key_d,jv_d,slot,weight,eid,prepare=None):
    with Mem(nc,tag) as m:
        tri=m.sb("tri",[128,2,128],BF); trif=m.sb("trif",[128,2,128]); key=m.sb("key",[128,GR,NT]); jv=m.sb("jv",[128,EXPERTS,SLOTS0])
        e=m.sb("e",[128,GR,NT]); p=m.sb("p",[128,GR,NT]); q=m.sb("q",[128,GR,NT]); oh=m.sb("oh",[128,2,GR,NT])
        a=m.sb("a",[128,NT]); v=m.sb("v",[128,4,NT])
        d=m.sb("d",[128,GR,PER,NT]); pu=m.sb("pu",[128,GR,PER,NT]); c=m.sb("c",[128,GR,PER,NT]); mg=m.sb("mg",[128,GR,NT]); sg=m.sb("sg",[128,GR,NT])
        E=m.sb("E",[128,2,GR,PER,NT]); M=m.sb("M",[128,EXPERTS*NT]); Mb=m.sb("Mb",[128,EXPERTS*NT],BF)
        S=m.sb("S",[128,EXPERTS*NT]); ex=m.sb("ex",[128,EXPERTS*NT]); tot=m.sb("tot",[128,EXPERTS*NT]); zero=m.sb("zero",[128,EXPERTS*NT])
        cnt=m.sb("cnt",[128,4,EXPERTS]); cnti=m.sb("cnti",[128,EXPERTS],I32); sl=m.sb("sl",[128,EXPERTS,NT]); prod=m.sb("prod",[128,2,EXPERTS,NT])
        slf=m.sb("slf",[128,2,NT]); ge=m.sb("ge",[128,EXPERTS,SLOTS0]); ef=m.sb("ef",[128,SLOTS0])
        R=m.ps("R",[128,2,512])
        consts=m.sem("consts"); dve_done=m.sem("dve_done"); x_ready=m.sem("x_ready"); e_ready=m.sem("e_ready"); m_ready=m.sem("m_ready"); r_full=m.sem("r_full")
        prepared=m.sem("prepared")
        lm=lg[:,0:GR,:]; lu=lg[:,GR:LG,:].rearrange("p (g i) t -> p g i t",i=PER)
        def over(x,n): return x.rearrange("p (o t) -> p o t",o=1).broadcast_to([128,n,NT])
        with nc.Block() as block:
            @block.sync
            def _(sp):
                sp.dma_start(trif[:],tri_d).then_inc(consts,16)
                sp.dma_start(key[:],key_d).then_inc(consts,16)
                sp.dma_start(jv[:],jv_d).then_inc(consts,16)
                if prepare:
                    w1,w1_d,w2,w2_d,zeros_d,xs_d=prepare
                    sp.dma_start(w1[:],w1_d.rearrange("(k p) n -> p k n",p=128)).then_inc(prepared,16)
                    sp.dma_start(w2[:],w2_d.rearrange("(k p) n -> p k n",p=128)).then_inc(prepared,16)
                    chunk=zeros_d.shape[0]*zeros_d.shape[1]//DIM
                    for i in range(SLOTS0*128//chunk):
                        sp.dma_start(xs_d[i*chunk:(i+1)*chunk].rearrange("(p b) c -> p (b c)",p=128),zeros_d).then_inc(prepared,16)
                    sp.wait_ge(prepared,16*(2+SLOTS0*128//chunk))
            @block.scalar
            def _(act):
                nc.scalar.preload_act_table(ACT.Exp)
                act.wait_ge(x_ready,1).then_inc(x_ready,-1)
                nc.scalar.activation(e[:],p[:],ACT.Exp).then_inc(e_ready,1)
                nc.scalar.activation(pu[:],d[:],ACT.Exp).then_inc(e_ready,1)
            @block.tensor
            def _(pe):
                pe.wait_ge(m_ready,1).then_inc(m_ready,-1)
                pe.matmul(R[:,0,0:256],tri[:,0,:],Mb[:],start=True,stop=True)
                pe.matmul(R[:,1,0:256],tri[:,1,:],Mb[:],start=True,stop=True).then_inc(r_full,1)
            @block.vector
            def _(dve):
                V=nc.vector
                def done(i):
                    i.then_inc(dve_done,1); dve.wait_ge(dve_done,1).then_inc(dve_done,-1)
                def tt(o,x,y,op): done(V.tensor_tensor(o,x,y,op))
                def ts(o,x,s1,s2,o1,o2=ALU.bypass): done(V.tensor_scalar(o,x,s1,s2,o1,o2))
                def red(o,x,op): done(V.tensor_reduce(o,x,AX.X,op))
                dve.wait_ge(consts,48)
                done(V.memset(zero[:],0.0))
                done(V.tensor_copy(tri[:],trif[:]))
                red(a[:],lm.rearrange("p g t -> p t g"),ALU.max)
                tt(p[:],lm,over(a[:],GR),ALU.subtract)
                tt(mg[:],lu[:,:,0,:],lu[:,:,1,:],ALU.max)
                for i in range(PER): tt(d[:,:,i,:],lu[:,:,i,:],mg[:],ALU.subtract)
                dve.sem_inc(x_ready,1)
                dve.wait_ge(e_ready,2).then_inc(e_ready,-2)
                red(a[:],e[:].rearrange("p g t -> p t g"),ALU.add)
                done(V.reciprocal(a[:],a[:]))
                tt(p[:],e[:],over(a[:],GR),ALU.mult)
                for s in range(2):
                    src=p if s==0 else q
                    red(v[:,s],src[:].rearrange("p g t -> p t g"),ALU.max)
                    tt(e[:],src[:],over(v[:,s],GR),ALU.is_equal)
                    tt(e[:],e[:],key[:],ALU.mult)
                    red(a[:],e[:].rearrange("p g t -> p t g"),ALU.max)
                    tt(oh[:,s],e[:],over(a[:],GR),ALU.is_equal)
                    if s==0: done(V.scalar_tensor_tensor(out=q[:],in0=oh[:,0],scalar=-2.0,in1=p[:],op0=ALU.mult,op1=ALU.add))
                tt(a[:],v[:,0],v[:,1],ALU.add)
                ts(a[:],a[:],EPS,None,ALU.add)
                done(V.reciprocal(a[:],a[:]))
                tt(sg[:],pu[:,:,0,:],pu[:,:,1,:],ALU.add)
                done(V.reciprocal(sg[:],sg[:]))
                for i in range(PER): tt(pu[:,:,i,:],pu[:,:,i,:],sg[:],ALU.mult)
                tt(mg[:],pu[:,:,0,:],pu[:,:,1,:],ALU.max)
                tt(c[:,:,1,:],pu[:,:,1,:],pu[:,:,0,:],ALU.is_gt)
                ts(c[:,:,0,:],c[:,:,1,:],-1.0,1.0,ALU.mult,ALU.add)
                ts(sg[:],mg[:],EPS,None,ALU.add)
                done(V.reciprocal(sg[:],sg[:]))
                tt(mg[:],mg[:],sg[:],ALU.mult)
                for s in range(2):
                    tt(e[:],oh[:,s],mg[:],ALU.mult)
                    red(v[:,2],e[:].rearrange("p g t -> p t g"),ALU.add)
                    tt(v[:,3],v[:,s],a[:],ALU.mult)
                    tt(weight[:,s],v[:,2],v[:,3],ALU.mult)
                    for i in range(PER): tt(E[:,s,:,i,:],oh[:,s],c[:,:,i,:],ALU.mult)
                Ef=[E[:,s].rearrange("p g i t -> p (g i t)") for s in range(2)]
                tt(M[:],Ef[0],Ef[1],ALU.add)
                done(V.tensor_copy(Mb[:],M[:]))
                dve.sem_inc(m_ready,1)
                dve.wait_ge(r_full,1).then_inc(r_full,-1)
                done(V.tensor_copy(tot[:],R[:,1,0:256]))
                done(V.tensor_tensor_scan(out=S[:],data0=tot[:],data1=zero[:],initial=0.0,op0=ALU.add,op1=ALU.add))
                tt(ex[:],S[:],tot[:],ALU.subtract)
                S3=S[:].rearrange("p (e t) -> p e t",t=NT); ex3=ex[:].rearrange("p (e t) -> p e t",t=NT)
                first=ex3[:,:,0]; end=S3[:,:,NT-1]
                tt(cnt[:,0],end,first,ALU.subtract)
                ts(cnt[:,0],cnt[:,0],127.0,None,ALU.add)
                done(V.tensor_copy(cnti[:],cnt[:,0]))
                ts(cnti[:],cnti[:],7,7,ALU.arith_shift_right,ALU.logical_shift_left)
                done(V.tensor_copy(cnt[:,0],cnti[:]))
                done(V.tensor_tensor_scan(out=cnt[:,1],data0=cnt[:,0],data1=zero[:,0:EXPERTS],initial=0.0,op0=ALU.add,op1=ALU.add))
                tt(cnt[:,2],cnt[:,1],cnt[:,0],ALU.subtract)
                tt(cnt[:,3],cnt[:,2],first,ALU.subtract)
                tt(sl[:],ex3,cnt[:,3].rearrange("p (e o) -> p e o",o=1).broadcast_to([128,EXPERTS,NT]),ALU.add)
                tt(sl[:],sl[:],R[:,0,0:256].rearrange("p (e t) -> p e t",t=NT),ALU.add)
                for s in range(2):
                    tt(prod[:,s],Ef[s].rearrange("p (e t) -> p e t",t=NT),sl[:],ALU.mult)
                    red(slf[:,s],prod[:,s].rearrange("p e t -> p t e"),ALU.add)
                    done(V.tensor_copy(slot[:,s],slf[:,s]))
                tt(ge[:],jv[:],cnt[:,1].rearrange("p (e o) -> p e o",o=1).broadcast_to([128,EXPERTS,SLOTS0]),ALU.is_ge)
                red(ef[:],ge[:].rearrange("p e j -> p j e"),ALU.add)
                ts(ef[:],ef[:],float(EXPERTS-1),None,ALU.min)
                done(V.tensor_copy(eid[:],ef[:]))

def experts(nc,tag,zn,slot,eid,w1,w2,xs_d,ys_d,ident_d):
    with Mem(nc,tag) as m:
        ident=m.sb("ident",[128,128]); R=4
        xs=m.sb("xs",[128,R,DIM]); xT=m.sb("xT",[128,2,DIM]); h=m.sb("h",[128,2,F0]); hT=m.sb("hT",[128,2,F0]); y=m.sb("y",[128,2,DIM])
        TX=m.ps("TX",[128,2,512]); TH=m.ps("TH",[128,2,512]); H=m.ps("H",[128,2,512]); Y=m.ps("Y",[128,2,512])
        consts=m.sem("consts"); scattered=m.sem("scattered"); sorted_=m.sem("sorted")
        x_loaded=[m.sem(f"x_loaded{i}") for i in range(R)]; x_free=m.sem("x_free"); tx_full=m.sem("tx_full"); xT_ready=m.sem("xT_ready")
        h_full=m.sem("h_full"); h_ready=m.sem("h_ready"); th_full=m.sem("th_full"); hT_ready=m.sem("hT_ready"); y_full=m.sem("y_full"); y_free=m.sem("y_free"); y_ready=m.sem("y_ready")
        y_stored=[m.sem(f"y_stored{i}") for i in range(2)]; dve_done=m.sem("dve_done")
        U=4
        with nc.Block() as block:
            @block.gpsimd
            def _(pool):
                for t in range(NT):
                    for s in range(2):
                        nc.gpsimd.indirect_dma_start(out=xs_d,out_offset=bass.IndirectOffsetOnAxis(ap=slot[:,s,t:t+1],axis=0),in_=zn[:,t,:],in_offset=None).then_inc(scattered,16)
                pool.wait_ge(scattered,16*2*NT)
                pool.sem_inc(sorted_,1)
            @block.sync
            def _(sp):
                sp.dma_start(ident[:],ident_d).then_inc(consts,16)
                sp.wait_ge(sorted_,1).then_inc(sorted_,-1)
                with sp.Fori(0,SLOTS0//U) as j:
                    for u in range(U):
                        sp.wait_ge(x_free,1).then_inc(x_free,-1)
                        sp.dma_start(xs[:,u%R],xs_d[bass.ds((j*U+u)*128,128),:]).then_inc(x_loaded[u%R],16)
            @block.tensor
            def _(pe):
                pe.sem_inc(x_free,R); pe.sem_inc(y_free,2)
                pe.wait_ge(consts,16)
                def turn_x(u):
                    pe.wait_ge(x_loaded[u%R],16).then_inc(x_loaded[u%R],-16)
                    for k in range(KC):
                        mm=pe.transpose(TX[:,u%2,128*k:128*k+128],xs[:,u%R,128*k:128*k+128],ident[:])
                    mm.then_inc(tx_full,1)
                def first(u,e):
                    pe.wait_ge(xT_ready,1).then_inc(xT_ready,-1)
                    pe.sem_inc(x_free,1)
                    for k in range(KC):
                        mm=pe.matmul(H[:,u%2,:],xT[:,u%2,128*k:128*k+128],w1[:,k,bass.ds(e*F0,F0)],start=k==0,stop=k==KC-1)
                    mm.then_inc(h_full,1)
                def turn_h(u):
                    pe.wait_ge(h_ready,1).then_inc(h_ready,-1)
                    for k in range(F0//128):
                        mm=pe.transpose(TH[:,u%2,128*k:128*k+128],h[:,u%2,128*k:128*k+128],ident[:])
                    mm.then_inc(th_full,1)
                def second(u,e):
                    pe.wait_ge(hT_ready,1).then_inc(hT_ready,-1); pe.wait_ge(y_free,1).then_inc(y_free,-1)
                    for k in range(F0//128):
                        mm=pe.matmul(Y[:,u%2,0:DIM],hT[:,u%2,128*k:128*k+128],w2[:,k,bass.ds(e*DIM,DIM)],start=k==0,stop=k==F0//128-1)
                    mm.then_inc(y_full,1)
                def expert_of(t):
                    return pe.value_load(eid[0:1,bass.ds(t,1)],min_val=0,max_val=EXPERTS-1)
                def four(t,last):
                    for u in range(U):
                        more=not(last and u+1>=U)
                        turn_h(u)
                        if not(last and u+2>=U): turn_x(u+2)
                        if more: first(u+1,expert_of(t+u+1))
                        second(u,expert_of(t+u))
                turn_x(0); turn_x(1); first(0,expert_of(0))
                with pe.Fori(0,SLOTS0//U-1) as j:
                    four(j*U,False)
                four(SLOTS0-U,True)
            @block.scalar
            def _(act):
                nc.scalar.preload_act_table(ACT.Silu)
                def x_turned(u):
                    act.wait_ge(tx_full,1).then_inc(tx_full,-1)
                    nc.scalar.activation(xT[:,u%2],TX[:,u%2,0:DIM],ACT.Copy).then_inc(xT_ready,1)
                def silu(u):
                    act.wait_ge(h_full,1).then_inc(h_full,-1)
                    nc.scalar.activation(h[:,u%2],H[:,u%2,:],ACT.Silu).then_inc(h_ready,1)
                def store(t,u):
                    act.wait_ge(y_ready,1).then_inc(y_ready,-1)
                    act.dma_start(ys_d[bass.ds(t*128,128),:],y[:,u%2]).then_inc(y_stored[u%2],16)
                def four(t,last,first=False):
                    for u in range(U):
                        if not(last and u+2>=U): x_turned(u+2)
                        if not(last and u+1>=U): silu(u+1)
                        if not(first and u==0): store(t+u-1,u-1)
                x_turned(0); x_turned(1); silu(0)
                four(0,False,first=True)
                with act.Fori(1,SLOTS0//U-1) as j:
                    four(j*U,False)
                four(SLOTS0-U,True)
                store(SLOTS0-1,U-1)
            @block.vector
            def _(dve):
                for i in range(2): dve.sem_inc(y_stored[i],16)
                with dve.Fori(0,SLOTS0//U) as j:
                    for u in range(U):
                        dve.wait_ge(th_full,1).then_inc(th_full,-1)
                        nc.vector.tensor_copy(hT[:,u%2],TH[:,u%2,:]).then_inc(hT_ready,1)
                        dve.wait_ge(y_full,1).then_inc(y_full,-1); dve.wait_ge(y_stored[u%2],16).then_inc(y_stored[u%2],-16)
                        nc.vector.tensor_copy(y[:,u%2],Y[:,u%2,0:DIM]).then_inc(dve_done,1)
                        dve.wait_ge(dve_done,1).then_inc(dve_done,-1)
                        dve.sem_inc(y_free,1)
                        dve.sem_inc(y_ready,1)
                for i in range(2): dve.wait_ge(y_stored[i],16)

def combine(nc,tag,z,slot,weight,ys_d):
    with Mem(nc,tag) as m:
        R=8
        y=m.sb("y",[128,R,DIM])
        y_loaded=[m.sem(f"y_loaded{i}") for i in range(R)]; y_free=m.sem("y_free"); dve_done=m.sem("dve_done")
        with nc.Block() as block:
            @block.gpsimd
            def _(pool):
                for n in range(2*NT):
                    pool.wait_ge(y_free,1).then_inc(y_free,-1)
                    t,s=n//2,n%2
                    nc.gpsimd.indirect_dma_start(out=y[:,n%R,:],out_offset=None,in_=ys_d,in_offset=bass.IndirectOffsetOnAxis(ap=slot[:,s,t:t+1],axis=0)).then_inc(y_loaded[n%R],16)
            @block.vector
            def _(dve):
                dve.sem_inc(y_free,R)
                for n in range(2*NT):
                    t,s=n//2,n%2
                    dve.wait_ge(y_loaded[n%R],16*(n//R+1))
                    nc.vector.scalar_tensor_tensor(out=z[:,t,:],in0=y[:,n%R],scalar=weight[:,s,t:t+1],in1=z[:,t,:],op0=ALU.mult,op1=ALU.add).then_inc(dve_done,1)
                    dve.wait_ge(dve_done,1).then_inc(dve_done,-1)
                    dve.sem_inc(y_free,1)

BITS=4; LEVELS=32//BITS; CANDS=2**BITS-1

def assign(nc,tag,scores,tri_d,cand_d,pos):
    with Mem(nc,tag) as m:
        tri=m.sb("tri",[128,2,128],BF); trif=m.sb("trif",[128,2,128]); jt=m.sb("jt",[128,LEVELS,CANDS],I32)
        keep=m.sb("keep",[128,NT]); out_=m.sb("out",[128,NT]); s=m.sb("s",[128,NT]); P=m.sb("P",[128,1],I32)
        cand=m.sb("cand",[128,CANDS],I32); msk=m.sb("msk",[128,CANDS],I32); ge=m.sb("ge",[128,CANDS,NT]); part=m.sb("part",[128,CANDS],BF)
        ok=m.sb("ok",[128,CANDS]); jf=m.sb("jf",[128,1]); ji=m.sb("ji",[128,1],I32)
        thr=m.sb("thr",[128,1],I32); flags=m.sb("flags",[128,2,NT],BF); gt=m.sb("gt",[128,2,NT]); tot=m.sb("tot",[128,2,NT]); zero=m.sb("zero",[128,NT]); S=m.sb("S",[128,2,NT])
        rank=m.sb("rank",[128,2,NT]); need=m.sb("need",[128,1]); sel=m.sb("sel",[128,NT]); w=m.sb("w",[128,NT]); base=m.sb("base",[128,1]); posf=m.sb("posf",[128,NT])
        CN=m.ps("CN",[128,512]); R=m.ps("R",[128,2,512])
        consts=m.sem("consts"); dve_done=m.sem("dve_done"); part_ready=m.sem("part_ready"); count_full=m.sem("count_full"); flags_ready=m.sem("flags_ready"); rank_full=m.sem("rank_full")
        with nc.Block() as block:
            @block.sync
            def _(sp):
                sp.dma_start(trif[:],tri_d).then_inc(consts,16)
                sp.dma_start(jt[:],cand_d).then_inc(consts,16)
            @block.tensor
            def _(pe):
                def ranks():
                    pe.wait_ge(flags_ready,1).then_inc(flags_ready,-1)
                    for i in range(2):
                        mm=pe.matmul(R[:,i,0:2*NT],tri[:,i,:],flags[:].rearrange("p f t -> p (f t)"),start=True,stop=True)
                    mm.then_inc(rank_full,1)
                with pe.Fori(0,EXPERTS-1):
                    for l in range(LEVELS):
                        pe.wait_ge(part_ready,1).then_inc(part_ready,-1)
                        pe.matmul(CN[:,0:CANDS],tri[:,1,:],part[:],start=True,stop=True).then_inc(count_full,1)
                    ranks()
                ranks()
            @block.vector
            def _(dve):
                V=nc.vector
                def done(i):
                    i.then_inc(dve_done,1); dve.wait_ge(dve_done,1).then_inc(dve_done,-1)
                def tt(o,x,y,op): done(V.tensor_tensor(o,x,y,op))
                def ts(o,x,s1,s2,o1,o2=ALU.bypass): done(V.tensor_scalar(o,x,s1,s2,o1,o2))
                def red(o,x,op): done(V.tensor_reduce(o,x,AX.X,op))
                dve.wait_ge(consts,32)
                done(V.tensor_copy(tri[:],trif[:]))
                done(V.memset(zero[:],0.0)); done(V.memset(keep[:],1.0)); done(V.memset(base[:],0.0)); done(V.memset(posf[:],0.0))
                def ranks():
                    dve.sem_inc(flags_ready,1)
                    dve.wait_ge(rank_full,1).then_inc(rank_full,-1)
                    done(V.tensor_copy(tot[:].rearrange("p f t -> p (f t)"),R[:,1,0:2*NT]))
                    for i in range(2):
                        done(V.tensor_tensor_scan(out=S[:,i],data0=tot[:,i],data1=zero[:],initial=0.0,op0=ALU.add,op1=ALU.add))
                    tt(rank[:],S[:],tot[:],ALU.subtract)
                    tt(rank[:],rank[:],R[:,0,0:2*NT].rearrange("p (f t) -> p f t",t=NT),ALU.add)
                with dve.Fori(0,EXPERTS-1) as e:
                    sc=scores[:,bass.ds(e,1),:].rearrange("p o t -> p (o t)")
                    ts(out_[:],keep[:],1.0,3.0e38,ALU.subtract,ALU.mult)
                    tt(s[:],sc,keep[:],ALU.mult)
                    tt(s[:],s[:],out_[:],ALU.add)
                    done(V.memset(P[:],-2**31))
                    for l in range(LEVELS):
                        tt(cand[:],jt[:,l,:],P[:].broadcast_to([128,CANDS]),ALU.bitwise_xor)
                        ts(msk[:],cand[:],31,0x7fffffff,ALU.arith_shift_right,ALU.bitwise_and)
                        tt(cand[:],cand[:],msk[:],ALU.bitwise_xor)
                        tt(ge[:],s[:].rearrange("p (o t) -> p o t",o=1).broadcast_to([128,CANDS,NT]),cand[:].bitcast(F32).rearrange("p (c o) -> p c o",o=1).broadcast_to([128,CANDS,NT]),ALU.is_ge)
                        with nc.allow_low_precision("counts up to 32 are exact"):
                            red(part[:],ge[:],ALU.add)
                        dve.sem_inc(part_ready,1)
                        dve.wait_ge(count_full,1).then_inc(count_full,-1)
                        ts(ok[:],CN[:,0:CANDS],float(CAP),None,ALU.is_ge)
                        red(jf[:],ok[:],ALU.add)
                        done(V.tensor_copy(ji[:],jf[:]))
                        ts(ji[:],ji[:],32-BITS*(l+1),None,ALU.logical_shift_left)
                        tt(P[:],ji[:],P[:],ALU.bitwise_xor)
                    ts(thr[:],P[:],31,0x7fffffff,ALU.arith_shift_right,ALU.bitwise_and)
                    tt(thr[:],thr[:],P[:],ALU.bitwise_xor)
                    ts(gt[:,0],s[:],thr[:].bitcast(F32),None,ALU.is_gt)
                    ts(gt[:,1],s[:],thr[:].bitcast(F32),None,ALU.is_equal)
                    done(V.tensor_copy(flags[:],gt[:]))
                    ranks()
                    ts(need[:],S[:,0,NT-1:NT],-1.0,float(CAP),ALU.mult,ALU.add)
                    ts(w[:],rank[:,1],need[:],None,ALU.is_lt)
                    tt(w[:],w[:],gt[:,1],ALU.mult)
                    tt(sel[:],w[:],gt[:,0],ALU.add)
                    ts(w[:],rank[:,1],need[:],base[:],ALU.min,ALU.add)
                    tt(w[:],w[:],rank[:,0],ALU.add)
                    tt(w[:],w[:],sel[:],ALU.mult)
                    tt(posf[:],posf[:],w[:],ALU.add)
                    tt(keep[:],keep[:],sel[:],ALU.subtract)
                    ts(base[:],base[:],float(CAP),None,ALU.add)
                done(V.memset(flags[:],0.0))
                done(V.tensor_copy(flags[:,0],keep[:]))
                ranks()
                ts(w[:],rank[:,0],base[:],None,ALU.add)
                tt(w[:],w[:],keep[:],ALU.mult)
                tt(posf[:],posf[:],w[:],ALU.add)
                done(V.tensor_copy(pos[:],posf[:]))

def experts1(nc,tag,norm,pos,w1_d,w2_d,b1_d,b2_d,xs_d,ys_d,ident_d):
    T4=CAP//128; FC=F1//128
    with Mem(nc,tag) as m:
        ident=m.sb("ident",[128,128]); b1=m.sb("b1",[128,EXPERTS,FC]); b2=m.sb("b2",[128,EXPERTS*DIM])
        w1=m.sb("w1",[128,2,KC,F1]); w2=m.sb("w2",[128,2,FC,DIM]); xs=m.sb("xs",[128,2,T4,DIM]); xT=m.sb("xT",[128,KC,CAP]); hT=m.sb("hT",[128,FC,CAP]); y=m.sb("y",[128,2,DIM])
        TX=m.ps("TX",[128,2,512]); H=m.ps("H",[128,2,512]); Y=m.ps("Y",[128,4,512])
        consts=m.sem("consts"); scattered=m.sem("scattered"); sorted_=m.sem("sorted")
        w_loaded=[m.sem(f"w_loaded{i}") for i in range(2)]; x_loaded=[m.sem(f"x_loaded{i}") for i in range(2)]; w_free=m.sem("w_free")
        tx_full=m.sem("tx_full"); xT_ready=m.sem("xT_ready"); h_full=m.sem("h_full"); hT_ready=m.sem("hT_ready")
        y_full=m.sem("y_full"); y_ready=m.sem("y_ready"); y_stored=[m.sem(f"y_stored{i}") for i in range(2)]
        with nc.Block() as block:
            @block.gpsimd
            def _(pool):
                for t in range(NT):
                    nc.gpsimd.indirect_dma_start(out=xs_d,out_offset=bass.IndirectOffsetOnAxis(ap=pos[:,t:t+1],axis=0),in_=norm[:,t,:],in_offset=None).then_inc(scattered,16)
                pool.wait_ge(scattered,16*NT)
                pool.sem_inc(sorted_,1)
            @block.sync
            def _(sp):
                sp.dma_start(ident[:],ident_d).then_inc(consts,16)
                sp.dma_start(b1[:],b1_d).then_inc(consts,16)
                sp.dma_start(b2[:],b2_d.partition_broadcast(128)).then_inc(consts,16)
                sp.wait_ge(sorted_,1).then_inc(sorted_,-1)
                with sp.Fori(0,EXPERTS//2) as j:
                    for i in range(2):
                        sp.wait_ge(w_free,1).then_inc(w_free,-1)
                        e=bass.ds(j*2+i,1)
                        sp.dma_start(xs[:,i],xs_d[bass.ds((j*2+i)*CAP,CAP),:].rearrange("(t p) d -> p t d",p=128)).then_inc(x_loaded[i],16)
                        sp.dma_start(w1[:,i],w1_d[e][0].rearrange("(k p) f -> p k f",p=128)).then_inc(w_loaded[i],16)
                        sp.dma_start(w2[:,i],w2_d[e][0].rearrange("(k p) d -> p k d",p=128)).then_inc(w_loaded[i],16)
            @block.tensor
            def _(pe):
                pe.sem_inc(w_free,2)
                pe.wait_ge(consts,48)
                with pe.Fori(0,EXPERTS//2):
                    for i in range(2):
                        pe.wait_ge(x_loaded[i],16).then_inc(x_loaded[i],-16)
                        for k in range(KC):
                            for t in range(T4):
                                mm=pe.transpose(TX[:,k,128*t:128*t+128],xs[:,i,t,128*k:128*k+128],ident[:])
                            mm.then_inc(tx_full,1)
                        pe.wait_ge(w_loaded[i],32).then_inc(w_loaded[i],-32)
                        pe.wait_ge(xT_ready,2).then_inc(xT_ready,-2)
                        for c in range(FC):
                            if c>=2: pe.wait_ge(hT_ready,1).then_inc(hT_ready,-1)
                            for k in range(KC):
                                mm=pe.matmul(H[:,c%2,:],w1[:,i,k,128*c:128*c+128],xT[:,k,:],start=k==0,stop=k==KC-1)
                            mm.then_inc(h_full,1)
                        pe.wait_ge(hT_ready,2).then_inc(hT_ready,-2)
                        for t in range(T4):
                            for c in range(FC):
                                mm=pe.matmul(Y[:,t,0:DIM],hT[:,c,128*t:128*t+128],w2[:,i,c,:],start=c==0,stop=c==FC-1)
                            mm.then_inc(y_full,1)
            @block.scalar
            def _(act):
                nc.scalar.preload_act_table(ACT.Gelu_apprx_tanh)
                act.wait_ge(consts,48)
                for i in range(2): act.sem_inc(y_stored[i],16)
                with act.Fori(0,EXPERTS//2) as j:
                    for i in range(2):
                        for c in range(FC):
                            act.wait_ge(h_full,1).then_inc(h_full,-1)
                            nc.scalar.activation(hT[:,c,:],H[:,c%2,:],ACT.Gelu_apprx_tanh,bias=b1[:,bass.ds(j*2+i,1),c:c+1].rearrange("p o c -> p (o c)")).then_inc(hT_ready,1)
                        for t in range(T4):
                            act.wait_ge(y_ready,1).then_inc(y_ready,-1)
                            act.dma_start(ys_d[bass.ds((j*2+i)*CAP+t*128,128),:],y[:,t%2]).then_inc(y_stored[t%2],16)
            @block.vector
            def _(dve):
                with dve.Fori(0,EXPERTS//2) as j:
                    for i in range(2):
                        for k in range(KC):
                            dve.wait_ge(tx_full,1).then_inc(tx_full,-1)
                            nc.vector.tensor_copy(xT[:,k,:],TX[:,k,:]).then_inc(xT_ready,1)
                        for t in range(T4):
                            dve.wait_ge(y_full,1).then_inc(y_full,-1); dve.wait_ge(y_stored[t%2],16).then_inc(y_stored[t%2],-16)
                            nc.vector.tensor_tensor(y[:,t%2],Y[:,t,0:DIM],b2[:,bass.ds((j*2+i)*DIM,DIM)],ALU.add).then_inc(y_ready,1)
                        dve.sem_inc(w_free,1)
                for i in range(2): dve.wait_ge(y_stored[i],16)

def finish(nc,tag,x,f,pos,ys_d,out_d):
    with Mem(nc,tag) as m:
        R=8
        y=m.sb("y",[128,R,DIM]); o=m.sb("o",[128,R,DIM]); st=m.sb("st",[128,R,12]); fin=m.sb("fin",[128,R,DIM]); half=m.sb("half",[128,1])
        y_loaded=[m.sem(f"y_loaded{i}") for i in range(R)]; y_free=m.sem("y_free"); dve_done=m.sem("dve_done"); half_done=m.sem("half_done")
        var=m.sem("var"); rstd=m.sem("rstd"); fin_ready=m.sem("fin_ready"); stored=[m.sem(f"stored{i}") for i in range(R)]
        LAG=3
        with nc.Block() as block:
            @block.gpsimd
            def _(pool):
                nc.gpsimd.memset(half[:],-0.5).then_inc(half_done,1)
                pool.wait_ge(half_done,1)
                def gather(n):
                    if n>=R: pool.wait_ge(y_free,1).then_inc(y_free,-1)
                    nc.gpsimd.indirect_dma_start(out=y[:,n%R,:],out_offset=None,in_=ys_d,in_offset=bass.IndirectOffsetOnAxis(ap=pos[:,n:n+1],axis=0)).then_inc(y_loaded[n%R],16)
                def root(n):
                    pool.wait_ge(var,1).then_inc(var,-1)
                    nc.gpsimd.tensor_tensor(st[:,n%R,9:10],st[:,n%R,8:9],half[:],ALU.pow).then_inc(rstd,1)
                staged([gather,lambda n:None,lambda n:None,lambda n:None,root],NT)
            @block.vector
            def _(dve):
                def done(i):
                    i.then_inc(dve_done,1); dve.wait_ge(dve_done,1).then_inc(dve_done,-1)
                def add(n):
                    dve.wait_ge(y_loaded[n%R],16*(n//R+1))
                    done(nc.vector.tensor_tensor(o[:,n%R],y[:,n%R],f[:,n,:],ALU.add))
                    dve.sem_inc(y_free,1)
                    done(nc.vector.bn_stats(st[:,n%R,0:6],o[:,n%R]))
                    done(nc.vector.bn_aggr(st[:,n%R,6:8],st[:,n%R,0:6]))
                    nc.vector.tensor_scalar(st[:,n%R,8:9],st[:,n%R,7:8],LN_EPS,None,ALU.add).then_inc(var,1)
                def norm(n):
                    dve.wait_ge(rstd,1).then_inc(rstd,-1)
                    done(nc.vector.tensor_scalar(o[:,n%R],o[:,n%R],st[:,n%R,6:7],st[:,n%R,9:10],ALU.subtract,ALU.mult))
                    if n>=R: dve.wait_ge(stored[n%R],16).then_inc(stored[n%R],-16)
                    nc.vector.tensor_tensor(fin[:,n%R],o[:,n%R],x[:,n,:],ALU.add).then_inc(fin_ready,1)
                staged([add,lambda n:None,norm],NT)
                for i in range(R): dve.wait_ge(stored[i],16)
            @block.sync
            def _(sp):
                for n in range(NT):
                    sp.wait_ge(fin_ready,1).then_inc(fin_ready,-1)
                    sp.dma_start(out_d[n*128:n*128+128,:],fin[:,n%R]).then_inc(stored[n%R],16)

def two_layers(nc,out,x,w_qkv0,w_out0,norm_w,w_route,w1_0,w2_0,w_qkv1,b_qkv1,w_out1,b_out1,ln_g,ln_b,centroids,
               w1_1,w2_1,b1_1,b2_1,ident,prefix,order,starts,cands,positions,masks,zeros):
    def scratch(name,*shape): return nc.dram_tensor(name,shape,F32,kind="Internal").ap()
    qkv=scratch("qkv",BATCH*GROUPS,3,SEQ,4*HD); ao=scratch("ao",BATCH*GROUPS,SEQ,4*HD)
    x1=scratch("x1",TOK,DIM); x2=scratch("x2",TOK,DIM)
    sorted_in=scratch("sorted_in",SLOTS0*128,DIM); sorted_out=scratch("sorted_out",SLOTS0*128,DIM)
    ln_qkv(nc,"qkv0",x,w_qkv0,qkv,ident)
    attention(nc,"att0",qkv,ao,False,1.0/DIM**0.5,ident)
    with Mem(nc,"l0") as m:
        z=m.sb("z",[128,NT,DIM])
        attn_post(nc,"post0",ao,w_out0,x,ident,x_out=x1,z=z)
        with Mem(nc,"ffn0") as f:
            zn=f.sb("zn",[128,NT,DIM]); w1=f.sb("w1",[128,KC,EXPERTS*F0]); w2=f.sb("w2",[128,F0//128,EXPERTS*DIM])
            logits=f.sb("logits",[128,LG,NT]); slot=f.sb("slot",[128,2,NT],U32); weight=f.sb("weight",[128,2,NT]); tile_expert=f.sb("tile_expert",[128,SLOTS0],I32)
            for loop in range(2):
                first=loop==0
                rms_logits(nc,f"rms{loop}",z,zn,logits,norm_w,w_route,ident)
                route(nc,f"route{loop}",logits,prefix,order,starts,slot,weight,tile_expert,
                      prepare=(w1,w1_0,w2,w2_0,zeros,sorted_in) if first else None)
                experts(nc,f"experts{loop}",zn,slot,tile_expert,w1,w2,sorted_in,sorted_out,ident)
                combine(nc,f"combine{loop}",z,slot,weight,sorted_out)
        ln_qkv(nc,"qkv1",x1,w_qkv1,qkv,ident,bias_d=b_qkv1,z=z,x_out=x2)
    attention(nc,"att1",qkv,ao,True,1.0/HD**0.5,ident,positions,masks)
    with Mem(nc,"l1") as m:
        x3=m.sb("x3",[128,NT,DIM]); f=m.sb("f",[128,NT,DIM]); norm=m.sb("norm",[128,NT,DIM])
        scores=m.sb("scores",[128,EXPERTS,NT]); pos=m.sb("pos",[128,NT],U32)
        attn_post(nc,"post1",ao,w_out1,x2,ident,z=x3,bias_d=b_out1,g_d=ln_g,b_d=ln_b,cent_d=centroids,f=f,norm=norm,scores=scores)
        assign(nc,"assign",scores,prefix,cands,pos)
        experts1(nc,"ffn1",norm,pos,w1_1,w2_1,b1_1,b2_1,sorted_in,sorted_out,ident)
        finish(nc,"finish",x3,f,pos,sorted_out,out)

def twelve_bits(x):
    bits=np.asarray(x,np.float32).view(np.uint32).astype(np.uint64)
    return ((bits+0x800)&0xFFFFF000).astype(np.uint32).view(np.float32)

def position_columns():
    start=2.0**(-8.0/HEADS)
    slopes=4*np.array([start*start**i for i in range(HEADS)],dtype=np.float32)
    high=twelve_bits(slopes); low=slopes-high
    table=np.zeros((128,2,2*GROUPS,TILES,2,AUG),np.float32)
    place=(np.arange(TILES)[None,:]*128+np.arange(128)[:,None]).astype(np.float32)
    for pair in range(2*GROUPS):
        for h in range(2):
            head=pair*2+h
            for col,value in ((1,high[head]),(2,-place),(3,low[head]),(4,-place)):
                table[:,0,pair,:,h,col]=value
            for col,value in ((0,-1.0),(1,place),(2,high[head]),(3,place),(4,low[head])):
                table[:,1,pair,:,h,col]=value
    return table.reshape(128,2,2*GROUPS,TILES*2*AUG)

def causal_masks():
    row=np.arange(128)[:,None]; col=np.arange(128)[None,:]
    t=np.zeros((128,4,128),np.float32)
    t[:,0]=row==col; t[:,1]=np.where(col>row,-1e30,0); t[:,2]=-1e30; t[:,3]=np.where(col<row,-1e30,0)
    return t.reshape(128,512)

def prefix_and_ones():
    p=np.arange(128)
    t=np.ones((128,2,128),np.float32); t[:,0]=p[:,None]<p[None,:]
    return t

def group_order():
    return np.broadcast_to((2*GR-np.arange(GR,dtype=np.float32))[None,:,None],(128,GR,NT))

def slot_starts():
    return np.broadcast_to((np.arange(SLOTS0)*128).astype(np.float32),(128,EXPERTS,SLOTS0))

def candidate_bits():
    t=np.array([[j<<(32-BITS*(l+1)) for j in range(1,CANDS+1)] for l in range(LEVELS)],np.int64)
    return np.broadcast_to(t.astype(np.uint32).view(np.int32),(128,LEVELS,CANDS))

def by_group(w):
    return w.reshape(-1,3,GROUPS,4*HD).transpose(0,2,1,3).reshape(w.shape[0],3*DIM)


def kernel(**inputs):
    import concourse.bacc as _bacc
    from concourse.bass_utils import run_bass_kernel_spmd as _run
    a={n:np.asarray(v) for n,v in inputs.items()}
    att=lambda n: a["L1_attn_"+n]
    ffn=lambda n: a["L1_ffn_"+n]
    laid=dict(
        x=a["L0_attn_x"].reshape(TOK,DIM), w_qkv0=by_group(a["L0_attn_w_qkv"]), w_out0=a["L0_attn_w_out"],
        norm_w=a["L0_ffn_norm_w"], w_route=np.concatenate([a["L0_ffn_w_macro"],a["L0_ffn_w_micro"].reshape(EXPERTS,DIM)]).T,
        w1_0=a["L0_ffn_w1"].transpose(2,0,1).reshape(DIM,EXPERTS*F0), w2_0=a["L0_ffn_w2"].transpose(2,0,1).reshape(F0,EXPERTS*DIM),
        w_qkv1=by_group(np.concatenate([att("q_w").T,att("k_w").T,att("v_w").T],axis=1)),
        b_qkv1=by_group(np.concatenate([att("q_b"),att("k_b"),att("v_b")])[None])[0],
        w_out1=att("o_w").T, b_out1=att("o_b"), ln_g=ffn("ln_g"), ln_b=ffn("ln_b"), centroids=ffn("centroids").T,
        w1_1=ffn("w1"), w2_1=ffn("w2"), b1_1=ffn("b1").reshape(EXPERTS,F1//128,128).transpose(2,0,1), b2_1=ffn("b2").reshape(EXPERTS*DIM),
        ident=np.eye(128,dtype=np.float32), prefix=prefix_and_ones(), order=group_order(), starts=slot_starts(),
        cands=candidate_bits(), positions=position_columns(), masks=causal_masks(), zeros=np.zeros((128,2048),np.float32))
    nc=_bacc.Bacc("TRN2",target_bir_lowering=False,num_devices=1)
    arrays,aps={},{}
    for name,value in laid.items():
        value=np.ascontiguousarray(value)
        arrays["in_"+name]=value
        aps[name]=nc.dram_tensor("in_"+name,value.shape,mybir.dt.from_np(value.dtype),kind="ExternalInput").ap()
    out=nc.dram_tensor("out",(TOK,DIM),F32,kind="ExternalOutput").ap()
    two_layers(nc,out,**aps)
    result=_run(nc,[arrays],core_ids=[0])
    return result.results[0]["out"].reshape(BATCH,SEQ,DIM)
```

```python
from contextlib import ExitStack
import numpy as np
import concourse.bass as bass
from concourse import mybir
F32=mybir.dt.float32; F32R=mybir.dt.float32r; BF=mybir.dt.bfloat16; I32=mybir.dt.int32; U32=mybir.dt.uint32
ALU=mybir.AluOpType; ACT=mybir.ActivationFunctionType; AX=mybir.AxisListType
BATCH,SEQ,DIM,HEADS,HD=4,1024,256,16,16
TILES=SEQ//128
GROUPS=4
AUG=5
WIDE=64

class Mem:
    def __init__(self,nc,tag):
        self.nc,self.tag,self.ctx,self.sems=nc,tag,ExitStack(),[]
    def __enter__(self): return self
    def __exit__(self,*a):
        self.ctx.close()
        if self.sems:
            self.nc.clear_and_free_semaphores(self.sems)
            self.nc.all_engine_barrier()
    def sb(self,n,s,d=F32): return self.ctx.enter_context(self.nc.sbuf_tensor(f"{self.tag}_{n}",s,d))
    def ps(self,n,s,d=F32): return self.ctx.enter_context(self.nc.psum_tensor(f"{self.tag}_{n}",s,d))
    def sem(self,n):
        s=self.nc.alloc_semaphore(name=f"{self.tag}_{n}")
        self.sems.append(s)
        return s

def attention(nc, tag, qkv, ao, causal, exp_scale, ident_d, aug_d=None, masks_d=None):
    with Mem(nc,tag) as m:
        sb,ps,sem=m.sb,m.ps,m.sem
        ident=sb("ident",[128,128])
        raw=sb("raw",[128,3,TILES,64])
        qn=sb("qn",[128,TILES,2,WIDE]); kn=sb("kn",[128,TILES,2,WIDE])
        hiR=sb("hiR",[128,2,TILES,2,HD],F32R)
        vn=sb("vn",[128,2,TILES,2,32])
        qT=sb("qT",[128,2,SEQ],F32R)
        kT=sb("kT",[128,2,2,SEQ],F32R)
        pr=sb("pr",[128,4,2,512])
        ot=sb("ot",[128,512])
        mparts=sb("mparts",[128,2,TILES,2]); m16=sb("m16",[128,2*TILES]); mT=sb("mT",[2*TILES,128],F32R)
        osum=sb("osum",[128,4,2,HD+1]); rcp=sb("rcp",[128,4,2,1]); aon=sb("aon",[128,TILES,4,HD])
        if causal:
            augt=sb("augt",[128,2,2*GROUPS,TILES*2*AUG])
            maskf=sb("maskf",[128,128+128+256])
            maskr=sb("maskr",[128,128+128+256],F32R)
        S1=ps("S1",[128,3,512]); S2=ps("S2",[128,3,512]); OP=ps("OP",[128,512]); TP=ps("TP",[128,512])
        consts=sem("consts"); qk_loaded=sem("qk_loaded"); qk_free=sem("qk_free"); rv_loaded=sem("rv_loaded"); rv_free=sem("rv_free")
        nat_ready=sem("nat_ready"); nat_free=sem("nat_free"); v_ready=[sem("v_ready0"),sem("v_ready1")]; v_free=[sem("v_free0"),sem("v_free1")]
        pool_done=sem("pool_done"); dve_done=sem("dve_done"); zeros_done=sem("zeros_done")
        t_dve=sem("t_dve"); t_free=sem("t_free")
        s1_full=sem("s1_full"); half_full=sem("half_full"); half_copied=sem("half_copied"); o_step=sem("o_step"); s1_free=sem("s1_free"); m_ready=sem("m_ready"); mT_ready=sem("mT_ready"); m_placed=sem("m_placed")
        s2_full=sem("s2_full"); s2_free=sem("s2_free")
        o_full=sem("o_full"); ot_ready=sem("ot_ready"); ao_ready=sem("ao_ready"); ao_stored=sem("ao_stored")

        steps=[(c,kt) for c in range(2) for kt in range(4*(c+1) if causal else TILES)]
        def first_col(c,kt):
            return 0 if (not causal or kt<2) else max(0,kt*128-c*512)
        def width(qt,half):
            return 512 if not causal else min(512,(qt+1)*128-half*512)
        maxes=[(qt,heads,half) for q0,half in ((0,0),(4,0),(0,1),(4,1)) for qt in range(q0,q0+4) if width(qt,half)>0
               for heads in (((0,1),) if width(qt,half)<=256 else ((0,),(1,)))]
        EARLY=len([1 for qt,_,half in maxes if qt<4 and half==0])
        NS=len(steps)
        CYCLES=NS//2
        per=(len(maxes)-8)//(CYCLES-2)
        share=[maxes[:8]]+[maxes[8+per*c:8+per*(c+1)] for c in range(CYCLES-1)]
        BANKS=3
        assert (len(maxes)+1)%BANKS==0
        CHUNK0=(4 if causal else TILES)//2
        last_groups=(CHUNK0-1,CYCLES-1)

        with nc.Block() as block:
            @block.sync
            def _(sp):
                sp.dma_start(ident[:],ident_d).then_inc(consts,16)
                if causal:
                    sp.dma_start(augt[:],aug_d).then_inc(consts,16)
                    sp.dma_start(maskf[:],masks_d).then_inc(consts,16)
                def load(bg):
                    sp.wait_ge(qk_free,1).then_inc(qk_free,-1)
                    for m in range(2):
                        sp.dma_start(raw[:,m],qkv[bg][0,m].rearrange("(t p) c -> p t c",p=128)).then_inc(qk_loaded,16)
                    sp.wait_ge(rv_free,1).then_inc(rv_free,-1)
                    sp.dma_start(raw[:,2],qkv[bg][0,2].rearrange("(t p) c -> p t c",p=128)).then_inc(rv_loaded,16)
                def place(s):
                    sp.wait_ge(mT_ready,1).then_inc(mT_ready,-1)
                    for h in range(2):
                        sp.dma_start(qT[64*h:64*h+1,s,:].bitcast(F32).rearrange("o (t q) -> o t q",t=TILES),
                                     mT[TILES*h:TILES*h+TILES,:].bitcast(F32)).then_inc(m_placed,16)
                load(bass.ds(0,1))
                place(0)
                def store(bg):
                    sp.wait_ge(ao_ready,1).then_inc(ao_ready,-1)
                    sp.dma_start(ao[bass.ds(bg,1)][0].rearrange("(t p) c -> p t c",p=128),aon[:].rearrange("p t h d -> p t (h d)")).then_inc(ao_stored,16)
                def loop_body(bg,first,last):
                    if not last: load(bass.ds(bg+1,1))
                    if not first: store(bg-1)
                    place(1)
                    if not last:
                        place(0)
                loop_body(0,True,False)
                with sp.Fori(1,BATCH*GROUPS-1) as bg:
                    loop_body(bg,False,False)
                loop_body(BATCH*GROUPS-1,False,True)
                store(BATCH*GROUPS-1)
                sp.wait_ge(ao_stored,16)

            @block.gpsimd
            def _(pool):
                nc.gpsimd.memset(qn[:],0.0).then_inc(pool_done,1)
                nc.gpsimd.memset(kn[:],0.0).then_inc(pool_done,1)
                nc.gpsimd.memset(vn[:],0.0).then_inc(pool_done,1)
                pool.wait_ge(pool_done,3).then_inc(pool_done,-3)
                nc.gpsimd.memset(kn[:,:,:,0:1],-1.0).then_inc(pool_done,1)
                nc.gpsimd.memset(vn[:,:,:,:,HD:HD+1],1.0).then_inc(pool_done,1)
                pool.wait_ge(pool_done,2).then_inc(pool_done,-2)
                pool.sem_inc(qk_free,1); pool.sem_inc(rv_free,1)
                if causal: pool.wait_ge(consts,48)
                def natural(pair,first=False):
                    s=pair[1]
                    pool.wait_ge(nat_free,1).then_inc(nat_free,-1)
                    for m in range(2):
                        r=raw[:,m,:,32*s:32*s+32].rearrange("p t (h d) -> p t h d",h=2)
                        nc.gpsimd.tensor_copy(hiR[:,m],r).then_inc(pool_done,1)
                    if causal:
                        for m,n in ((0,qn),(1,kn)):
                            src=augt[:,m,pair[0],:]
                            nc.gpsimd.tensor_copy(n[:,:,:,0:AUG],src.rearrange("p (t h a) -> p t h a",t=TILES,h=2)).then_inc(pool_done,1)
                    pool.wait_ge(pool_done,4 if causal else 2).then_inc(pool_done,-(4 if causal else 2))
                    A,B,C=AUG,AUG+HD,AUG+2*HD
                    for m,n,his,lo in ((0,qn,(A,B),C),(1,kn,(A,C),B)):
                        r=raw[:,m,:,32*s:32*s+32].rearrange("p t (h d) -> p t h d",h=2)
                        hi=hiR[:,m].bitcast(F32)
                        for at in his:
                            nc.gpsimd.tensor_copy(n[:,:,:,at:at+HD],hi).then_inc(pool_done,1)
                        nc.gpsimd.tensor_tensor(n[:,:,:,lo:lo+HD],r,hi,ALU.subtract).then_inc(pool_done,1)
                    pool.wait_ge(pool_done,6).then_inc(pool_done,-6)
                    pool.sem_inc(nat_ready,1)
                def values(s):
                    pool.wait_ge(v_free[s],1).then_inc(v_free[s],-1)
                    nc.gpsimd.tensor_copy(vn[:,s,:,:,0:HD],raw[:,2,:,32*s:32*s+32].rearrange("p t (h d) -> p t h d",h=2)).then_inc(v_ready[s],1)
                def group(g):
                    pool.wait_ge(qk_loaded,32).then_inc(qk_loaded,-32)
                    natural((2*g,0))
                    pool.wait_ge(rv_loaded,16).then_inc(rv_loaded,-16)
                    values(0)
                    natural((2*g+1,1))
                    pool.sem_inc(qk_free,1)
                def body(g):
                    values(1)
                    pool.drain().then_inc(rv_free,1)
                    group(g)
                group(0)
                nb=BATCH*GROUPS
                if causal:
                    body(1); body(2); body(3)
                    with pool.Fori(1,BATCH):
                        for g in range(GROUPS): body(g)
                    values(1)
                else:
                    with pool.Fori(1,nb):
                        body(0)
                    values(1)

            @block.tensor
            def _(pe):
                pe.sem_inc(nat_free,1); pe.sem_inc(v_free[0],1); pe.sem_inc(v_free[1],1)
                pe.wait_ge(consts,48 if causal else 16)
                if causal: pe.wait_ge(zeros_done,1).then_inc(zeros_done,-1)
                reader=[t_free]
                def t_bank_free():
                    pe.wait_ge(reader[0],1).then_inc(reader[0],-1)
                    reader[0]=t_free
                def fill(f,half):
                    if f==0 and half==0: pe.wait_ge(nat_ready,1).then_inc(nat_ready,-1)
                    t_bank_free()
                    for t in range(4):
                        mm=pe.transpose(TP[:,128*t:128*t+128],(kn,qn)[f][:,4*half+t].rearrange("p h w -> p (h w)"),ident[:])
                    mm.then_inc(half_full,1)
                    reader[0]=half_copied
                def pass1(s,mx):
                    qt,heads,half=mx
                    x=maxes.index(mx); b=x%BANKS
                    if x==EARLY: pe.sem_inc(nat_free,1)
                    pe.wait_ge(s1_free,1).then_inc(s1_free,-1)
                    n=width(qt,half)
                    diag=causal and qt//4==half
                    for i,h in enumerate(heads):
                        mm=pe.matmul(S1[:,b,n*i:n*i+n],qT[:,s,qt*128:qt*128+128],kT[:,s,h,half*512:half*512+n],start=True,stop=not diag)
                        if diag:
                            mm=pe.matmul(S1[:,b,n*i+n-128:n*i+n],maskr[:,0:128],maskr[:,128:256],start=False,stop=True)
                    mm.then_inc(s1_full,1)
                def qk(s,n,h):
                    c,kt=steps[n]
                    b=(2*n+h)%3
                    if n==0 and h==0:
                        pe.wait_ge(m_placed,32).then_inc(m_placed,-32)
                        pe.wait_ge(s2_free,3).then_inc(s2_free,-3); pe.sem_inc(s2_free,2)
                    else: pe.wait_ge(s2_free,1).then_inc(s2_free,-1)
                    f=first_col(c,kt)
                    diag=causal and kt*128>=c*512
                    mm=pe.matmul(S2[:,b,f:512],kT[:,s,h,kt*128:kt*128+128],qT[:,s,c*512+f:c*512+512],start=True,stop=not diag)
                    if diag:
                        e=kt*128-c*512+128
                        w=e-f
                        mm=pe.matmul(S2[:,b,f:e],maskr[:,0:128],maskr[:,512-w:512],start=False,stop=True)
                    mm.then_inc(s2_full,1)
                def pv(s,g):
                    if g==CYCLES-1:
                        pe.wait_ge(s2_free,3).then_inc(s2_free,-3); pe.sem_inc(s2_free,3)
                    if g==0: pe.wait_ge(v_ready[s],1).then_inc(v_ready[s],-1)
                    for h in range(2):
                        for x in range(2):
                            n=2*g+x; c,kt=steps[n]; f=first_col(c,kt); j=2*h+x
                            mm=pe.matmul(OP[32*j:32*j+32,f:512],vn[:,s,kt,h,:],pr[:,n%4,h,f:512],start=kt<2,stop=g in last_groups,skip_group_check=True)
                    if g in last_groups: mm.then_inc(o_full,1)
                def finish(free_v=None):
                    pe.wait_ge(ot_ready,1).then_inc(ot_ready,-1)
                    if free_v is not None: pe.sem_inc(v_free[free_v],1)
                    t_bank_free()
                    for t in range(4):
                        mm=pe.transpose(TP[:,128*t:128*t+128],ot[:,128*t:128*t+128],ident[:])
                    mm.then_inc(t_dve,1)
                def mtrans():
                    pe.wait_ge(m_ready,1).then_inc(m_ready,-1); pe.wait_ge(s1_free,1).then_inc(s1_free,-1)
                    pe.transpose(S1[0:2*TILES,len(maxes)%BANKS,0:128],m16[:],ident[:]).then_inc(s1_full,1)
                def slot(p2,p1,prev,more):
                    maxima=share[0] if p1 is not None else []
                    if p1 is not None: fill(0,1)
                    for mx in maxima[:2]: pass1(p1,mx)
                    if prev is not None: pv(prev,CYCLES-1)
                    for mx in maxima[2:3]: pass1(p1,mx)
                    if p1 is not None: fill(1,1)
                    for mx in maxima[3:4]: pass1(p1,mx)
                    if prev is not None: finish(free_v=prev)
                    elif p1 is not None:
                        t_bank_free(); pe.sem_inc(t_free,1)
                    for c in range(CYCLES):
                        if p1 is not None: maxima=share[c] if c else share[0][4:]
                        for x in range(4):
                            if x==2 and c==CYCLES-2 and more: fill(0,0)
                            if x==2 and c==CYCLES-1 and more: fill(1,0)
                            for mx in maxima[x:x+1]: pass1(p1,mx)
                            if p2 is not None: qk(p2,2*c+x//2,x%2)
                        if p2 is not None and c==CHUNK0+1: finish()
                        if c==CYCLES-1 and p1 is not None: mtrans()
                        if p2 is not None and c>=1: pv(p2,c-1)
                fill(0,0); fill(1,0)
                slot(None,0,None,True)
                slot(0,1,None,True); slot(1,0,0,True)
                with pe.Fori(1,BATCH*GROUPS-1):
                    slot(0,1,1,True); slot(1,0,0,True)
                slot(0,1,1,False); slot(1,None,0,False)
                pv(1,CYCLES-1)
                finish()

            @block.scalar
            def _(act):
                nc.scalar.preload_act_table(ACT.Exp)
                act.sem_inc(s2_free,3)
                def evac(s,f,half):
                    act.wait_ge(half_full,1).then_inc(half_full,-1)
                    cols=slice(half*512,half*512+512)
                    if f==0:
                        for h in range(2):
                            x=nc.scalar.activation(kT[64*h:64*h+64,s,h,cols],TP[64*h:64*h+64,:],ACT.Copy)
                    else:
                        x=nc.scalar.activation(qT[:,s,cols],TP[:],ACT.Copy)
                    x.then_inc(half_copied,1)
                def exp(n):
                    c,kt=steps[n]; f=first_col(c,kt)
                    for h in range(2):
                        act.wait_ge(s2_full,1).then_inc(s2_full,-1)
                        nc.scalar.activation(pr[:,n%4,h,f:512],S2[:,(2*n+h)%3,f:512],ACT.Exp,scale=exp_scale).then_inc(s2_free,1)
                def slot(p2,p1,more):
                    if p1 is not None:
                        evac(p1,0,1); evac(p1,1,1)
                    for n in range(NS):
                        if p2 is not None: exp(n)
                        if more and n==NS-4: evac(1 if p2 is None else p2,0,0)
                        if more and n==NS-2: evac(1 if p2 is None else p2,1,0)
                evac(0,0,0); evac(0,1,0)
                slot(None,0,True)
                slot(0,1,True); slot(1,0,True)
                with act.Fori(1,BATCH*GROUPS-1):
                    slot(0,1,True); slot(1,0,True)
                slot(0,1,False); slot(1,None,False)

            @block.vector
            def _(dve):
                nc.vector.memset(kT[64:128,:,0,:].bitcast(F32),0.0).then_inc(dve_done,1)
                nc.vector.memset(kT[0:64,:,1,:].bitcast(F32),0.0).then_inc(dve_done,1)
                nc.vector.memset(mparts[:],-3.0e38).then_inc(dve_done,1)
                dve.wait_ge(dve_done,3).then_inc(dve_done,-3)
                if causal:
                    dve.wait_ge(consts,48)
                    nc.vector.tensor_copy(maskr[:],maskf[:]).then_inc(zeros_done,1)
                dve.sem_inc(t_free,1); dve.sem_inc(s1_free,3)
                def rowmax(mx):
                    qt,heads,half=mx
                    b=maxes.index(mx)%BANKS
                    n=width(qt,half)
                    dve.wait_ge(s1_full,1).then_inc(s1_full,-1)
                    nc.vector.tensor_reduce(mparts[:,heads[0]:heads[-1]+1,qt,half],S1[:,b,0:len(heads)*n].rearrange("p (h n) -> p h n",n=n),AX.X,ALU.max).then_inc(s1_free,1)
                def evac_o():
                    dve.wait_ge(o_full,1).then_inc(o_full,-1)
                    nc.vector.tensor_copy(ot[:],OP[:]).then_inc(ot_ready,1)
                def finish(s,c):
                    def add():
                        if s==0 and c==0: dve.wait_ge(ao_stored,16).then_inc(ao_stored,-16)
                        dve.wait_ge(t_dve,1).then_inc(t_dve,-1)
                        o4=TP[:].rearrange("p (t h x d) -> p t h x d",t=4,h=2,x=2)
                        nc.vector.tensor_reduce(osum[:],o4[:,:,:,:,0:HD+1].rearrange("p t h x d -> p t h d x"),AX.X,ALU.add).then_inc(o_step,1)
                    def invert():
                        dve.wait_ge(o_step,1).then_inc(o_step,-1)
                        dve.sem_inc(t_free,1)
                        nc.vector.reciprocal(rcp[:],osum[:,:,:,HD:HD+1]).then_inc(o_step,1)
                    def scale():
                        dve.wait_ge(o_step,1).then_inc(o_step,-1)
                        x=nc.vector.tensor_tensor(aon[:,4*c:4*c+4,2*s:2*s+2,:],osum[:,:,:,0:HD],rcp[:].broadcast_to([128,4,2,HD]),ALU.mult)
                        x.then_inc(ao_ready if (s==1 and c==1) else o_step,1)
                        if not (s==1 and c==1): dve.wait_ge(o_step,1).then_inc(o_step,-1)
                    return [add,invert,scale]
                def mfinal():
                    dve.drain().then_inc(dve_done,1)
                    dve.wait_ge(dve_done,1).then_inc(dve_done,-1)
                    nc.vector.tensor_reduce(m16[:].rearrange("p (h t) -> p h t",h=2),mparts[:],AX.X,ALU.max).then_inc(m_ready,1)
                def mcopy():
                    dve.wait_ge(s1_full,1).then_inc(s1_full,-1)
                    nc.vector.tensor_copy(mT[:],S1[0:2*TILES,len(maxes)%BANKS,0:128]).then_inc(dve_done,1)
                    dve.wait_ge(dve_done,1).then_inc(dve_done,-1)
                    dve.sem_inc(mT_ready,1); dve.sem_inc(s1_free,1)
                def slot(p2,p1,prev):
                    maxima=share[0] if p1 is not None else []
                    for mx in maxima[:2]: rowmax(mx)
                    if prev is not None: evac_o()
                    for mx in maxima[2:4]: rowmax(mx)
                    between=[]
                    if prev is not None: between+=finish(prev,1)
                    for c in range(CYCLES):
                        if p1 is not None: maxima=share[c] if c else share[0][4:]
                        for x in range(4):
                            if c==CHUNK0+2 and x==0 and p2 is not None: between+=finish(p2,0)
                            if between: between.pop(0)()
                            for mx in maxima[x:x+1]: rowmax(mx)
                            if x==0 and p2 is not None and c==CHUNK0+1: evac_o()
                    if p1 is not None:
                        mfinal(); mcopy()
                dve.sem_inc(ao_stored,16)
                slot(None,0,None)
                slot(0,1,None); slot(1,0,0)
                with dve.Fori(1,BATCH*GROUPS-1):
                    slot(0,1,1); slot(1,0,0)
                slot(0,1,1); slot(1,None,0)
                evac_o()
                for step in finish(1,1): step()

TOK=BATCH*SEQ
NT=TOK//128
KC=DIM//128
EXPERTS=8
F0=512
SLOTS0=NT*2+EXPERTS
F1=1024
CAP=TOK//EXPERTS
RMS_EPS=1e-6; LN_EPS=1e-5; EPS=1e-9

def staged(stages,count):
    for n in range(count+len(stages)-1):
        for k in reversed(range(len(stages))):
            if 0<=n-k<count: stages[k](n-k)

def rows_of(ap,b,u):
    return ap[bass.ds(b*SEQ+u*128,128),:]

def stepwise(eng,depth,step):
    def behind(b,u,here):
        return lambda k: None if not here(u-k) else (b,u-k) if u>=k else (b-1,u-k+TILES)
    for u in range(TILES): step(behind(0,u,lambda n: n>=0))
    with eng.Fori(1,BATCH) as b:
        for u in range(TILES): step(behind(b,u,lambda n: True))
    for u in range(depth): step(behind(BATCH,u,lambda n: n<0))

def pipelined(eng,stages):
    def step(at):
        for k,stage in enumerate(stages):
            if stage is not None and at(k): stage(*at(k))
    stepwise(eng,len(stages)-1,step)

def row(x,b,u):
    return x[:,bass.ds(b*TILES+u,1),:].rearrange("p o d -> p (o d)")

STAT=13
def roots(nc,pool,half,s,done,out):
    nc.gpsimd.tensor_tensor(s[:,10:12],s[:,8:10],half[:],ALU.pow).then_inc(done,1)
    pool.wait_ge(done,1).then_inc(done,-1)
    nc.gpsimd.tensor_scalar(s[:,12:13],s[:,6:7],s[:,10:11],-1.0,ALU.mult,ALU.mult).then_inc(out,1)

def ln_qkv(nc,tag,src,w_d,qkv,ident_d):
    W=3*DIM
    with Mem(nc,tag) as m:
        ident=m.sb("ident",[128,128]); w=m.sb("w",[128,KC,W]); half=m.sb("half",[128,1])
        R=4
        xt=m.sb("xt",[128,R,DIM]); st=m.sb("st",[128,R,12]); xn=m.sb("xn",[128,2,DIM]); xT=m.sb("xT",[128,2,DIM]); y=m.sb("y",[128,2,W])
        T=m.ps("T",[128,2,512]); Y=m.ps("Y",[128,2,1024])
        consts=m.sem("consts"); half_done=m.sem("half_done")
        x_loaded=[m.sem(f"x_loaded{i}") for i in range(R)]; x_free=m.sem("x_free")
        dve_done=m.sem("dve_done"); var_ready=m.sem("var_ready"); rstd_ready=m.sem("rstd_ready");
        xn_ready=m.sem("xn_ready"); xn_free=m.sem("xn_free"); t_full=m.sem("t_full"); xT_ready=m.sem("xT_ready")
        y_full=m.sem("y_full"); y_copied=m.sem("y_copied"); y_free=m.sem("y_free")
        stored=[m.sem(f"stored{i}") for i in range(2)]
        with nc.Block() as block:
            @block.sync
            def _(sp):
                sp.dma_start(ident[:],ident_d).then_inc(consts,16)
                sp.dma_start(w[:],w_d.rearrange("(k p) n -> p k n",p=128)).then_inc(consts,16)
                def load(b,u):
                    sp.wait_ge(x_free,1).then_inc(x_free,-1)
                    sp.dma_start(xt[:,u%R],rows_of(src,b,u)).then_inc(x_loaded[u%R],16)
                pipelined(sp,[load])
            @block.gpsimd
            def _(pool):
                nc.gpsimd.memset(half[:],-0.5).then_inc(half_done,1)
                pool.wait_ge(half_done,1)
                def root(b,u):
                    pool.wait_ge(var_ready,1).then_inc(var_ready,-1)
                    nc.gpsimd.tensor_tensor(st[:,u%R,9:10],st[:,u%R,8:9],half[:],ALU.pow).then_inc(rstd_ready,1)
                pipelined(pool,[root])
            @block.vector
            def _(dve):
                def done(i):
                    i.then_inc(dve_done,1); dve.wait_ge(dve_done,1).then_inc(dve_done,-1)
                def x_stats(b,u):
                    dve.wait_ge(x_loaded[u%R],16).then_inc(x_loaded[u%R],-16)
                    s=st[:,u%R]
                    done(nc.vector.bn_stats(s[:,0:6],xt[:,u%R]))
                    done(nc.vector.bn_aggr(s[:,6:8],s[:,0:6]))
                    nc.vector.tensor_scalar(s[:,8:9],s[:,7:8],LN_EPS,None,ALU.add).then_inc(var_ready,1)
                def normal(b,u):
                    dve.wait_ge(rstd_ready,1).then_inc(rstd_ready,-1); dve.wait_ge(xn_free,1).then_inc(xn_free,-1)
                    done(nc.vector.tensor_scalar(xn[:,u%2],xt[:,u%R],st[:,u%R,6:7],st[:,u%R,9:10],ALU.subtract,ALU.mult))
                    dve.sem_inc(xn_ready,1)
                    dve.sem_inc(x_free,1)
                pipelined(dve,[x_stats,normal])
            @block.tensor
            def _(pe):
                pe.sem_inc(xn_free,2); pe.sem_inc(x_free,R); pe.sem_inc(y_free,2)
                pe.wait_ge(consts,32)
                def turn(b,u):
                    pe.wait_ge(xn_ready,1).then_inc(xn_ready,-1)
                    for k in range(KC):
                        mm=pe.transpose(T[:,u%2,128*k:128*k+128],xn[:,u%2,128*k:128*k+128],ident[:])
                    mm.then_inc(t_full,1)
                def product(b,u):
                    pe.wait_ge(xT_ready,1).then_inc(xT_ready,-1)
                    pe.sem_inc(xn_free,1)
                    pe.wait_ge(y_free,1).then_inc(y_free,-1)
                    for n0,n1 in ((0,512),(512,W)):
                        for k in range(KC):
                            mm=pe.matmul(Y[:,u%2,n0:n1],xT[:,u%2,128*k:128*k+128],w[:,k,n0:n1],start=k==0,stop=k==KC-1)
                    mm.then_inc(y_full,1)
                pipelined(pe,[turn,product])
            @block.scalar
            def _(act):
                nc.scalar.preload_act_table(ACT.Exp)
                for i in range(2): act.sem_inc(stored[i],16)
                def turned(b,u):
                    act.wait_ge(t_full,1).then_inc(t_full,-1)
                    nc.scalar.activation(xT[:,u%2],T[:,u%2,0:DIM],ACT.Copy).then_inc(xT_ready,1)
                def y_out(b,u):
                    act.wait_ge(y_full,1).then_inc(y_full,-1); act.wait_ge(stored[u%2],16).then_inc(stored[u%2],-16)
                    nc.scalar.activation(y[:,u%2],Y[:,u%2,0:W],ACT.Copy).then_inc(y_copied,1)
                    act.wait_ge(y_copied,1).then_inc(y_copied,-1)
                    act.sem_inc(y_free,1)
                    act.dma_start(qkv[bass.ds(b*GROUPS,GROUPS)][:,:,u*128:u*128+128,:].rearrange("g m p c -> p (g m) c"),
                                  y[:,u%2].rearrange("p (a c) -> p a c",c=64)).then_inc(stored[u%2],16)
                pipelined(act,[turned,y_out])
                for i in range(2): act.wait_ge(stored[i],16)

def attn_post(nc,tag,ao,w_d,x_in,ident_d,x_out=None,z=None,bias_d=None,g_d=None,b_d=None,cent_d=None,f=None,norm=None,scores=None):
    last=bias_d is not None
    with Mem(nc,tag) as m:
        ident=m.sb("ident",[128,128]); w=m.sb("w",[128,KC,DIM]); half=m.sb("half",[128,2])
        R=4
        RL=8; at=m.sb("at",[128,RL,DIM]); xt=m.sb("xt",[128,RL,DIM]); aT=m.sb("aT",[128,2,DIM])
        s1=m.sb("s1",[128,R,STAT]); s2=m.sb("s2",[128,R,STAT])
        t=m.sb("t",[128,R,DIM]); xo=m.sb("xo",[128,R,DIM])
        T=m.ps("T",[128,2,512]); Y=m.ps("Y",[128,4,512])
        consts=m.sem("consts"); half_done=m.sem("half_done"); pool_done=m.sem("pool_done")
        a_loaded=[m.sem(f"a_loaded{i}") for i in range(RL)]; x_loaded=[m.sem(f"x_loaded{i}") for i in range(RL)]; a_free=m.sem("a_free"); x_free=m.sem("x_free")
        dve_done=m.sem("dve_done"); var1=m.sem("var1"); rstd1=m.sem("rstd1"); var2=m.sem("var2"); rstd2=m.sem("rstd2"); root_given=m.sem("root_given"); stats2_free=m.sem("stats2_free")
        t_full=m.sem("t_full"); aT_ready=m.sem("aT_ready"); y_full=m.sem("y_full"); y_free=m.sem("y_free"); t_ready=m.sem("t_ready")
        x_stored=[m.sem(f"x_stored{i}") for i in range(R)]
        NCONST=16*(2 if not last else 6)
        if last:
            ones=m.sb("ones",[1,128]); bias=m.sb("bias",[1,DIM]); gm=m.sb("gm",[128,DIM]); bm=m.sb("bm",[128,DIM]); cent=m.sb("cent",[128,KC,EXPERTS])
            n1=m.sb("n1",[128,2,DIM]); nrm=m.sb("nrm",[128,R,DIM]); nT=m.sb("nT",[128,2,DIM]); T2=m.ps("T2",[128,512]); SC=m.ps("SC",[128,512])
            n_ready=m.sem("n_ready"); n_keep=m.sem("n_keep"); n_kept=m.sem("n_kept"); n_turned=m.sem("n_turned")
            t2_full=m.sem("t2_full"); nT_ready=m.sem("nT_ready"); sc_full=m.sem("sc_full"); sc_free=m.sem("sc_free")
        with nc.Block() as block:
            @block.sync
            def _(sp):
                sp.dma_start(ident[:],ident_d).then_inc(consts,16)
                sp.dma_start(w[:],w_d.rearrange("(k p) n -> p k n",p=128)).then_inc(consts,16)
                if last:
                    for dst,s in ((gm,g_d),(bm,b_d)):
                        sp.dma_start(dst[:],s.partition_broadcast(128)).then_inc(consts,16)
                    sp.dma_start(bias[:],bias_d.rearrange("(o d) -> o d",o=1)).then_inc(consts,16)
                    sp.dma_start(cent[:],cent_d.rearrange("(k p) n -> p k n",p=128)).then_inc(consts,16)
                def load(b,u):
                    sp.wait_ge(a_free,1).then_inc(a_free,-1)
                    sp.dma_start(at[:,u%RL].rearrange("p (g c) -> p g c",g=GROUPS),ao[bass.ds(b*GROUPS,GROUPS)][:,u*128:u*128+128,:].rearrange("g p c -> p g c")).then_inc(a_loaded[u%RL],16)
                    sp.wait_ge(x_free,1).then_inc(x_free,-1)
                    sp.dma_start(xt[:,u%RL],rows_of(x_in,b,u)).then_inc(x_loaded[u%RL],16)
                pipelined(sp,[load])
            @block.gpsimd
            def _(pool):
                nc.gpsimd.memset(half[:],-0.5).then_inc(half_done,1)
                pool.wait_ge(half_done,1)
                def root1(b,u):
                    pool.wait_ge(var1,1).then_inc(var1,-1)
                    roots(nc,pool,half,s1[:,u%R],pool_done,rstd1)
                def root2(b,u):
                    pool.wait_ge(var2,1).then_inc(var2,-1)
                    roots(nc,pool,half,s2[:,u%R],pool_done,pool_done)
                    pool.wait_ge(pool_done,1).then_inc(pool_done,-1)
                    pool.sem_inc(rstd2,1); pool.sem_inc(root_given,1)
                pipelined(pool,[root1,None,root2])
            @block.tensor
            def _(pe):
                pe.sem_inc(a_free,RL); pe.sem_inc(x_free,RL); pe.sem_inc(y_free,4); pe.sem_inc(stats2_free,R)
                if last: pe.sem_inc(sc_free,1); pe.sem_inc(n_kept,R); pe.sem_inc(n_turned,R)
                pe.wait_ge(consts,NCONST)
                if last: pe.wait_ge(half_done,2)
                def turn(b,u):
                    pe.wait_ge(a_loaded[u%RL],16).then_inc(a_loaded[u%RL],-16)
                    for k in range(KC):
                        mm=pe.transpose(T[:,u%2,128*k:128*k+128],at[:,u%RL,128*k:128*k+128],ident[:])
                    mm.then_inc(t_full,1)
                def product(b,u):
                    pe.wait_ge(aT_ready,1).then_inc(aT_ready,-1)
                    pe.sem_inc(a_free,1)
                    pe.wait_ge(y_free,1).then_inc(y_free,-1)
                    for k in range(KC):
                        mm=pe.matmul(Y[:,u%4,0:DIM],aT[:,u%2,128*k:128*k+128],w[:,k,:],start=k==0,stop=k==KC-1 and not last)
                    if last:
                        mm=pe.matmul(Y[:,u%4,0:DIM],ones[:],bias[:],start=False,stop=True)
                    mm.then_inc(y_full,1)
                def turn_norm(b,u):
                    pe.wait_ge(n_ready,1).then_inc(n_ready,-1)
                    for k in range(KC):
                        mm=pe.transpose(T2[:,128*k:128*k+128],nrm[:,u%R,128*k:128*k+128],ident[:])
                    mm.then_inc(t2_full,1)
                def score(b,u):
                    pe.wait_ge(nT_ready,1).then_inc(nT_ready,-1)
                    pe.sem_inc(n_turned,1)
                    if u==0: pe.wait_ge(sc_free,1).then_inc(sc_free,-1)
                    for k in range(KC):
                        mm=pe.matmul(SC[:,EXPERTS*u:EXPERTS*u+EXPERTS],nT[:,u%2,128*k:128*k+128],cent[:,k,:],start=k==0,stop=k==KC-1)
                    if u==TILES-1: mm.then_inc(sc_full,1)
                def step(at):
                    if at(0): turn(*at(0))
                    if at(1): product(*at(1))
                    if last and at(7): score(*at(7))
                    if last and at(6): turn_norm(*at(6))
                stepwise(pe,7 if last else 1,step)
            @block.scalar
            def _(act):
                nc.scalar.preload_act_table(ACT.Exp)
                if not last:
                    for i in range(R): act.sem_inc(x_stored[i],16)
                def turned(b,u):
                    act.wait_ge(t_full,1).then_inc(t_full,-1)
                    nc.scalar.activation(aT[:,u%2],T[:,u%2,0:DIM],ACT.Copy).then_inc(aT_ready,1)
                def normal_y(b,u):
                    act.wait_ge(rstd1,1).then_inc(rstd1,-1)
                    nc.scalar.activation(t[:,u%R],Y[:,u%4,0:DIM],ACT.Identity,bias=s1[:,u%R,12:13],scale=s1[:,u%R,10:11]).then_inc(t_ready,1)
                def normal_x(b,u):
                    act.wait_ge(rstd2,1).then_inc(rstd2,-1)
                    if not last: act.dma_start(rows_of(x_out,b,u),xo[:,u%R]).then_inc(x_stored[u%R],16)
                    nc.scalar.activation(row(f if last else z,b,u),row(z,b,u) if last else xo[:,u%R],ACT.Identity,bias=s2[:,u%R,12:13],scale=s2[:,u%R,10:11]).then_inc(stats2_free,1)
                def norm_turned(b,u):
                    act.wait_ge(t2_full,1).then_inc(t2_full,-1)
                    nc.scalar.activation(nT[:,u%2],T2[:,0:DIM],ACT.Copy).then_inc(nT_ready,1)
                    act.wait_ge(n_keep,1).then_inc(n_keep,-1)
                    nc.scalar.activation(row(norm,b,u),nrm[:,u%R],ACT.Copy).then_inc(n_kept,1)
                pipelined(act,[turned,None,normal_y,None,normal_x]+([None,norm_turned] if last else []))
            @block.vector
            def _(dve):
                if last:
                    nc.vector.memset(ones[:],1.0).then_inc(half_done,1)
                    dve.wait_ge(consts,NCONST)
                V=nc.vector
                def x_of(b,u): return row(z,b,u) if last else xo[:,u%R]
                def step(at):
                    y,x,n,c=at(0),at(2),at(4) if last else None,at(7) if last and at(7) and at(7)[1]==TILES-1 else None
                    count=0
                    if x:
                        dve.wait_ge(t_ready,1).then_inc(t_ready,-1)
                        dve.sem_inc(y_free,1)
                    if y:
                        dve.wait_ge(y_full,1).then_inc(y_full,-1)
                        V.bn_stats(s1[:,y[1]%R,0:6],Y[:,y[1]%4,0:DIM]).then_inc(dve_done,1); count+=1
                    if x:
                        r=x[1]%R
                        dve.wait_ge(x_loaded[x[1]%RL],16).then_inc(x_loaded[x[1]%RL],-16)
                        dve.wait_ge(stats2_free,1).then_inc(stats2_free,-1)
                        if not last: dve.wait_ge(x_stored[r],16).then_inc(x_stored[r],-16)
                        V.tensor_tensor(x_of(*x),t[:,r],xt[:,x[1]%RL],ALU.add).then_inc(dve_done,1); count+=1
                    if n:
                        r=n[1]%R
                        dve.wait_ge(root_given,1).then_inc(root_given,-1)
                        V.scalar_tensor_tensor(out=n1[:,r%2],in0=row(z,*n),scalar=s2[:,r,6:7],in1=gm[:],op0=ALU.subtract,op1=ALU.mult).then_inc(dve_done,1); count+=1
                    if count: dve.wait_ge(dve_done,count).then_inc(dve_done,-(count))
                    count=0
                    if x: dve.sem_inc(x_free,1)
                    if y: V.bn_aggr(s1[:,y[1]%R,6:8],s1[:,y[1]%R,0:6]).then_inc(dve_done,1); count+=1
                    if x: V.bn_stats(s2[:,x[1]%R,0:6],x_of(*x)).then_inc(dve_done,1); count+=1
                    if n:
                        r=n[1]%R
                        dve.wait_ge(n_kept,1).then_inc(n_kept,-1); dve.wait_ge(n_turned,1).then_inc(n_turned,-1)
                        V.scalar_tensor_tensor(out=nrm[:,r],in0=n1[:,r%2],scalar=s2[:,r,11:12],in1=bm[:],op0=ALU.mult,op1=ALU.add).then_inc(dve_done,1); count+=1
                    if count: dve.wait_ge(dve_done,count).then_inc(dve_done,-(count))
                    count=0
                    if n: dve.sem_inc(n_ready,1); dve.sem_inc(n_keep,1)
                    if y:
                        r=y[1]%R
                        V.tensor_scalar(s1[:,r,8:9],s1[:,r,7:8],LN_EPS,None,ALU.add).then_inc(dve_done,1); count+=1
                        V.tensor_scalar(s1[:,r,9:10],s1[:,r,7:8],LN_EPS,None,ALU.add).then_inc(dve_done,1); count+=1
                    if x: V.bn_aggr(s2[:,x[1]%R,6:8],s2[:,x[1]%R,0:6]).then_inc(dve_done,1); count+=1
                    if c:
                        dve.wait_ge(sc_full,1).then_inc(sc_full,-1)
                        V.tensor_copy(scores[:,:,bass.ds(c[0]*TILES,TILES)],SC[:,0:TILES*EXPERTS].rearrange("p (t e) -> p e t",e=EXPERTS)).then_inc(dve_done,1); count+=1
                    if count: dve.wait_ge(dve_done,count).then_inc(dve_done,-(count))
                    if y: dve.sem_inc(var1,1)
                    if c: dve.sem_inc(sc_free,1)
                    if x:
                        r=x[1]%R
                        V.tensor_scalar(s2[:,r,8:9],s2[:,r,7:8],LN_EPS,None,ALU.add).then_inc(dve_done,1)
                        V.tensor_scalar(s2[:,r,9:10],s2[:,r,7:8],1.0+LN_EPS,LN_EPS*LN_EPS,ALU.mult,ALU.add).then_inc(dve_done,1)
                        dve.wait_ge(dve_done,2).then_inc(dve_done,-2)
                        dve.sem_inc(var2,1)
                stepwise(dve,7 if last else 2,step)
                if not last:
                    for i in range(R): dve.wait_ge(x_stored[i],16)

GR,PER=4,2
LG=GR+GR*PER

def rms_logits(nc,tag,z,rstd,lg,norm_d,wg_d,ident_d,combined=None,prepare=None):
    with Mem(nc,tag) as m:
        R=4
        if combined:
            slot,weight,ys_d=combined
            rows=m.sb("rows",[128,R,2,DIM])
            rows_loaded=[m.sem(f"rows_loaded{i}") for i in range(R)]; rows_ready=m.sem("rows_ready"); rows_free=m.sem("rows_free"); z_ready=m.sem("z_ready"); dve_done=m.sem("dve_done")
        ident=m.sb("ident",[128,128]); wg=m.sb("wg",[128,KC,LG]); nw=m.sb("nw",[128,DIM]); half=m.sb("half",[128,NT])
        sq=m.sb("sq",[128,2,DIM]); ss=m.sb("ss",[128,NT]); ms=m.sb("ms",[128,NT])
        ZR=4; zs=m.sb("zs",[128,ZR,DIM]); zT=m.sb("zT",[128,2,DIM])
        T=m.ps("T",[128,2,512]); L=m.ps("L",[128,2,512])
        consts=m.sem("consts"); half_done=m.sem("half_done"); squares=m.sem("squares"); ms_ready=m.sem("ms_ready"); rstd_ready=m.sem("rstd_ready")
        zs_ready=m.sem("zs_ready"); zs_free=m.sem("zs_free"); t_full=m.sem("t_full"); zT_ready=m.sem("zT_ready"); l_full=m.sem("l_full"); l_free=m.sem("l_free")
        act_done=m.sem("act_done"); prepared=m.sem("prepared")
        with nc.Block() as block:
            @block.sync
            def _(sp):
                sp.dma_start(ident[:],ident_d).then_inc(consts,16)
                sp.dma_start(wg[:],wg_d.rearrange("(k p) n -> p k n",p=128)).then_inc(consts,16)
                sp.dma_start(nw[:],norm_d.partition_broadcast(128)).then_inc(consts,16)
                if prepare:
                    w1,w1_d,w2,w2_d,zeros_d,xs_d=prepare
                    sp.dma_start(w1[:].bitcast(F32),w1_d.rearrange("(k p) n -> p k n",p=128)).then_inc(prepared,16)
                    sp.dma_start(w2[:].bitcast(F32),w2_d.rearrange("(k p) n -> p k n",p=128)).then_inc(prepared,16)
                    chunk=zeros_d.shape[0]*zeros_d.shape[1]//DIM
                    for i in range(SLOTS0*128//chunk):
                        sp.dma_start(xs_d[i*chunk:(i+1)*chunk].rearrange("(p b) c -> p (b c)",p=128),zeros_d).then_inc(prepared,16)
                    sp.wait_ge(prepared,16*(2+SLOTS0*128//chunk))
            @block.gpsimd
            def _(pool):
                nc.gpsimd.memset(half[:],-0.5).then_inc(half_done,1)
                pool.wait_ge(half_done,1)
                if combined:
                    for n in range(NT+2):
                        if n<NT:
                            if n>=R: pool.wait_ge(rows_free,1).then_inc(rows_free,-1)
                            for s in range(2):
                                nc.gpsimd.indirect_dma_start(out=rows[:,n%R,s,:],out_offset=None,in_=ys_d,in_offset=bass.IndirectOffsetOnAxis(ap=slot[:,s,n:n+1],axis=0)).then_inc(rows_loaded[n%R],16)
                        if n>=2:
                            pool.wait_ge(rows_loaded[(n-2)%R],32*((n-2)//R+1))
                            pool.sem_inc(rows_ready,1)
                pool.wait_ge(ms_ready,1).then_inc(ms_ready,-1)
                nc.gpsimd.tensor_tensor(rstd[:],ms[:],half[:],ALU.pow).then_inc(rstd_ready,1)
            @block.scalar
            def _(act):
                nc.scalar.preload_act_table(ACT.Exp)
                act.sem_inc(act_done,2)
                def square(b,u):
                    if combined: act.wait_ge(z_ready,1).then_inc(z_ready,-1)
                    act.wait_ge(act_done,1).then_inc(act_done,-1)
                    t=bass.ds(b*TILES+u,1)
                    nc.scalar.activation(sq[:,u%2],z[:,t,:].rearrange("p o d -> p (o d)"),ACT.Square,accum_out=ss[:,t]).then_inc(act_done,1)
                pipelined(act,[square])
                act.wait_ge(act_done,2).then_inc(act_done,-2)
                act.sem_inc(squares,1)
                def turned(b,u):
                    act.wait_ge(t_full,1).then_inc(t_full,-1)
                    nc.scalar.activation(zT[:,u%2],T[:,u%2,0:DIM],ACT.Copy).then_inc(zT_ready,1)
                pipelined(act,[turned])
            @block.vector
            def _(dve):
                dve.wait_ge(consts,48)
                if combined:
                    def weighted(s,b,u):
                        nc.vector.scalar_tensor_tensor(out=row(z,b,u),in0=rows[:,u%R,s],scalar=weight[:,s,bass.ds(b*TILES+u,1)],in1=row(z,b,u),op0=ALU.mult,op1=ALU.add).then_inc(dve_done,1)
                    def step(at):
                        if at(0):
                            dve.wait_ge(rows_ready,1).then_inc(rows_ready,-1)
                            weighted(0,*at(0))
                        if at(1): weighted(1,*at(1))
                        dve.wait_ge(dve_done,2 if at(0) and at(1) else 1).then_inc(dve_done,-(2 if at(0) and at(1) else 1))
                        if at(1): dve.sem_inc(rows_free,1); dve.sem_inc(z_ready,1)
                    stepwise(dve,1,step)
                dve.wait_ge(squares,1).then_inc(squares,-1)
                nc.vector.tensor_scalar(ms[:],ss[:],1.0/DIM,RMS_EPS,ALU.mult,ALU.add).then_inc(ms_ready,1)
                dve.wait_ge(rstd_ready,1).then_inc(rstd_ready,-1)
                def scaled(b,u):
                    dve.wait_ge(zs_free,1).then_inc(zs_free,-1)
                    t=bass.ds(b*TILES+u,1)
                    nc.vector.scalar_tensor_tensor(out=zs[:,u%ZR],in0=z[:,t,:].rearrange("p o d -> p (o d)"),scalar=rstd[:,t],in1=nw[:],op0=ALU.mult,op1=ALU.mult).then_inc(zs_ready,1)
                def batch_out(b,u):
                    if u==TILES-1:
                        dve.wait_ge(l_full,1).then_inc(l_full,-1)
                        nc.vector.tensor_copy(lg[:,:,bass.ds(b*TILES,TILES)],L[:,0,0:TILES*LG].rearrange("p (t l) -> p l t",l=LG)).then_inc(l_free,1)
                pipelined(dve,[scaled,None,None,batch_out])
            @block.tensor
            def _(pe):
                pe.sem_inc(zs_free,ZR); pe.sem_inc(l_free,1)
                pe.wait_ge(consts,48)
                def turn(b,u):
                    pe.wait_ge(zs_ready,1).then_inc(zs_ready,-1)
                    for k in range(KC):
                        mm=pe.transpose(T[:,u%2,128*k:128*k+128],zs[:,u%ZR,128*k:128*k+128],ident[:])
                    mm.then_inc(t_full,1)
                def product(b,u):
                    pe.wait_ge(zT_ready,1).then_inc(zT_ready,-1)
                    pe.sem_inc(zs_free,1)
                    if u==0: pe.wait_ge(l_free,1).then_inc(l_free,-1)
                    for k in range(KC):
                        mm=pe.matmul(L[:,0,LG*u:LG*u+LG],zT[:,u%2,128*k:128*k+128],wg[:,k,:],start=k==0,stop=k==KC-1)
                    if u==TILES-1: mm.then_inc(l_full,1)
                pipelined(pe,[turn,product])

def route(nc,tag,lg,tri_d,key_d,jv_d,slot,weight,eid):
    with Mem(nc,tag) as m:
        tri=m.sb("tri",[128,2,128],BF); trif=m.sb("trif",[128,2,128]); key=m.sb("key",[128,GR,NT]); jv=m.sb("jv",[128,EXPERTS,SLOTS0])
        e=m.sb("e",[128,GR,NT]); p=m.sb("p",[128,GR,NT]); q=m.sb("q",[128,GR,NT]); oh=m.sb("oh",[128,2,GR,NT])
        a=m.sb("a",[128,NT]); v=m.sb("v",[128,4,NT])
        d=m.sb("d",[128,GR,PER,NT]); pu=m.sb("pu",[128,GR,PER,NT]); c=m.sb("c",[128,GR,PER,NT]); mg=m.sb("mg",[128,GR,NT]); sg=m.sb("sg",[128,GR,NT])
        E=m.sb("E",[128,2,GR,PER,NT]); M=m.sb("M",[128,EXPERTS*NT]); Mb=m.sb("Mb",[128,EXPERTS*NT],BF)
        S=m.sb("S",[128,EXPERTS*NT]); ex=m.sb("ex",[128,EXPERTS*NT]); tot=m.sb("tot",[128,EXPERTS*NT]); zero=m.sb("zero",[128,EXPERTS*NT])
        cnt=m.sb("cnt",[128,4,EXPERTS]); cnti=m.sb("cnti",[128,EXPERTS],I32); sl=m.sb("sl",[128,EXPERTS,NT]); prod=m.sb("prod",[128,2,EXPERTS,NT])
        slf=m.sb("slf",[128,2,NT]); ge=m.sb("ge",[128,EXPERTS,SLOTS0]); ef=m.sb("ef",[128,SLOTS0])
        R=m.ps("R",[128,2,512])
        consts=m.sem("consts"); dve_done=m.sem("dve_done"); x_ready=m.sem("x_ready"); e_ready=m.sem("e_ready"); m_ready=m.sem("m_ready"); r_full=m.sem("r_full")
        lm=lg[:,0:GR,:]; lu=lg[:,GR:LG,:].rearrange("p (g i) t -> p g i t",i=PER)
        def over(x,n): return x.rearrange("p (o t) -> p o t",o=1).broadcast_to([128,n,NT])
        with nc.Block() as block:
            @block.sync
            def _(sp):
                sp.dma_start(trif[:],tri_d).then_inc(consts,16)
                sp.dma_start(key[:],key_d).then_inc(consts,16)
                sp.dma_start(jv[:],jv_d).then_inc(consts,16)
            @block.scalar
            def _(act):
                nc.scalar.preload_act_table(ACT.Exp)
                act.wait_ge(x_ready,1).then_inc(x_ready,-1)
                nc.scalar.activation(e[:],p[:],ACT.Exp).then_inc(e_ready,1)
                nc.scalar.activation(pu[:],d[:],ACT.Exp).then_inc(e_ready,1)
            @block.tensor
            def _(pe):
                pe.wait_ge(m_ready,1).then_inc(m_ready,-1)
                pe.matmul(R[:,0,0:256],tri[:,0,:],Mb[:],start=True,stop=True)
                pe.matmul(R[:,1,0:256],tri[:,1,:],Mb[:],start=True,stop=True).then_inc(r_full,1)
            @block.vector
            def _(dve):
                V=nc.vector
                def done(i):
                    i.then_inc(dve_done,1); dve.wait_ge(dve_done,1).then_inc(dve_done,-1)
                def tt(o,x,y,op): done(V.tensor_tensor(o,x,y,op))
                def ts(o,x,s1,s2,o1,o2=ALU.bypass): done(V.tensor_scalar(o,x,s1,s2,o1,o2))
                def red(o,x,op): done(V.tensor_reduce(o,x,AX.X,op))
                dve.wait_ge(consts,48)
                done(V.memset(zero[:],0.0))
                done(V.tensor_copy(tri[:],trif[:]))
                red(a[:],lm.rearrange("p g t -> p t g"),ALU.max)
                tt(p[:],lm,over(a[:],GR),ALU.subtract)
                tt(mg[:],lu[:,:,0,:],lu[:,:,1,:],ALU.max)
                for i in range(PER): tt(d[:,:,i,:],lu[:,:,i,:],mg[:],ALU.subtract)
                dve.sem_inc(x_ready,1)
                dve.wait_ge(e_ready,2).then_inc(e_ready,-2)
                red(a[:],e[:].rearrange("p g t -> p t g"),ALU.add)
                done(V.reciprocal(a[:],a[:]))
                tt(p[:],e[:],over(a[:],GR),ALU.mult)
                for s in range(2):
                    src=p if s==0 else q
                    red(v[:,s],src[:].rearrange("p g t -> p t g"),ALU.max)
                    tt(e[:],src[:],over(v[:,s],GR),ALU.is_equal)
                    tt(e[:],e[:],key[:],ALU.mult)
                    red(a[:],e[:].rearrange("p g t -> p t g"),ALU.max)
                    tt(oh[:,s],e[:],over(a[:],GR),ALU.is_equal)
                    if s==0: done(V.scalar_tensor_tensor(out=q[:],in0=oh[:,0],scalar=-2.0,in1=p[:],op0=ALU.mult,op1=ALU.add))
                tt(a[:],v[:,0],v[:,1],ALU.add)
                ts(a[:],a[:],EPS,None,ALU.add)
                done(V.reciprocal(a[:],a[:]))
                tt(sg[:],pu[:,:,0,:],pu[:,:,1,:],ALU.add)
                done(V.reciprocal(sg[:],sg[:]))
                for i in range(PER): tt(pu[:,:,i,:],pu[:,:,i,:],sg[:],ALU.mult)
                tt(mg[:],pu[:,:,0,:],pu[:,:,1,:],ALU.max)
                tt(c[:,:,1,:],pu[:,:,1,:],pu[:,:,0,:],ALU.is_gt)
                ts(c[:,:,0,:],c[:,:,1,:],-1.0,1.0,ALU.mult,ALU.add)
                ts(sg[:],mg[:],EPS,None,ALU.add)
                done(V.reciprocal(sg[:],sg[:]))
                tt(mg[:],mg[:],sg[:],ALU.mult)
                for s in range(2):
                    tt(e[:],oh[:,s],mg[:],ALU.mult)
                    red(v[:,2],e[:].rearrange("p g t -> p t g"),ALU.add)
                    tt(v[:,3],v[:,s],a[:],ALU.mult)
                    tt(weight[:,s],v[:,2],v[:,3],ALU.mult)
                    for i in range(PER): tt(E[:,s,:,i,:],oh[:,s],c[:,:,i,:],ALU.mult)
                Ef=[E[:,s].rearrange("p g i t -> p (g i t)") for s in range(2)]
                tt(M[:],Ef[0],Ef[1],ALU.add)
                done(V.tensor_copy(Mb[:],M[:]))
                dve.sem_inc(m_ready,1)
                dve.wait_ge(r_full,1).then_inc(r_full,-1)
                done(V.tensor_copy(tot[:],R[:,1,0:256]))
                done(V.tensor_tensor_scan(out=S[:],data0=tot[:],data1=zero[:],initial=0.0,op0=ALU.add,op1=ALU.add))
                tt(ex[:],S[:],tot[:],ALU.subtract)
                S3=S[:].rearrange("p (e t) -> p e t",t=NT); ex3=ex[:].rearrange("p (e t) -> p e t",t=NT)
                first=ex3[:,:,0]; end=S3[:,:,NT-1]
                tt(cnt[:,0],end,first,ALU.subtract)
                ts(cnt[:,0],cnt[:,0],127.0,None,ALU.add)
                done(V.tensor_copy(cnti[:],cnt[:,0]))
                ts(cnti[:],cnti[:],7,7,ALU.arith_shift_right,ALU.logical_shift_left)
                done(V.tensor_copy(cnt[:,0],cnti[:]))
                done(V.tensor_tensor_scan(out=cnt[:,1],data0=cnt[:,0],data1=zero[:,0:EXPERTS],initial=0.0,op0=ALU.add,op1=ALU.add))
                tt(cnt[:,2],cnt[:,1],cnt[:,0],ALU.subtract)
                tt(cnt[:,3],cnt[:,2],first,ALU.subtract)
                tt(sl[:],ex3,cnt[:,3].rearrange("p (e o) -> p e o",o=1).broadcast_to([128,EXPERTS,NT]),ALU.add)
                tt(sl[:],sl[:],R[:,0,0:256].rearrange("p (e t) -> p e t",t=NT),ALU.add)
                for s in range(2):
                    tt(prod[:,s],Ef[s].rearrange("p (e t) -> p e t",t=NT),sl[:],ALU.mult)
                    red(slf[:,s],prod[:,s].rearrange("p e t -> p t e"),ALU.add)
                    done(V.tensor_copy(slot[:,s],slf[:,s]))
                tt(ge[:],jv[:],cnt[:,1].rearrange("p (e o) -> p e o",o=1).broadcast_to([128,EXPERTS,SLOTS0]),ALU.is_ge)
                red(ef[:],ge[:].rearrange("p e j -> p j e"),ALU.add)
                ts(ef[:],ef[:],float(EXPERTS-1),None,ALU.min)
                done(V.tensor_copy(eid[:],ef[:]))

def experts(nc,tag,z,rstd,norm_d,slot,eid,w1,w2,w1h,w2h,split,xs_d,ys_d,ident_d):
    with Mem(nc,tag) as m:
        ident=m.sb("ident",[128,128]); nw=m.sb("nw",[128,DIM]); R=4
        zn=m.sb("zn",[128,R,DIM])
        xs=m.sb("xs",[128,R,DIM]); xh=m.sb("xh",[128,2,DIM],F32R); xl=m.sb("xl",[128,2,DIM],F32R); h=m.sb("h",[128,2,F0])
        hh=m.sb("hh",[128,2,F0],F32R); hl=m.sb("hl",[128,2,F0],F32R); y=m.sb("y",[128,2,DIM])
        TX=m.ps("TX",[128,2,512]); TH=m.ps("TH",[128,2,512]); H=m.ps("H",[128,2,512]); Y=m.ps("Y",[128,2,512])
        consts=m.sem("consts"); scattered=[m.sem(f"scattered{i}") for i in range(R)]; sorted_=m.sem("sorted"); split_done=m.sem("split_done")
        zn_ready=m.sem("zn_ready"); zn_free=m.sem("zn_free")
        x_loaded=[m.sem(f"x_loaded{i}") for i in range(R)]; x_free=m.sem("x_free"); tx_full=m.sem("tx_full"); xh_ready=m.sem("xh_ready"); x_ready=m.sem("x_ready")
        h_full=m.sem("h_full"); h_ready=m.sem("h_ready"); th_full=m.sem("th_full"); hh_ready=m.sem("hh_ready"); hT_ready=m.sem("hT_ready"); h_high_ready=m.sem("h_high_ready"); y_full=m.sem("y_full"); y_free=m.sem("y_free"); y_ready=m.sem("y_ready")
        y_stored=[m.sem(f"y_stored{i}") for i in range(2)]; dve_done=m.sem("dve_done")
        U=4
        with nc.Block() as block:
            @block.gpsimd
            def _(pool):
                for t in range(NT):
                    pool.wait_ge(zn_ready,1).then_inc(zn_ready,-1)
                    for s in range(2):
                        nc.gpsimd.indirect_dma_start(out=xs_d,out_offset=bass.IndirectOffsetOnAxis(ap=slot[:,s,t:t+1],axis=0),in_=zn[:,t%R,:],in_offset=None).then_inc(scattered[t%R],16)
                    if t>=2:
                        k=t-2
                        pool.wait_ge(scattered[k%R],32*(k//R+1))
                        pool.sem_inc(zn_free,1)
                for i in range(R): pool.wait_ge(scattered[i],32*(NT//R))
                pool.sem_inc(sorted_,1)
            @block.sync
            def _(sp):
                sp.dma_start(ident[:],ident_d).then_inc(consts,16)
                sp.dma_start(nw[:],norm_d.partition_broadcast(128)).then_inc(consts,16)
                sp.wait_ge(sorted_,1).then_inc(sorted_,-1)
                with sp.Fori(0,SLOTS0//U) as j:
                    for u in range(U):
                        sp.wait_ge(x_free,1).then_inc(x_free,-1)
                        sp.dma_start(xs[:,u%R],xs_d[bass.ds((j*U+u)*128,128),:]).then_inc(x_loaded[u%R],16)
            @block.tensor
            def _(pe):
                pe.sem_inc(x_free,R); pe.sem_inc(y_free,2)
                pe.wait_ge(consts,32)
                pe.wait_ge(split_done,1).then_inc(split_done,-1)
                def passes(out,chunks,at,width,pairs,start,stop):
                    for n,(a,b) in enumerate(pairs):
                        for k in range(chunks):
                            mm=pe.matmul(out,a[:,128*k:128*k+128],b[:,k,bass.ds(at,width)],start=start and n==0 and k==0,stop=stop and n==len(pairs)-1 and k==chunks-1)
                    return mm
                def turn_x(u):
                    pe.wait_ge(x_loaded[u%R],16).then_inc(x_loaded[u%R],-16)
                    for k in range(KC):
                        mm=pe.transpose(TX[:,u%2,128*k:128*k+128],xs[:,u%R,128*k:128*k+128],ident[:])
                    mm.then_inc(tx_full,1)
                def first(u,e):
                    pe.wait_ge(x_ready,1).then_inc(x_ready,-1)
                    pe.sem_inc(x_free,1)
                    passes(H[:,u%2,:],KC,e*F0,F0,((xh[:,u%2],w1h),(xh[:,u%2],w1),(xl[:,u%2],w1h)),True,True).then_inc(h_full,1)
                def turn_h(u):
                    pe.wait_ge(h_ready,1).then_inc(h_ready,-1)
                    for k in range(F0//128):
                        mm=pe.transpose(TH[:,u%2,128*k:128*k+128],h[:,u%2,128*k:128*k+128],ident[:])
                    mm.then_inc(th_full,1)
                def second(u,e):
                    pe.wait_ge(h_high_ready,1).then_inc(h_high_ready,-1); pe.wait_ge(y_free,1).then_inc(y_free,-1)
                    passes(Y[:,u%2,0:DIM],F0//128,e*DIM,DIM,((hh[:,u%2],w2h),(hh[:,u%2],w2)),True,False)
                    pe.wait_ge(hT_ready,1).then_inc(hT_ready,-1)
                    passes(Y[:,u%2,0:DIM],F0//128,e*DIM,DIM,((hl[:,u%2],w2h),),False,True).then_inc(y_full,1)
                def expert_of(t):
                    return pe.value_load(eid[0:1,bass.ds(t,1)],min_val=0,max_val=EXPERTS-1)
                def four(t,last):
                    for u in range(U):
                        turn_h(u)
                        if not(last and u+2>=U): turn_x(u+2)
                        if not(last and u+1>=U): first(u+1,expert_of(t+u+1))
                        second(u,expert_of(t+u))
                turn_x(0); turn_x(1); first(0,expert_of(0))
                with pe.Fori(0,SLOTS0//U-1) as j:
                    four(j*U,False)
                four(SLOTS0-U,True)
            @block.scalar
            def _(act):
                nc.scalar.preload_act_table(ACT.Silu)
                def x_high(u):
                    act.wait_ge(tx_full,1).then_inc(tx_full,-1)
                    nc.scalar.activation(xh[:,u%2],TX[:,u%2,0:DIM],ACT.Copy).then_inc(xh_ready,1)
                def h_high(u):
                    act.wait_ge(th_full,1).then_inc(th_full,-1)
                    nc.scalar.activation(hh[:,u%2],TH[:,u%2,:],ACT.Copy).then_inc(hh_ready,1)
                def silu(u):
                    act.wait_ge(h_full,1).then_inc(h_full,-1)
                    nc.scalar.activation(h[:,u%2],H[:,u%2,:],ACT.Silu).then_inc(h_ready,1)
                def store(t,u):
                    act.wait_ge(y_ready,1).then_inc(y_ready,-1)
                    act.dma_start(ys_d[bass.ds(t*128,128),:],y[:,u%2]).then_inc(y_stored[u%2],16)
                def four(t,last,first=False):
                    for u in range(U):
                        h_high(u)
                        if not(last and u+2>=U): x_high(u+2)
                        if not(last and u+1>=U): silu(u+1)
                        if not(first and u==0): store(t+u-1,u-1)
                x_high(0); x_high(1); silu(0)
                four(0,False,first=True)
                with act.Fori(1,SLOTS0//U-1) as j:
                    four(j*U,False)
                four(SLOTS0-U,True)
                store(SLOTS0-1,U-1)
            @block.vector
            def _(dve):
                V=nc.vector
                dve.wait_ge(consts,32)
                for i in range(2): dve.sem_inc(y_stored[i],16)
                dve.sem_inc(zn_free,R)
                parts=[]
                for raw,high in ((w1,w1h),(w2,w2h)):
                    a,b=(v[:].rearrange("p k n -> p (k n)") for v in (raw,high))
                    parts+=[(a[:,c:c+1024],b[:,c:c+1024]) for c in range(0,KC*EXPERTS*F0,1024)]
                for t in range(NT):
                    dve.wait_ge(zn_free,1).then_inc(zn_free,-1)
                    V.scalar_tensor_tensor(out=zn[:,t%R],in0=z[:,t,:],scalar=rstd[:,t:t+1],in1=nw[:],op0=ALU.mult,op1=ALU.mult).then_inc(zn_ready,1)
                    if split and t<len(parts):
                        a,b=parts[t]
                        V.tensor_copy(b,a.bitcast(F32)).then_inc(dve_done,1)
                        dve.wait_ge(dve_done,1).then_inc(dve_done,-1)
                        V.tensor_tensor(a,a.bitcast(F32),b.bitcast(F32),ALU.subtract).then_inc(dve_done,1)
                        dve.wait_ge(dve_done,1).then_inc(dve_done,-1)
                dve.sem_inc(split_done,1)
                def x_low(u):
                    dve.wait_ge(xh_ready,1).then_inc(xh_ready,-1)
                    V.tensor_tensor(xl[:,u%2],TX[:,u%2,0:DIM],xh[:,u%2].bitcast(F32),ALU.subtract).then_inc(x_ready,1)
                def h_low(u):
                    dve.wait_ge(hh_ready,1).then_inc(hh_ready,-1)
                    dve.sem_inc(h_high_ready,1)
                    V.tensor_tensor(hl[:,u%2],TH[:,u%2,:],hh[:,u%2].bitcast(F32),ALU.subtract).then_inc(hT_ready,1)
                def y_out(u):
                    dve.wait_ge(y_full,1).then_inc(y_full,-1); dve.wait_ge(y_stored[u%2],16).then_inc(y_stored[u%2],-16)
                    V.tensor_copy(y[:,u%2],Y[:,u%2,0:DIM]).then_inc(dve_done,1)
                    dve.wait_ge(dve_done,1).then_inc(dve_done,-1)
                    dve.sem_inc(y_free,1)
                    dve.sem_inc(y_ready,1)
                def four(last):
                    for u in range(U):
                        h_low(u)
                        if not(last and u+2>=U): x_low(u+2)
                        y_out(u)
                x_low(0); x_low(1)
                with dve.Fori(0,SLOTS0//U-1):
                    four(False)
                four(True)
                for i in range(2): dve.wait_ge(y_stored[i],16)

def combine_qkv(nc,tag,z,slot,weight,ys_d,src,w_d,bias_d,x_out,qkv,ident_d):
    W=3*DIM
    with Mem(nc,tag) as m:
        R=4
        ident=m.sb("ident",[128,128]); w=m.sb("w",[128,KC,W]); bias=m.sb("bias",[128,W]); half=m.sb("half",[128,2])
        rows=m.sb("rows",[128,R,2,DIM]); RL=8; xt=m.sb("xt",[128,RL,DIM]); lnz=m.sb("lnz",[128,R,DIM]); x2=m.sb("x2",[128,R,DIM])
        sz=m.sb("sz",[128,R,STAT]); sx=m.sb("sx",[128,R,STAT]); xn=m.sb("xn",[128,2,DIM]); xT=m.sb("xT",[128,2,DIM]); y=m.sb("y",[128,2,W])
        T=m.ps("T",[128,2,512]); Y=m.ps("Y",[128,2,1024])
        consts=m.sem("consts"); half_done=m.sem("half_done"); pool_done=m.sem("pool_done"); dve_done=m.sem("dve_done")
        rows_loaded=[m.sem(f"rows_loaded{i}") for i in range(R)]; rows_ready=m.sem("rows_ready"); rows_free=m.sem("rows_free")
        x_loaded=[m.sem(f"x_loaded{i}") for i in range(RL)]; x_free=m.sem("x_free")
        varz=m.sem("varz"); rootz=m.sem("rootz"); varx=m.sem("varx"); rootx=m.sem("rootx"); lnz_ready=m.sem("lnz_ready")
        x2_ready=m.sem("x2_ready"); x2_free=m.sem("x2_free"); x2_stored=[m.sem(f"x2_stored{i}") for i in range(R)]
        xn_ready=m.sem("xn_ready"); xn_free=m.sem("xn_free"); t_full=m.sem("t_full"); xT_ready=m.sem("xT_ready")
        y_full=m.sem("y_full"); y_free=m.sem("y_free"); y_copied=m.sem("y_copied"); y_stored=[m.sem(f"y_stored{i}") for i in range(2)]
        with nc.Block() as block:
            @block.sync
            def _(sp):
                sp.dma_start(ident[:],ident_d).then_inc(consts,16)
                sp.dma_start(w[:],w_d.rearrange("(k p) n -> p k n",p=128)).then_inc(consts,16)
                sp.dma_start(bias[:],bias_d.partition_broadcast(128)).then_inc(consts,16)
                def load(b,u):
                    sp.wait_ge(x_free,1).then_inc(x_free,-1)
                    sp.dma_start(xt[:,u%RL],rows_of(src,b,u)).then_inc(x_loaded[u%RL],16)
                def keep(b,u):
                    sp.wait_ge(x2_ready,1).then_inc(x2_ready,-1)
                    sp.dma_start(rows_of(x_out,b,u),x2[:,u%R]).then_inc(x2_stored[u%R],16)
                pipelined(sp,[load,None,None,None,keep])
            @block.gpsimd
            def _(pool):
                nc.gpsimd.memset(half[:],-0.5).then_inc(half_done,1)
                pool.wait_ge(half_done,1)
                def gather(n):
                    if n>=R: pool.wait_ge(rows_free,1).then_inc(rows_free,-1)
                    for s in range(2):
                        nc.gpsimd.indirect_dma_start(out=rows[:,n%R,s,:],out_offset=None,in_=ys_d,in_offset=bass.IndirectOffsetOnAxis(ap=slot[:,s,n:n+1],axis=0)).then_inc(rows_loaded[n%R],16)
                def arrived(n):
                    pool.wait_ge(rows_loaded[n%R],32*(n//R+1))
                    pool.sem_inc(rows_ready,1)
                def root_z(n):
                    pool.wait_ge(varz,1).then_inc(varz,-1)
                    roots(nc,pool,half,sz[:,n%R],pool_done,rootz)
                def root_x(n):
                    pool.wait_ge(varx,1).then_inc(varx,-1)
                    roots(nc,pool,half,sx[:,n%R],pool_done,rootx)
                for n in range(NT+7):
                    for lag,stage in ((0,gather),(2,arrived),(3,root_z),(6,root_x)):
                        if 0<=n-lag<NT: stage(n-lag)
            @block.tensor
            def _(pe):
                pe.sem_inc(xn_free,2); pe.sem_inc(x_free,RL); pe.sem_inc(y_free,2); pe.sem_inc(x2_free,R)
                pe.wait_ge(consts,48)
                def turn(b,u):
                    pe.wait_ge(xn_ready,1).then_inc(xn_ready,-1)
                    pe.sem_inc(x2_free,1)
                    for k in range(KC):
                        mm=pe.transpose(T[:,u%2,128*k:128*k+128],xn[:,u%2,128*k:128*k+128],ident[:])
                    mm.then_inc(t_full,1)
                def product(b,u):
                    pe.wait_ge(xT_ready,1).then_inc(xT_ready,-1)
                    pe.sem_inc(xn_free,1)
                    pe.wait_ge(y_free,1).then_inc(y_free,-1)
                    for n0,n1 in ((0,512),(512,W)):
                        for k in range(KC):
                            mm=pe.matmul(Y[:,u%2,n0:n1],xT[:,u%2,128*k:128*k+128],w[:,k,n0:n1],start=k==0,stop=k==KC-1)
                    mm.then_inc(y_full,1)
                pipelined(pe,[turn,product])
            @block.scalar
            def _(act):
                nc.scalar.preload_act_table(ACT.Exp)
                for i in range(R): act.sem_inc(x2_stored[i],16)
                for i in range(2): act.sem_inc(y_stored[i],16)
                def ln_z(b,u):
                    act.wait_ge(rootz,1).then_inc(rootz,-1)
                    nc.scalar.activation(lnz[:,u%R],row(z,b,u),ACT.Identity,bias=sz[:,u%R,12:13],scale=sz[:,u%R,10:11]).then_inc(lnz_ready,1)
                def ln_x(b,u):
                    act.wait_ge(rootx,1).then_inc(rootx,-1); act.wait_ge(xn_free,1).then_inc(xn_free,-1)
                    nc.scalar.activation(xn[:,u%2],x2[:,u%R],ACT.Identity,bias=sx[:,u%R,12:13],scale=sx[:,u%R,10:11]).then_inc(xn_ready,1)
                def turned(b,u):
                    act.wait_ge(t_full,1).then_inc(t_full,-1)
                    nc.scalar.activation(xT[:,u%2],T[:,u%2,0:DIM],ACT.Copy).then_inc(xT_ready,1)
                def store(b,u):
                    act.wait_ge(y_copied,1).then_inc(y_copied,-1)
                    act.sem_inc(y_free,1)
                    act.dma_start(qkv[bass.ds(b*GROUPS,GROUPS)][:,:,u*128:u*128+128,:].rearrange("g m p c -> p (g m) c"),
                                  y[:,u%2].rearrange("p (a c) -> p a c",c=64)).then_inc(y_stored[u%2],16)
                pipelined(act,[ln_z,None,None,ln_x,turned,store])
            @block.vector
            def _(dve):
                V=nc.vector
                dve.wait_ge(consts,48)
                def weighted(s,b,u):
                    V.scalar_tensor_tensor(out=row(z,b,u),in0=rows[:,u%R,s],scalar=weight[:,s,bass.ds(b*TILES+u,1)],in1=row(z,b,u),op0=ALU.mult,op1=ALU.add).then_inc(dve_done,1)
                def step(at):
                    a,x,q=at(0),at(3),at(6)
                    count=0
                    if a:
                        dve.wait_ge(rows_ready,1).then_inc(rows_ready,-1)
                        weighted(0,*a); count+=1
                    if x:
                        r=x[1]%R
                        dve.wait_ge(lnz_ready,1).then_inc(lnz_ready,-1); dve.wait_ge(x_loaded[x[1]%RL],16).then_inc(x_loaded[x[1]%RL],-16); dve.wait_ge(x2_stored[r],16).then_inc(x2_stored[r],-16); dve.wait_ge(x2_free,1).then_inc(x2_free,-1)
                        V.tensor_tensor(x2[:,r],lnz[:,r],xt[:,x[1]%RL],ALU.add).then_inc(dve_done,1); count+=1
                    if count: dve.wait_ge(dve_done,count).then_inc(dve_done,-(count))
                    count=0
                    if a: weighted(1,*a); count+=1
                    if x:
                        dve.sem_inc(x2_ready,1); dve.sem_inc(x_free,1)
                        V.bn_stats(sx[:,x[1]%R,0:6],x2[:,x[1]%R]).then_inc(dve_done,1); count+=1
                    if count: dve.wait_ge(dve_done,count).then_inc(dve_done,-(count))
                    count=0
                    if a:
                        dve.sem_inc(rows_free,1)
                        V.bn_stats(sz[:,a[1]%R,0:6],row(z,*a)).then_inc(dve_done,1); count+=1
                    if x: V.bn_aggr(sx[:,x[1]%R,6:8],sx[:,x[1]%R,0:6]).then_inc(dve_done,1); count+=1
                    if count: dve.wait_ge(dve_done,count).then_inc(dve_done,-(count))
                    count=0
                    if a: V.bn_aggr(sz[:,a[1]%R,6:8],sz[:,a[1]%R,0:6]).then_inc(dve_done,1); count+=1
                    if x:
                        for c in (8,9): V.tensor_scalar(sx[:,x[1]%R,c:c+1],sx[:,x[1]%R,7:8],LN_EPS,None,ALU.add).then_inc(dve_done,1); count+=1
                    if count: dve.wait_ge(dve_done,count).then_inc(dve_done,-(count))
                    if x: dve.sem_inc(varx,1)
                    if a:
                        for c in (8,9): V.tensor_scalar(sz[:,a[1]%R,c:c+1],sz[:,a[1]%R,7:8],LN_EPS,None,ALU.add).then_inc(dve_done,1)
                    if q:
                        dve.wait_ge(y_full,1).then_inc(y_full,-1); dve.wait_ge(y_stored[q[1]%2],16).then_inc(y_stored[q[1]%2],-16)
                        V.tensor_tensor(y[:,q[1]%2],Y[:,q[1]%2,0:W],bias[:],ALU.add).then_inc(y_copied,1)
                    if a:
                        dve.wait_ge(dve_done,2).then_inc(dve_done,-2)
                        dve.sem_inc(varz,1)
                stepwise(dve,8,step)
                for i in range(2): dve.wait_ge(y_stored[i],16)
                for i in range(R): dve.wait_ge(x2_stored[i],16)

BITS=4; LEVELS=32//BITS; CANDS=2**BITS-1

def assigned_experts(nc,tag,scores,norm,pos,tri_d,cand_d,w1_d,w2_d,b1_d,b2_d,xs_d,ys_d,ident_d):
    T4=CAP//128; FC=F1//128; FAR=2.0*TOK
    with Mem(nc,tag) as m:
        tri=m.sb("tri",[128,2,128],BF); trif=m.sb("trif",[128,2,128]); jt=m.sb("jt",[128,LEVELS,CANDS],I32)
        keep=m.sb("keep",[128,NT]); out_=m.sb("out",[128,NT]); s=m.sb("s",[128,NT]); P=m.sb("P",[128,1],I32)
        cand=m.sb("cand",[128,CANDS],I32); msk=m.sb("msk",[128,CANDS],I32); ge=m.sb("ge",[128,CANDS,NT]); part=m.sb("part",[128,CANDS],BF)
        ok=m.sb("ok",[128,CANDS]); found=m.sb("found",[128,1],I32)
        flags=m.sb("flags",[128,2,NT],BF); gt=m.sb("gt",[128,2,NT]); tot=m.sb("tot",[128,2,NT]); zero=m.sb("zero",[128,NT]); S=m.sb("S",[128,2,NT])
        rank=m.sb("rank",[128,2,NT]); need=m.sb("need",[128,1]); sel=m.sb("sel",[128,NT]); w=m.sb("w",[128,NT]); base=m.sb("base",[128,1]); posf=m.sb("posf",[128,NT])
        target=m.sb("target",[128,NT],U32)
        CN=m.ps("CN",[128,512]); RK=m.ps("RK",[128,512])
        consts=m.sem("consts"); dve_done=m.sem("dve_done"); part_ready=m.sem("part_ready"); count_full=m.sem("count_full"); flags_ready=m.sem("flags_ready"); rank_full=m.sem("rank_full")
        target_ready=m.sem("target_ready"); target_free=m.sem("target_free"); scattered=m.sem("scattered"); sorted_=m.sem("sorted"); tri_ready=m.sem("tri_ready")
        ident=m.sb("ident",[128,128]); b1=m.sb("b1",[128,EXPERTS,FC]); b2=m.sb("b2",[1,EXPERTS*DIM]); ones=m.sb("ones",[1,128])
        w1=m.sb("w1",[128,2,KC,F1]); w2=m.sb("w2",[128,2,FC,DIM]); xs=m.sb("xs",[128,2,T4,DIM]); xT=m.sb("xT",[128,KC,CAP]); hT=m.sb("hT",[128,FC,CAP]); y=m.sb("y",[128,2,DIM])
        TX=m.ps("TX",[128,2,512]); H=m.ps("H",[128,2,512]); Y=m.ps("Y",[128,2,512])
        w_loaded=[m.sem(f"w_loaded{i}") for i in range(2)]; x_loaded=[m.sem(f"x_loaded{i}") for i in range(2)]; w_free=m.sem("w_free")
        tx_full=m.sem("tx_full"); xT_ready=m.sem("xT_ready"); h_full=m.sem("h_full"); hT_ready=m.sem("hT_ready")
        y_full=m.sem("y_full"); y_free=m.sem("y_free"); y_copied=m.sem("y_copied"); y_stored=[m.sem(f"y_stored{i}") for i in range(2)]
        with nc.Block() as block:
            @block.gpsimd
            def _(pool):
                with pool.Fori(0,EXPERTS) as e:
                    pool.wait_ge(target_ready,1).then_inc(target_ready,-1)
                    for t in range(NT):
                        nc.gpsimd.indirect_dma_start(out=xs_d,out_offset=bass.IndirectOffsetOnAxis(ap=target[:,t:t+1],axis=0),in_=norm[:,t,:],in_offset=None,
                                                     bounds_check=TOK-1,oob_is_err=False).then_inc(scattered,16)
                    pool.wait_ge(scattered,(e+1)*(16*NT))
                    pool.sem_inc(target_free,1)
                    pool.sem_inc(sorted_,1)
            @block.sync
            def _(sp):
                sp.dma_start(trif[:],tri_d).then_inc(consts,16)
                sp.dma_start(jt[:],cand_d).then_inc(consts,16)
                sp.dma_start(ident[:],ident_d).then_inc(consts,16)
                sp.dma_start(b1[:],b1_d).then_inc(consts,16)
                sp.dma_start(b2[:],b2_d.rearrange("(o d) -> o d",o=1)).then_inc(consts,16)
                with sp.Fori(0,EXPERTS//2) as j:
                    for i in range(2):
                        sp.wait_ge(w_free,1).then_inc(w_free,-1)
                        e=bass.ds(j*2+i,1)
                        sp.dma_start(w1[:,i],w1_d[e][0].rearrange("(k p) f -> p k f",p=128)).then_inc(w_loaded[i],16)
                        sp.dma_start(w2[:,i],w2_d[e][0].rearrange("(k p) d -> p k d",p=128)).then_inc(w_loaded[i],16)
                        sp.wait_ge(sorted_,1).then_inc(sorted_,-1)
                        sp.dma_start(xs[:,i],xs_d[bass.ds((j*2+i)*CAP,CAP),:].rearrange("(t p) d -> p t d",p=128)).then_inc(x_loaded[i],16)
            @block.tensor
            def _(pe):
                pe.sem_inc(w_free,2); pe.sem_inc(y_free,2)
                pe.wait_ge(consts,16*5)
                pe.wait_ge(tri_ready,1).then_inc(tri_ready,-1)
                def turn_x(i):
                    pe.wait_ge(x_loaded[i],16).then_inc(x_loaded[i],-16)
                    for k in range(KC):
                        for t in range(T4):
                            mm=pe.transpose(TX[:,k,128*t:128*t+128],xs[:,i,t,128*k:128*k+128],ident[:])
                        mm.then_inc(tx_full,1)
                def first(i,c,k):
                    if c==0 and k==0: pe.wait_ge(w_loaded[i],32).then_inc(w_loaded[i],-32); pe.wait_ge(xT_ready,2).then_inc(xT_ready,-2)
                    if c>=2 and k==0: pe.wait_ge(hT_ready,1).then_inc(hT_ready,-1)
                    mm=pe.matmul(H[:,c%2,:],w1[:,i,k,128*c:128*c+128],xT[:,k,:],start=k==0,stop=k==KC-1)
                    if k==KC-1: mm.then_inc(h_full,1)
                def second(i,e,t,c):
                    if t==0 and c==0: pe.wait_ge(hT_ready,2).then_inc(hT_ready,-2)
                    if c==0: pe.wait_ge(y_free,1).then_inc(y_free,-1)
                    if c<FC: pe.matmul(Y[:,t%2,0:DIM],hT[:,c,128*t:128*t+128],w2[:,i,c,:],start=c==0,stop=False)
                    else: pe.matmul(Y[:,t%2,0:DIM],ones[:],b2[:,bass.ds(e*DIM,DIM)],start=False,stop=True).then_inc(y_full,1)
                PIECES=1+KC*FC+(FC+1)*T4
                def pieces(i,e,n0,n1):
                    for n in range(n0,n1):
                        if n==0: turn_x(i)
                        elif n<=KC*FC: first(i,(n-1)//KC,(n-1)%KC)
                        else: second(i,e,(n-1-KC*FC)//(FC+1),(n-1-KC*FC)%(FC+1))
                until=[2]+[2+3*l for l in range(1,6)]+[1+KC*FC+6,1+KC*FC+12]
                def ranks():
                    pe.wait_ge(flags_ready,1).then_inc(flags_ready,-1)
                    for i in range(2):
                        mm=pe.matmul(RK[:,2*NT*i:2*NT*i+2*NT],tri[:,i,:],flags[:].rearrange("p f t -> p (f t)"),start=True,stop=True)
                    mm.then_inc(rank_full,1)
                def search(beside=None):
                    for l in range(LEVELS):
                        pe.wait_ge(part_ready,1).then_inc(part_ready,-1)
                        pe.matmul(CN[:,0:CANDS],tri[:,1,:],part[:],start=True,stop=True).then_inc(count_full,1)
                        if beside: pieces(*beside,until[l-1] if l else 0,until[l])
                    ranks()
                    if beside: pieces(*beside,until[-1],PIECES)
                with pe.Fori(0,2): search()
                with pe.Fori(0,(EXPERTS-3)//2) as j:
                    for i in range(2): search((i,j*2+i))
                search((0,EXPERTS-4))
                ranks()
                for e in range(EXPERTS-3,EXPERTS): pieces(e%2,e,0,PIECES)
            @block.scalar
            def _(act):
                nc.scalar.preload_act_table(ACT.Gelu_apprx_tanh)
                act.wait_ge(consts,16*5)
                for i in range(2): act.sem_inc(y_stored[i],16)
                with act.Fori(0,EXPERTS) as e:
                    for k in range(KC):
                        act.wait_ge(tx_full,1).then_inc(tx_full,-1)
                        nc.scalar.activation(xT[:,k,:],TX[:,k,:],ACT.Copy).then_inc(xT_ready,1)
                    for c in range(FC):
                        act.wait_ge(h_full,1).then_inc(h_full,-1)
                        nc.scalar.activation(hT[:,c,:],H[:,c%2,:],ACT.Gelu_apprx_tanh,bias=b1[:,bass.ds(e,1),c:c+1].rearrange("p o c -> p (o c)")).then_inc(hT_ready,1)
                    for t in range(T4):
                        act.wait_ge(y_full,1).then_inc(y_full,-1); act.wait_ge(y_stored[t%2],16).then_inc(y_stored[t%2],-16)
                        nc.scalar.activation(y[:,t%2],Y[:,t%2,0:DIM],ACT.Copy).then_inc(y_copied,1)
                        act.wait_ge(y_copied,1).then_inc(y_copied,-1)
                        act.sem_inc(y_free,1)
                        act.dma_start(ys_d[bass.ds(e*CAP+t*128,128),:],y[:,t%2]).then_inc(y_stored[t%2],16)
                    act.sem_inc(w_free,1)
                for i in range(2): act.wait_ge(y_stored[i],16)
            @block.vector
            def _(dve):
                V=nc.vector
                def done(i):
                    i.then_inc(dve_done,1); dve.wait_ge(dve_done,1).then_inc(dve_done,-1)
                def tt(o,x,y,op): done(V.tensor_tensor(o,x,y,op))
                def ts(o,x,s1,s2,o1,o2=ALU.bypass): done(V.tensor_scalar(o,x,s1,s2,o1,o2))
                def red(o,x,op): done(V.tensor_reduce(o,x,AX.X,op))
                dve.wait_ge(consts,16*5)
                done(V.tensor_copy(tri[:],trif[:]))
                done(V.memset(ones[:],1.0))
                dve.sem_inc(tri_ready,1)
                done(V.memset(zero[:],0.0)); done(V.memset(keep[:],1.0)); done(V.memset(base[:],0.0)); done(V.memset(posf[:],0.0))
                def ranks():
                    dve.sem_inc(flags_ready,1)
                    dve.wait_ge(rank_full,1).then_inc(rank_full,-1)
                    done(V.tensor_copy(tot[:].rearrange("p f t -> p (f t)"),RK[:,2*NT:4*NT]))
                    for i in range(2):
                        done(V.tensor_tensor_scan(out=S[:,i],data0=tot[:,i],data1=zero[:],initial=0.0,op0=ALU.add,op1=ALU.add))
                    tt(rank[:],S[:],tot[:],ALU.subtract)
                    tt(rank[:],rank[:],RK[:,0:2*NT].rearrange("p (f t) -> p f t",t=NT),ALU.add)
                def place(chosen):
                    ts(out_[:],w[:],-FAR,None,ALU.add)
                    tt(out_[:],out_[:],chosen,ALU.mult)
                    ts(out_[:],out_[:],FAR,None,ALU.add)
                    dve.wait_ge(target_free,1).then_inc(target_free,-1)
                    V.tensor_copy(target[:],out_[:]).then_inc(target_ready,1)
                    tt(w[:],w[:],chosen,ALU.mult)
                    tt(posf[:],posf[:],w[:],ALU.add)
                dve.sem_inc(target_free,1)
                with dve.Fori(0,EXPERTS-1) as e:
                    sc=scores[:,bass.ds(e,1),:].rearrange("p o t -> p (o t)")
                    ts(out_[:],keep[:],1.0,3.0e38,ALU.subtract,ALU.mult)
                    tt(s[:],sc,keep[:],ALU.mult)
                    tt(s[:],s[:],out_[:],ALU.add)
                    done(V.memset(P[:],-2**31))
                    for l in range(LEVELS):
                        tt(cand[:],jt[:,l,:],P[:].broadcast_to([128,CANDS]),ALU.bitwise_xor)
                        if l==0:
                            ts(msk[:],cand[:],31,0x7fffffff,ALU.arith_shift_right,ALU.bitwise_and)
                            tt(cand[:],cand[:],msk[:],ALU.bitwise_xor)
                        tt(ge[:],s[:].rearrange("p (o t) -> p o t",o=1).broadcast_to([128,CANDS,NT]),cand[:].bitcast(F32).rearrange("p (c o) -> p c o",o=1).broadcast_to([128,CANDS,NT]),ALU.is_ge)
                        with nc.allow_low_precision("counts up to 32 are exact"):
                            red(part[:],ge[:],ALU.add)
                        dve.sem_inc(part_ready,1)
                        dve.wait_ge(count_full,1).then_inc(count_full,-1)
                        bit=32-BITS*(l+1) if l else 0
                        ts(ok[:],CN[:,0:CANDS],float(CAP),float(2**bit),ALU.is_ge,ALU.mult)
                        with nc.allow_low_precision("a count of up to 15 times a power of two is exact"):
                            red(found[:],ok[:],ALU.add)
                        if l==0: ts(found[:],found[:],32-BITS,None,ALU.logical_shift_left)
                        tt(P[:],found[:],P[:],ALU.bitwise_xor)
                        if l==0:
                            ts(msk[:,0:1],P[:],31,0x7fffffff,ALU.arith_shift_right,ALU.bitwise_and)
                            tt(P[:],P[:],msk[:,0:1],ALU.bitwise_xor)
                    ts(gt[:,0],s[:],P[:].bitcast(F32),None,ALU.is_gt)
                    ts(gt[:,1],s[:],P[:].bitcast(F32),None,ALU.is_equal)
                    done(V.tensor_copy(flags[:],gt[:]))
                    ranks()
                    ts(need[:],S[:,0,NT-1:NT],-1.0,float(CAP),ALU.mult,ALU.add)
                    ts(w[:],rank[:,1],need[:],None,ALU.is_lt)
                    tt(w[:],w[:],gt[:,1],ALU.mult)
                    tt(sel[:],w[:],gt[:,0],ALU.add)
                    ts(w[:],rank[:,1],need[:],base[:],ALU.min,ALU.add)
                    tt(w[:],w[:],rank[:,0],ALU.add)
                    place(sel[:])
                    tt(keep[:],keep[:],sel[:],ALU.subtract)
                    ts(base[:],base[:],float(CAP),None,ALU.add)
                done(V.memset(flags[:],0.0))
                done(V.tensor_copy(flags[:,0],keep[:]))
                ranks()
                ts(w[:],rank[:,0],base[:],None,ALU.add)
                place(keep[:])
                done(V.tensor_copy(pos[:],posf[:]))

def finish(nc,tag,x,f,pos,ys_d,out_d):
    with Mem(nc,tag) as m:
        R=8
        y=m.sb("y",[128,R,DIM]); o=m.sb("o",[128,R,DIM]); st=m.sb("st",[128,R,STAT]); ln=m.sb("ln",[128,R,DIM]); fin=m.sb("fin",[128,R,DIM]); half=m.sb("half",[128,2])
        y_loaded=[m.sem(f"y_loaded{i}") for i in range(R)]; y_free=m.sem("y_free"); dve_done=m.sem("dve_done"); half_done=m.sem("half_done"); pool_done=m.sem("pool_done")
        var=m.sem("var"); root=m.sem("root"); ln_ready=m.sem("ln_ready"); fin_ready=m.sem("fin_ready"); stored=[m.sem(f"stored{i}") for i in range(R)]
        ROOT,LN,FIN=3,3,4
        with nc.Block() as block:
            @block.gpsimd
            def _(pool):
                nc.gpsimd.memset(half[:],-0.5).then_inc(half_done,1)
                pool.wait_ge(half_done,1)
                for n in range(NT+ROOT):
                    if n<NT:
                        if n>=R: pool.wait_ge(y_free,1).then_inc(y_free,-1)
                        nc.gpsimd.indirect_dma_start(out=y[:,n%R,:],out_offset=None,in_=ys_d,in_offset=bass.IndirectOffsetOnAxis(ap=pos[:,n:n+1],axis=0)).then_inc(y_loaded[n%R],16)
                    if n>=ROOT:
                        pool.wait_ge(var,1).then_inc(var,-1)
                        roots(nc,pool,half,st[:,(n-ROOT)%R],pool_done,root)
            @block.scalar
            def _(act):
                nc.scalar.preload_act_table(ACT.Exp)
                for n in range(NT):
                    act.wait_ge(root,1).then_inc(root,-1)
                    nc.scalar.activation(ln[:,n%R],o[:,n%R],ACT.Identity,bias=st[:,n%R,12:13],scale=st[:,n%R,10:11]).then_inc(ln_ready,1)
            @block.vector
            def _(dve):
                V=nc.vector
                for n in range(NT+FIN):
                    k=n-FIN
                    count=0
                    if n<NT:
                        dve.wait_ge(y_loaded[n%R],16*(n//R+1))
                        V.tensor_tensor(o[:,n%R],y[:,n%R],f[:,n,:],ALU.add).then_inc(dve_done,1); count+=1
                    if count: dve.wait_ge(dve_done,1).then_inc(dve_done,-1)
                    if n<NT:
                        dve.sem_inc(y_free,1)
                        V.bn_stats(st[:,n%R,0:6],o[:,n%R]).then_inc(dve_done,1)
                    if k>=0:
                        dve.wait_ge(ln_ready,1).then_inc(ln_ready,-1)
                        if k>=R: dve.wait_ge(stored[k%R],16).then_inc(stored[k%R],-16)
                        V.tensor_tensor(fin[:,k%R],ln[:,k%R],x[:,k,:],ALU.add).then_inc(fin_ready,1)
                    if n<NT:
                        dve.wait_ge(dve_done,1).then_inc(dve_done,-1)
                        V.bn_aggr(st[:,n%R,6:8],st[:,n%R,0:6]).then_inc(dve_done,1)
                        dve.wait_ge(dve_done,1).then_inc(dve_done,-1)
                        for c in (8,9): V.tensor_scalar(st[:,n%R,c:c+1],st[:,n%R,7:8],LN_EPS,None,ALU.add).then_inc(dve_done,1)
                        dve.wait_ge(dve_done,2).then_inc(dve_done,-2)
                        dve.sem_inc(var,1)
                for i in range(R): dve.wait_ge(stored[i],16)
            @block.sync
            def _(sp):
                for n in range(NT):
                    sp.wait_ge(fin_ready,1).then_inc(fin_ready,-1)
                    sp.dma_start(out_d[n*128:n*128+128,:],fin[:,n%R]).then_inc(stored[n%R],16)

def two_layers(nc,out,x,w_qkv0,w_out0,norm_w,w_route,w1_0,w2_0,w_qkv1,b_qkv1,w_out1,b_out1,ln_g,ln_b,centroids,
               w1_1,w2_1,b1_1,b2_1,ident,prefix,order,starts,cands,positions,masks,zeros):
    def scratch(name,*shape): return nc.dram_tensor(name,shape,F32,kind="Internal").ap()
    qkv=scratch("qkv",BATCH*GROUPS,3,SEQ,4*HD); ao=scratch("ao",BATCH*GROUPS,SEQ,4*HD)
    x1=scratch("x1",TOK,DIM); x2=scratch("x2",TOK,DIM)
    sorted_in=scratch("sorted_in",SLOTS0*128,DIM); sorted_out=scratch("sorted_out",SLOTS0*128,DIM)
    ln_qkv(nc,"qkv0",x,w_qkv0,qkv,ident)
    attention(nc,"att0",qkv,ao,False,1.0/DIM**0.5,ident)
    with Mem(nc,"l0") as m:
        z=m.sb("z",[128,NT,DIM])
        attn_post(nc,"post0",ao,w_out0,x,ident,x_out=x1,z=z)
        slot=m.sb("slot",[128,2,NT],U32); weight=m.sb("weight",[128,2,NT])
        with Mem(nc,"ffn0") as f:
            w1,w1h=(f.sb(n,[128,KC,EXPERTS*F0],F32R) for n in ("w1","w1h")); w2,w2h=(f.sb(n,[128,F0//128,EXPERTS*DIM],F32R) for n in ("w2","w2h"))
            rstd=f.sb("rstd",[128,NT]); logits=f.sb("logits",[128,LG,NT]); tile_expert=f.sb("tile_expert",[128,SLOTS0],I32)
            for loop in range(2):
                first=loop==0
                rms_logits(nc,f"rms{loop}",z,rstd,logits,norm_w,w_route,ident,combined=None if first else (slot,weight,sorted_out),
                           prepare=(w1,w1_0,w2,w2_0,zeros,sorted_in) if first else None)
                route(nc,f"route{loop}",logits,prefix,order,starts,slot,weight,tile_expert)
                experts(nc,f"experts{loop}",z,rstd,norm_w,slot,tile_expert,w1,w2,w1h,w2h,first,sorted_in,sorted_out,ident)
        combine_qkv(nc,"qkv1",z,slot,weight,sorted_out,x1,w_qkv1,b_qkv1,x2,qkv,ident)
    attention(nc,"att1",qkv,ao,True,1.0/HD**0.5,ident,positions,masks)
    with Mem(nc,"l1") as m:
        x3=m.sb("x3",[128,NT,DIM]); f=m.sb("f",[128,NT,DIM]); norm=m.sb("norm",[128,NT,DIM])
        scores=m.sb("scores",[128,EXPERTS,NT]); pos=m.sb("pos",[128,NT],U32)
        attn_post(nc,"post1",ao,w_out1,x2,ident,z=x3,bias_d=b_out1,g_d=ln_g,b_d=ln_b,cent_d=centroids,f=f,norm=norm,scores=scores)
        assigned_experts(nc,"ffn1",scores,norm,pos,prefix,cands,w1_1,w2_1,b1_1,b2_1,sorted_in,sorted_out,ident)
        finish(nc,"finish",x3,f,pos,sorted_out,out)

def twelve_bits(x):
    bits=np.asarray(x,np.float32).view(np.uint32).astype(np.uint64)
    return ((bits+0x800)&0xFFFFF000).astype(np.uint32).view(np.float32)

def position_columns():
    start=2.0**(-8.0/HEADS)
    slopes=4*np.array([start*start**i for i in range(HEADS)],dtype=np.float32)
    high=twelve_bits(slopes); low=slopes-high
    table=np.zeros((128,2,2*GROUPS,TILES,2,AUG),np.float32)
    place=(np.arange(TILES)[None,:]*128+np.arange(128)[:,None]).astype(np.float32)
    for pair in range(2*GROUPS):
        for h in range(2):
            head=pair*2+h
            for col,value in ((1,high[head]),(2,-place),(3,low[head]),(4,-place)):
                table[:,0,pair,:,h,col]=value
            for col,value in ((0,-1.0),(1,place),(2,high[head]),(3,place),(4,low[head])):
                table[:,1,pair,:,h,col]=value
    return table.reshape(128,2,2*GROUPS,TILES*2*AUG)

def causal_masks():
    row=np.arange(128)[:,None]; col=np.arange(128)[None,:]
    t=np.zeros((128,4,128),np.float32)
    t[:,0]=row==col; t[:,1]=np.where(col>row,-1e30,0); t[:,2]=-1e30; t[:,3]=np.where(col<row,-1e30,0)
    return t.reshape(128,512)

def prefix_and_ones():
    p=np.arange(128)
    t=np.ones((128,2,128),np.float32); t[:,0]=p[:,None]<p[None,:]
    return t

def group_order():
    return np.broadcast_to((2*GR-np.arange(GR,dtype=np.float32))[None,:,None],(128,GR,NT))

def slot_starts():
    return np.broadcast_to((np.arange(SLOTS0)*128).astype(np.float32),(128,EXPERTS,SLOTS0))

def candidate_bits():
    t=np.array([[j<<(32-BITS*(l+1)) for j in range(1,CANDS+1)] for l in range(LEVELS)],np.int64)
    return np.broadcast_to(t.astype(np.uint32).view(np.int32),(128,LEVELS,CANDS))

def by_group(w):
    return w.reshape(-1,3,GROUPS,4*HD).transpose(0,2,1,3).reshape(w.shape[0],3*DIM)


def kernel(**inputs):
    import concourse.bacc as _bacc
    from concourse.bass_utils import run_bass_kernel_spmd as _run
    a={n:np.asarray(v) for n,v in inputs.items()}
    att=lambda n: a["L1_attn_"+n]
    ffn=lambda n: a["L1_ffn_"+n]
    laid=dict(
        x=a["L0_attn_x"].reshape(TOK,DIM), w_qkv0=by_group(a["L0_attn_w_qkv"]), w_out0=a["L0_attn_w_out"],
        norm_w=a["L0_ffn_norm_w"], w_route=np.concatenate([a["L0_ffn_w_macro"],a["L0_ffn_w_micro"].reshape(EXPERTS,DIM)]).T,
        w1_0=a["L0_ffn_w1"].transpose(2,0,1).reshape(DIM,EXPERTS*F0), w2_0=a["L0_ffn_w2"].transpose(2,0,1).reshape(F0,EXPERTS*DIM),
        w_qkv1=by_group(np.concatenate([att("q_w").T,att("k_w").T,att("v_w").T],axis=1)),
        b_qkv1=by_group(np.concatenate([att("q_b"),att("k_b"),att("v_b")])[None])[0],
        w_out1=att("o_w").T, b_out1=att("o_b"), ln_g=ffn("ln_g"), ln_b=ffn("ln_b"), centroids=ffn("centroids").T,
        w1_1=ffn("w1"), w2_1=ffn("w2"), b1_1=ffn("b1").reshape(EXPERTS,F1//128,128).transpose(2,0,1), b2_1=ffn("b2").reshape(EXPERTS*DIM),
        ident=np.eye(128,dtype=np.float32), prefix=prefix_and_ones(), order=group_order(), starts=slot_starts(),
        cands=candidate_bits(), positions=position_columns(), masks=causal_masks(), zeros=np.zeros((128,2048),np.float32))
    nc=_bacc.Bacc("TRN2",target_bir_lowering=False,num_devices=1)
    arrays,aps={},{}
    for name,value in laid.items():
        value=np.ascontiguousarray(value)
        arrays["in_"+name]=value
        aps[name]=nc.dram_tensor("in_"+name,value.shape,mybir.dt.from_np(value.dtype),kind="ExternalInput").ap()
    out=nc.dram_tensor("out",(TOK,DIM),F32,kind="ExternalOutput").ap()
    two_layers(nc,out,**aps)
    result=_run(nc,[arrays],core_ids=[0])
    return result.results[0]["out"].reshape(BATCH,SEQ,DIM)
```
